# Optimizing a Trainium2 kernel written in Bass

```python
import numpy as np
import jax
import jax.numpy as jnp

def _softmax(x, axis=-1):
    return jax.nn.softmax(x, axis=axis)

def _gelu(x):
    return jax.nn.gelu(x, approximate=True)

def _silu(x):
    return jax.nn.silu(x)

def _sigmoid(x):
    return jax.nn.sigmoid(x)

def _layernorm(x, axis=-1, eps=1e-05):
    m = jnp.mean(x, axis=axis, keepdims=True)
    v = jnp.var(x, axis=axis, keepdims=True)
    return (x - m) / jnp.sqrt(v + eps)

def _scatter_add(tgt, idx, src, axis=0):
    return tgt.at[idx].add(src)

def _segment_sum(src, seg, n):
    return jax.ops.segment_sum(src, seg, n)
kernel_name = 'mk_sandwich_d1_jaxref_r4_3f0395'

def setup_inputs(seed: int=0):
    np.random.seed(seed)
    _w = jnp.asarray

    def _L0_attn_setup():
        import jax, jax.numpy as jnp
        import numpy as np
        D_MODEL = 256
        N_HEADS = 16
        D_HEAD = D_MODEL // N_HEADS
        SCALE = 1.0 / np.sqrt(D_HEAD).astype(np.float32)

        def _feature_map(x):
            return jax.nn.elu(x) + 1.0
        key = jax.random.key(seed)
        ks = jax.random.split(key, 7)
        b, s = (4, 512)
        w = 1.0 / np.sqrt(D_MODEL).astype(np.float32)
        return {'x': jax.random.normal(ks[0], (b, s, D_MODEL), dtype=jnp.float32), 'Wq': jax.random.normal(ks[1], (D_MODEL, D_MODEL), dtype=jnp.float32) * w, 'Wk': jax.random.normal(ks[2], (D_MODEL, D_MODEL), dtype=jnp.float32) * w, 'Wv': jax.random.normal(ks[3], (D_MODEL, D_MODEL), dtype=jnp.float32) * w, 'Wo': jax.random.normal(ks[4], (D_MODEL, D_MODEL), dtype=jnp.float32) * w, 'Wg': jax.random.normal(ks[5], (N_HEADS, D_MODEL), dtype=jnp.float32) * w, 'bg': jax.random.normal(ks[6], (N_HEADS,), dtype=jnp.float32) * 0.02}
    _L0_attn_in = _L0_attn_setup()

    def _L0_ffn_setup():
        import jax, jax.numpy as jnp
        import numpy as np
        EXPERTS = 8
        TOP_K = 2

        def swiglu(x, w1, w2, w3):
            h = x @ w1
            return h * jax.nn.sigmoid(h) * (x @ w2) @ w3
        key = jax.random.key(seed)
        ks = jax.random.split(key, 9)
        B, S, D = (4, 512, 256)
        H = 2 * D
        s = 0.02
        x = jax.random.normal(ks[0], (B, S, D), dtype=jnp.float32)
        gate_w = jax.random.normal(ks[1], (D, EXPERTS), dtype=jnp.float32) * s
        ew1 = jax.random.normal(ks[2], (EXPERTS, D, H), dtype=jnp.float32) * s
        ew2 = jax.random.normal(ks[3], (EXPERTS, D, H), dtype=jnp.float32) * s
        ew3 = jax.random.normal(ks[4], (EXPERTS, H, D), dtype=jnp.float32) * s
        sw1 = jax.random.normal(ks[5], (D, H), dtype=jnp.float32) * s
        sw2 = jax.random.normal(ks[6], (D, H), dtype=jnp.float32) * s
        sw3 = jax.random.normal(ks[7], (H, D), dtype=jnp.float32) * s
        return {'x': x, 'gate_w': gate_w, 'ew1': ew1, 'ew2': ew2, 'ew3': ew3, 'sw1': sw1, 'sw2': sw2, 'sw3': sw3}
    _L0_ffn_in = _L0_ffn_setup()
    _d = {'L0_attn_x': _L0_attn_in['x'], 'L0_attn_Wq': _L0_attn_in['Wq'], 'L0_attn_Wk': _L0_attn_in['Wk'], 'L0_attn_Wv': _L0_attn_in['Wv'], 'L0_attn_Wo': _L0_attn_in['Wo'], 'L0_attn_Wg': _L0_attn_in['Wg'], 'L0_attn_bg': _L0_attn_in['bg'], 'L0_ffn_gate_w': _L0_ffn_in['gate_w'], 'L0_ffn_ew1': _L0_ffn_in['ew1'], 'L0_ffn_ew2': _L0_ffn_in['ew2'], 'L0_ffn_ew3': _L0_ffn_in['ew3'], 'L0_ffn_sw1': _L0_ffn_in['sw1'], 'L0_ffn_sw2': _L0_ffn_in['sw2'], 'L0_ffn_sw3': _L0_ffn_in['sw3']}
    _x0 = _d['L0_attn_x']
    _d['L0_attn_x'] = jax.random.normal(jax.random.fold_in(jax.random.key(seed), 1), (2, 2048, 256), dtype=_x0.dtype)
    del _x0
    return _d

def reference(L0_attn_x, L0_attn_Wq, L0_attn_Wk, L0_attn_Wv, L0_attn_Wo, L0_attn_Wg, L0_attn_bg, L0_ffn_gate_w, L0_ffn_ew1, L0_ffn_ew2, L0_ffn_ew3, L0_ffn_sw1, L0_ffn_sw2, L0_ffn_sw3):

    def _L0_attn_ref(x, Wq, Wk, Wv, Wo, Wg, bg):
        import jax, jax.numpy as jnp
        import numpy as np
        D_MODEL = 256
        N_HEADS = 16
        D_HEAD = D_MODEL // N_HEADS
        SCALE = 1.0 / np.sqrt(D_HEAD).astype(np.float32)

        def _feature_map(x):
            return jax.nn.elu(x) + 1.0
        b, s, _ = x.shape
        q = (x @ Wq.T).reshape(b, s, N_HEADS, D_HEAD)
        k = (x @ Wk.T).reshape(b, s, N_HEADS, D_HEAD)
        v = (x @ Wv.T).reshape(b, s, N_HEADS, D_HEAD)
        q = _feature_map(q * SCALE)
        k = _feature_map(k)
        gate = jax.nn.sigmoid(x @ Wg.T + bg)
        qt = jnp.moveaxis(q, 1, 0)
        kt = jnp.moveaxis(k, 1, 0)
        vt = jnp.moveaxis(v, 1, 0)
        gt = jnp.moveaxis(gate, 1, 0)
        S0 = jnp.zeros((b, N_HEADS, D_HEAD, D_HEAD), dtype=x.dtype)

        def step(S, inp):
            q_t, k_t, v_t, g_t = inp
            S = g_t[:, :, None, None] * S + k_t[..., :, None] * v_t[..., None, :]
            y_t = jnp.einsum('bhi,bhij->bhj', q_t, S)
            return (S, y_t)
        _, ys = jax.lax.scan(step, S0, (qt, kt, vt, gt))
        y = jnp.moveaxis(ys, 0, 1).reshape(b, s, D_MODEL)
        return y @ Wo.T

    def _L0_ffn_ref(x, gate_w, ew1, ew2, ew3, sw1, sw2, sw3):
        import jax, jax.numpy as jnp
        import numpy as np
        EXPERTS = 8
        TOP_K = 2

        def swiglu(x, w1, w2, w3):
            h = x @ w1
            return h * jax.nn.sigmoid(h) * (x @ w2) @ w3
        B, S, D = x.shape
        gate_out = x @ gate_w
        top_v, top_i = jax.lax.top_k(gate_out, TOP_K)
        masked = jnp.full_like(gate_out, -1e+20)
        bi = jnp.arange(B)[:, None, None]
        si = jnp.arange(S)[None, :, None]
        masked = masked.at[bi, si, top_i].set(top_v)
        probs = jax.nn.softmax(masked, axis=-1)
        chosen = jnp.zeros_like(gate_out, dtype=bool).at[bi, si, top_i].set(True)
        w = jnp.where(chosen, probs, 0.0)

        def one_expert(w1, w2, w3, we):
            return swiglu(x, w1, w2, w3) * we[..., None]
        out = jax.vmap(one_expert, in_axes=(0, 0, 0, 2))(ew1, ew2, ew3, w).sum(0)
        out = out + swiglu(x, sw1, sw2, sw3)
        return out
    x = L0_attn_x
    x = x + _layernorm(_L0_attn_ref(_layernorm(x, axis=-1), L0_attn_Wq, L0_attn_Wk, L0_attn_Wv, L0_attn_Wo, L0_attn_Wg, L0_attn_bg), axis=-1)
    x = x + _layernorm(_L0_ffn_ref(_layernorm(x, axis=-1), L0_ffn_gate_w, L0_ffn_ew1, L0_ffn_ew2, L0_ffn_ew3, L0_ffn_sw1, L0_ffn_sw2, L0_ffn_sw3), axis=-1)
    return x

_drawn_inputs = setup_inputs


def setup_inputs(seed=0):
    import zlib

    import numpy as np

    out = dict(_drawn_inputs(seed))
    spreads = {}
    factors = {'L0_attn_bg': 2.829}
    for name, (base, spread) in spreads.items():
        noise = np.random.default_rng([zlib.crc32(name.encode()), seed]).standard_normal(out[name].shape)
        drawn = base * np.exp(spread * noise) if base else spread * noise
        out[name] = jnp.asarray(drawn.astype(out[name].dtype))
    for name, factor in factors.items():
        out[name] = (out[name] * factor).astype(out[name].dtype)
    return out
```

```python
from contextlib import ExitStack

import concourse.bass as bass
from concourse import mybir

ALU = mybir.AluOpType
ACT = mybir.ActivationFunctionType
F32 = mybir.dt.float32
F16 = mybir.dt.float16
BF16 = mybir.dt.bfloat16
U32 = mybir.dt.uint32
I32 = mybir.dt.int32
AX_X = mybir.AxisListType.X
RMAX = bass.bass_isa.ReduceOp.max
EPS = 1e-5


class Step:

    def __init__(self, half, side):
        self.half, self.side = half, side

    @staticmethod
    def of(i):
        return Step(i // 2, i % 2)

    def __add__(self, d):
        q = self.side + d
        return Step(self.half + q // 2, q % 2)

    @property
    def index(self):
        return self.half * 2 + self.side

    @property
    def fixed(self):
        return isinstance(self.half, int)


def due(eng, sem, per, step, k):
    n = step.index * per + k
    if step.fixed and n <= 0:
        return
    eng.wait_ge(sem, n)


def due_dma(eng, sems, step, n=1):
    if step.fixed and step.half < 0:
        return
    eng.wait_ge(sems[step.side], (step.half + 1) * (16 * n))


def sandwich_kernel(nc, x, Wq, Wk, Wv, Wo, Wg, bg, gate_w, ew1, ew2, ew3, sw1, sw2, sw3, out):
    P = 128
    B, SEQ, D = x.shape
    HEADS = Wg.shape[0]
    DH = D // HEADS
    SCALE = float(DH) ** -0.5
    KC = D // P
    GH = P // DH
    GR = HEADS // GH
    SETH = 4
    NS = B * HEADS // SETH
    C = SEQ // P
    TOK = B * SEQ
    E = gate_w.shape[1]
    TOPK = 2
    H = ew1.shape[2]
    HC = H // P
    NE = E + 1
    HEAD = 6
    MW = KC * H
    CAP = TOK + P
    SHARED = E * CAP
    ROWS = SHARED + TOK
    ST = TOK // P
    RT = TOPK * TOK // P + E
    VW = 3 * DH
    NT = ST + RT
    assert (B, GR, KC, TOPK) == (2, 2, 2, 2) and C % 2 == 0 and HC * D == MW and RT % 2 == 0

    ctx = ExitStack()
    with ctx:
        def sem(name):
            return ctx.enter_context(nc.semaphore(name))

        def sb(name, shape, dt=F32):
            return ctx.enter_context(nc.sbuf_tensor(name, shape, dt))

        xs_d = nc.dram_tensor("xs_scratch", [ROWS, D], F32).ap()
        ys_d = nc.dram_tensor("ys_scratch", [NT * P, D], F32).ap()
        x1_d = nc.dram_tensor("x1_scratch", [TOK, D], F32).ap()

        bank = [ctx.enter_context(nc.psum_tensor(f"bank{n}", [P, 512], F32)) for n in range(8)]

        W = sb("W", [P, NE, 3, MW])
        W16 = W[:].rearrange("p e m n -> p (e m n)").bitcast(F16).rearrange(
            "p (e m s n) -> p e m s n", e=NE, m=3, s=2)
        ident = sb("ident", [P, P])
        half_neg = sb("half_neg", [P, 2])
        wts_all = sb("wts_all", [P, C, B, TOPK])
        pos_all = sb("pos_all", [P, C, B * TOPK], U32)
        wmax = sb("wmax", [P, 2, NE])
        w_scale = sb("w_scale", [P, 3, NE])
        tab = sb("tab", [1, 2, NT], I32)
        choice_all = sb("choice_all", [P, C, B * TOPK])
        place_all = sb("place_all", [P, C, B * TOPK])
        iota8 = sb("iota8", [P, E])
        capoff = sb("capoff", [P, E])
        rowid = sb("rowid", [P, 1])
        total = sb("total", [P, E])
        pad_row = sb("pad_row", [P, E], U32)
        zrow = sb("zrow", [P, D])
        tile_f = sb("tile_f", [1, RT])
        te = sb("te", [P, 5, E])
        te_i = sb("te_i", [P, E], I32)

        s_w = [sem(f"s_w_loaded{n}") for n in range(2)]
        s_init = sem("s_init")
        s_vinit = sem("s_vinit")
        dve_chain = sem("dve_chain")

        phase_a = ExitStack()

        def sa(name, shape, dt=F32):
            return phase_a.enter_context(nc.sbuf_tensor(name, shape, dt))

        late = W[:, HEAD:NE].rearrange("p e m n -> p (e m n)")
        taken = [0]

        def in_late(*shape):
            n = 1
            for d in shape:
                n *= d
            taken[0] += n
            assert taken[0] <= (NE - HEAD) * 3 * MW
            ap = late[:, taken[0] - n:taken[0]]
            if len(shape) == 3:
                return ap.rearrange("p (a b c) -> p a b c", a=shape[0], b=shape[1])
            return ap.rearrange("p (a b c d) -> p a b c d", a=shape[0], b=shape[1], c=shape[2])

        qbd = in_late(B, GR, GH, P)
        wraw = qbd.rearrange("p b g h t -> p (b g h t)")[:, 0:5 * GR * D].rearrange(
            "p (n g d) -> p n g d", n=5, g=GR)
        wT = sa("wT", [P, 5, KC, D])
        gw = sa("gw", [P, KC, E])
        nbg = sa("nbg", [P, GR])
        sel = sa("sel", [P, GH, P], BF16)
        diag4 = sa("diag4", [P, SETH, P])
        later = sa("later", [P, P])
        ones = sa("ones", [P, P])
        hmask = sa("hmask", [P, GH])
        tmp8 = sa("tmp8", [P, 2, GH])
        part_mask = sa("part_mask", [P, 2])
        zeros = sa("zeros", [P, P])

        x_in = [sa(f"x_in{n}", [P, B, D]) for n in range(2)]
        x_res = [sa(f"x_res{n}", [P, B, D]) for n in range(2)]
        st1 = sa("st1", [P, B, 6])
        mv1 = [sa(f"mv1_{n}", [P, B, 2]) for n in range(2)]
        ve = sa("ve", [P, 3, B])
        rs1 = [sa(f"rs1_{n}", [P, B]) for n in range(2)]
        xn = sa("xn", [P, B, D])
        xnT = [sa(f"xnT{n}", [P, KC, B * P]) for n in range(2)]
        rneg = sa("rneg", [P, GR * B * P])
        ef = [sa(f"ef{n}", [P, GR * B * P]) for n in range(2)]
        qT = [sa(f"qT{n}", [P, GR, B, P]) for n in range(2)]
        kT = [sa(f"kT{n}", [P, GR, B, P]) for n in range(2)]
        eg = sa("eg", [P, GR, B, P])
        gT = sa("gT", [P, GR, B, P])
        ghi = sa("ghi", [P, GR, B, P], BF16)
        gt1 = sa("gt1", [P, GR, B, P])
        gr1 = sa("gr1", [P, GR, B, P])
        gparts = [sa(f"gparts{n}", [P, GR, B, P], BF16) for n in range(2)]
        gam = [in_late(GR, B, P) for n in range(2)]
        qg = [in_late(GR, B, P) for n in range(2)]
        vp = [in_late(B, HEADS, VW) for n in range(2)]
        tb = sa("tb", [1, 8, RT])
        tg = sa("tg", [1, 2, RT, E])
        found = sa("found", [P, C * B * TOPK, E])
        decay = [sa(f"decay{n}", [P, SETH, P]) for n in range(2)]
        probs = [sa(f"probs{n}", [P, SETH, P]) for n in range(2)]
        kd = sa("kd", [P, B, GR, P])
        um = sa("um", [P, B, GR, P])
        state = sa("state", [P, B, GR, P])
        yT = [sa(f"yT{n}", [P, B, GR, P]) for n in range(2)]
        sto = sa("sto", [P, B, 6])
        mvo = sa("mvo", [P, B, 2])
        rso = sa("rso", [P, B])
        ln_o = sa("ln_o", [P, B, D])
        x1 = [sa(f"x1_{n}", [P, B, D]) for n in range(2)]
        st2 = sa("st2", [P, B, 6])
        mv2 = sa("mv2", [P, B, 2])
        rs2 = sa("rs2", [P, B])
        xn2 = [sa(f"xn2_{n}", [P, B, D]) for n in range(2)]
        xn2T = sa("xn2T", [P, KC, B * P])
        lg = sa("lg", [P, B, E])
        mx = sa("mx", [P, B, 8])
        mi = sa("mi", [P, B, 8], U32)
        mif = sa("mif", [P, B, 8])
        dv = sa("dv", [P, B])
        ew = sa("ew", [P, B])
        wtmp = sa("wtmp", [P, 2, B])
        oh = sa("oh", [P, B, TOPK, E])
        chosen = sa("chosen", [P, B, E])
        csum = sa("csum", [P, E])
        slot = sa("slot", [P, B, E])
        posf = sa("posf", [P, B * TOPK])
        posi = [sa(f"posi{n}", [P, B * TOPK], U32) for n in range(2)]

        pA, pG, pY, pU, X0, X1 = bank[0:2], bank[2:4], bank[4], bank[5], bank[6], bank[7]

        names = ("wraw_loaded wT_done wT_ready xn_stats rstd1_ready xn_ready xT_done xnT_ready q_done rq_ready"
                 " eq_ready qT_ready k_done rk_ready ek_ready kT_ready g_done eg_ready g1_ready gT_ready ghi_ready"
                 " gpool gparts_ready gam_ready qg_ready qbd_ready v_done v_ready ktok_done gbc_done decay_ready"
                 " A_done probs_ready kd_ready PV_done U_done um_ready state_ready yT_ready o_done o_stats"
                 " rstdo_ready ln_ready x1_ready x1_stats rstd2_ready xn2_ready xn2T_done xn2T_ready gate_done"
                 " top_ready ew_ready chosen_ready prefix_done pos_ready wts_ready csum_ready pool_chain").split()
        S = {n: sem(n) for n in names}
        CONSTANTS = 26
        x_loaded = [sem(f"x_loaded{n}") for n in range(2)]
        xr_loaded = [sem(f"xr_loaded{n}") for n in range(2)]
        x1_stored = [sem(f"x1_stored{n}") for n in range(2)]
        xs_stored = [sem(f"xs_stored{n}") for n in range(2)]
        scattered = [sem(f"scattered{n}") for n in range(2)]
        s_total = sem("s_total")
        s_totals = sem("s_totals")
        s_pad = sem("s_pad_rows")
        s_padded = sem("s_padded")
        s_wmax = sem("s_wmax")
        s_wall = sem("s_wmax_all")
        s_scale = sem("s_scale")
        s_tab = sem("s_table")

        x_by_step = x.rearrange("b (c p) d -> c p b d", p=P)
        x1_by_step = x1_d.rearrange("(b c p) d -> c p b d", b=B, p=P)
        xs_by_step = xs_d[SHARED:SHARED + TOK, :].rearrange("(b c p) d -> c p b d", b=B, p=P)

        def settle(eng):
            eng.nop(nofuse=True)

        def free2(ap):
            return ap.rearrange("p a b -> p (a b)")

        def free3(ap):
            return ap.rearrange("p a b c -> p (a b c)")

        FIRST, LAST = -1, C
        LOOP = (3, C - 1)

        def run_bodies(eng, body):
            for i in range(FIRST, LOOP[0]):
                body(Step.of(i))
            with eng.Fori(LOOP[0] // 2, LOOP[1] // 2) as j:
                body(Step(j, 1))
                body(Step(j + 1, 0))
            for i in range(LOOP[1], LAST + 1):
                body(Step.of(i))

        def has(step):
            return not step.fixed or 0 <= step.index < C

        def sync_a(sp):
            for n, w in enumerate((Wq, Wk, Wv, Wo)):
                sp.dma_start(wraw[:, n], w.rearrange("(g p) d -> p g d", p=P)).then_inc(S["wraw_loaded"], 16)
            for g in range(GR):
                for h in range(GH):
                    r = g * GH + h
                    sp.dma_start(wraw[h * DH:(h + 1) * DH, 4, g, :], Wg[r:r + 1, :].broadcast_to([DH, D]))\
                      .then_inc(S["wraw_loaded"], 16)
                    sp.dma_start(nbg[h * DH:(h + 1) * DH, g:g + 1],
                                 bg[r:r + 1].unsqueeze(1).broadcast_to([DH, 1])).then_inc(S["wraw_loaded"], 16)
            sp.dma_start(gw[:, :, :], gate_w.rearrange("(k p) e -> p k e", p=P)).then_inc(S["wraw_loaded"], 16)

            def body(i):
                a1, a3 = i + 1, i + -1
                if has(a1):
                    due(sp, S["xn_ready"], B, a1 + -2, B)
                    sp.dma_start(x_in[a1.side][:, :, :], x_by_step[a1.index]).then_inc(x_loaded[a1.side], 16)
                if has(a3):
                    due(sp, S["x1_ready"], 1, a3 + -2, 1)
                    sp.dma_start(x_res[a3.side][:, :, :], x_by_step[a3.index]).then_inc(xr_loaded[a3.side], 16)
                    due(sp, S["x1_ready"], 1, a3, 1)
                    sp.dma_start(x1_by_step[a3.index], x1[a3.side][:, :, :]).then_inc(x1_stored[a3.side], 16)
                    due(sp, S["xn2_ready"], B, a3, B)
                    sp.dma_start(xs_by_step[a3.index], xn2[a3.side][:, :, :]).then_inc(xs_stored[a3.side], 16)
            run_bodies(sp, body)

        def load_experts(act, first, end):
            for e in range(first, end):
                src = (ew1[e - 1], ew2[e - 1], ew3[e - 1]) if e else (sw1, sw2, sw3)
                for m in range(3):
                    act.dma_start(W[:, e, m, :].rearrange("p (c n) -> p c n", c=KC if m < 2 else HC),
                                  src[m].rearrange("(c p) n -> p c n", p=P)).then_inc(s_w[int(e >= HEAD)], 16)

        def scalar_a(act):
            load_experts(act, 0, HEAD)
            act.wait_ge(S["wT_done"], 5)
            for n in range(5):
                act.activation(free2(wT[:, n]), bank[n][:, :], ACT.Copy, scale=SCALE if n == 0 else 1.0)\
                   .then_inc(S["wT_ready"], 1)

            def feature(i, src, done, r_ready, e_ready, used, dst):
                due(act, S[done], 1, i, 1)
                due(act, S["ek_ready" if done == "q_done" else "eq_ready"], 1,
                    i + -1 if done == "q_done" else i, 1)
                act.activation(rneg[:, :], src[:, :], ACT.Relu, scale=-1.0).then_inc(S[r_ready], 1)
                due(act, S[r_ready], 1, i, 1)
                due(act, S[used], 1, i + -1, 1)
                act.activation(dst[:, :], rneg[:, :], ACT.Exp, scale=-1.0).then_inc(S[e_ready], 1)

            def body(i):
                a1, a2, a3 = i + 1, i, i + -1
                if has(a1):
                    due(act, S["xT_done"], 1, a1, 1)
                    due(act, S["v_done"], 1, a1 + -2, 1)
                    act.activation(free2(xnT[a1.side][:, :, :]), X1[:, :], ACT.Copy).then_inc(S["xnT_ready"], 1)
                    feature(a1, X0, "q_done", "rq_ready", "eq_ready", "qT_ready", ef[0])
                    feature(a1, X1, "k_done", "rk_ready", "ek_ready", "kT_ready", ef[1])
                    due(act, S["g_done"], 1, a1, 1)
                    due(act, S["gT_ready"], 1, a1 + -1, 1)
                    for g in range(GR):
                        act.activation(eg[:, g].rearrange("p b t -> p (b t)"), X0[:, g * B * P:(g + 1) * B * P],
                                       ACT.Exp, bias=nbg[:, g:g + 1], scale=-1.0).then_inc(S["eg_ready"], 1)
                if has(a3):
                    due(act, S["xn2T_done"], 1, a3, 1)
                    due(act, S["gate_done"], 1, a3 + -1, 1)
                    act.activation(free2(xn2T[:, :, :]), X1[:, :], ACT.Copy).then_inc(S["xn2T_ready"], 1)
                if has(a1):
                    due(act, S["v_done"], 1, a1, 1)
                    due(act, S["U_done"], 1, a1 + -2, 1)
                    for b in range(B):
                        act.activation(vp[a1.side][:, b, :, DH:2 * DH],
                                       X0[:, b * D:(b + 1) * D].rearrange("p (h j) -> p h j", j=DH), ACT.Copy)\
                           .then_inc(S["v_ready"], 1)
                    due(act, S["gT_ready"], 1, a1, 1)
                    due(act, S["gpool"], 4, a1 + -1, 1)
                    act.activation(free3(ghi[:, :, :, :]), free3(gT[:, :, :, :]), ACT.Copy)\
                       .then_inc(S["ghi_ready"], 1)
                if has(a3):
                    due(act, S["top_ready"], 1, a3, 1)
                    due(act, S["wts_ready"], 1, a3 + -1, 1)
                    act.activation(ew[:, :], dv[:, :], ACT.Exp).then_inc(S["ew_ready"], 1)
                if has(a2):
                    due(act, S["PV_done"], NS, a2, NS)
                    due(act, S["o_done"], 1, a2 + -2, 1)
                    act.activation(free3(yT[a2.side][:, :, :, :]), pY[:, :], ACT.Copy).then_inc(S["yT_ready"], 1)
            run_bodies(act, body)
            act.wait_ge(S["U_done"], C)
            act.wait_ge(S["state_ready"], C * GR * B)
            load_experts(act, HEAD, NE)

        def pool_a(pool):
            made = [0]

            def link(ins):
                made[0] += 1
                ins.then_inc(s_init, 1)
                pool.wait_ge(s_init, made[0])

            link(pool.memset(ident[:, :], 0.0))
            link(pool.affine_select(out=ident[:, :], in_=ident[:, :], compare_op=ALU.not_equal, fill=1.0,
                                    base=0, pattern=[[-1, P]], channel_multiplier=1))
            link(pool.memset(ones[:, :], 1.0))
            link(pool.memset(half_neg[:, :], -0.5))
            link(pool.memset(diag4[:, :, :], 0.0))
            link(pool.affine_select(out=diag4[:, :, :], in_=diag4[:, :, :], compare_op=ALU.not_equal, fill=1.0,
                                    base=0, pattern=[[0, SETH], [-1, P]], channel_multiplier=1))
            link(pool.affine_select(out=later[:, :], in_=ones[:, :], compare_op=ALU.is_gt, fill=0.0,
                                    base=0, pattern=[[1, P]], channel_multiplier=-1))
            link(pool.memset(sel[:, :, :], 1.0))
            link(pool.affine_select(out=sel[:, :, :], in_=sel[:, :, :], compare_op=ALU.is_ge, fill=0.0,
                                    base=0, pattern=[[-DH, GH], [0, P]], channel_multiplier=1))
            link(pool.affine_select(out=sel[:, :, :], in_=sel[:, :, :], compare_op=ALU.is_ge, fill=0.0,
                                    base=2, pattern=[[DH, GH], [0, P]], channel_multiplier=-1))
            for dst, low in ((hmask[:, :], 0), (tmp8[:, 0], 1), (tmp8[:, 1], 2)):
                link(pool.memset(dst, 1.0))
                link(pool.affine_select(out=dst, in_=dst, compare_op=ALU.is_ge, fill=0.0,
                                        base=-low, pattern=[[-DH, GH]], channel_multiplier=1))
                link(pool.affine_select(out=dst, in_=dst, compare_op=ALU.is_ge, fill=0.0,
                                        base=DH - 1, pattern=[[DH, GH]], channel_multiplier=-1))
            link(pool.iota(iota8[:, :], pattern=[[1, E]], base=0, channel_multiplier=0,
                           allow_small_or_imprecise_dtypes=True))
            link(pool.iota(capoff[:, :], pattern=[[CAP, E]], base=0, channel_multiplier=0,
                           allow_small_or_imprecise_dtypes=True))
            link(pool.iota(rowid[:, :], pattern=[[0, 1]], base=0, channel_multiplier=1,
                           allow_small_or_imprecise_dtypes=True))
            link(pool.iota(tile_f[:, :], pattern=[[1, RT]], base=0, channel_multiplier=0,
                           allow_small_or_imprecise_dtypes=True))
            link(pool.memset(zrow[:, :], 0.0))
            link(pool.memset(tab[:, 0, 0:ST], 0))
            link(pool.iota(tab[:, 1, 0:ST], pattern=[[P, ST]], base=SHARED, channel_multiplier=0))
            assert made[0] == CONSTANTS

            def rstd(dst, mv, col, per, i, stats, ready, used):
                due(pool, S[stats], B, i, B)
                settle(pool)
                pool.tensor_scalar(ve[:, col, :], mv[:, :, 1], EPS, None, ALU.add).then_inc(S["pool_chain"], 1)
                due(pool, S["pool_chain"], 3, i, per)
                due(pool, S[used], B, i + -1, B)
                pool.tensor_tensor(dst[:, :], ve[:, col, :], half_neg[:, 0:B], ALU.pow).then_inc(S[ready], 1)

            def block_diagonal(i, b):
                due(pool, S["qT_ready"], 1, i, 1)
                due(pool, S["A_done"], NS, i + -1, (b + 1) * NS // B)
                for g in range(GR):
                    pool.tensor_tensor(qbd[:, b, g], qT[i.side][:, g, b].unsqueeze(1).broadcast_to([P, GH, P]),
                                       hmask[:, :].unsqueeze(2).broadcast_to([P, GH, P]), ALU.mult)\
                        .then_inc(S["qbd_ready"], 1)

            pool.wait_ge(s_vinit, 5)

            def body(i):
                a1, a3 = i + 1, i + -1
                if has(a1):
                    due(pool, S["xn_stats"], B, a1, B)
                    settle(pool)
                    pool.tensor_scalar(ve[:, 0, :], mv1[a1.side][:, :, 1], EPS, None, ALU.add)\
                        .then_inc(S["rstd1_ready"], 1)
                    due(pool, S["rstd1_ready"], 2, a1, 1)
                    due(pool, S["xn_ready"], B, a1 + -2, B)
                    pool.tensor_tensor(rs1[a1.side][:, :], ve[:, 0, :], half_neg[:, 0:B], ALU.pow)\
                        .then_inc(S["rstd1_ready"], 1)
                if has(a3):
                    due(pool, S["o_stats"], B, a3, B)
                    settle(pool)
                    pool.tensor_scalar(ve[:, 1, :], mvo[:, :, 1], EPS, None, ALU.add).then_inc(S["rstdo_ready"], 1)
                    due(pool, S["rstdo_ready"], 2, a3, 1)
                    due(pool, S["ln_ready"], B, a3 + -1, B)
                    pool.tensor_tensor(rso[:, :], ve[:, 1, :], half_neg[:, 0:B], ALU.pow)\
                        .then_inc(S["rstdo_ready"], 1)
                    due(pool, S["ln_ready"], B, a3, B)
                    due_dma(pool, xr_loaded, a3)
                    due_dma(pool, x1_stored, a3 + -2)
                    due(pool, S["xn2_ready"], B, a3 + -2, B)
                    pool.tensor_tensor(free2(x1[a3.side][:, :, :]), free2(ln_o[:, :, :]),
                                       free2(x_res[a3.side][:, :, :]), ALU.add).then_inc(S["x1_ready"], 1)
                    due(pool, S["x1_stats"], B, a3, B)
                    settle(pool)
                    pool.tensor_scalar(ve[:, 2, :], mv2[:, :, 1], EPS, None, ALU.add).then_inc(S["rstd2_ready"], 1)
                    due(pool, S["rstd2_ready"], 2, a3, 1)
                    due(pool, S["xn2_ready"], B, a3 + -1, B)
                    pool.tensor_tensor(rs2[:, :], ve[:, 2, :], half_neg[:, 0:B], ALU.pow)\
                        .then_inc(S["rstd2_ready"], 1)
                if has(a1):
                    block_diagonal(a1, 0)
                    due(pool, S["ghi_ready"], 1, a1, 1)
                    settle(pool)
                    pool.tensor_scalar(free3(gt1[:, :, :, :]), free3(ghi[:, :, :, :]), part_mask[:, 0:1], None,
                                       ALU.mult).then_inc(S["gpool"], 1)
                    due(pool, S["gpool"], 4, a1, 1)
                    pool.tensor_tensor(free3(gr1[:, :, :, :]), free3(gT[:, :, :, :]), free3(gt1[:, :, :, :]),
                                       ALU.subtract).then_inc(S["gpool"], 1)
                    due(pool, S["gpool"], 4, a1, 2)
                    due(pool, S["gbc_done"], NS, a1 + -2, NS)
                    gp = gparts[a1.side]
                    settle(pool)
                    pool.tensor_copy(gp[:, :, :, 1:P].rearrange("p g b t -> p (g b) t"),
                                     gr1[:, :, :, 1:P].rearrange("p g b t -> p (g b) t")).then_inc(S["gpool"], 1)
                    due(pool, S["gpool"], 4, a1, 3)
                    settle(pool)
                    pool.tensor_scalar(gt1[:, :, :, 1:P].rearrange("p g b t -> p (g b) t"),
                                       gp[:, :, :, 1:P].rearrange("p g b t -> p (g b) t"), part_mask[:, 1:2], None,
                                       ALU.mult).then_inc(S["gpool"], 1)
                    due(pool, S["gpool"], 4, a1, 4)
                    pool.tensor_tensor(gp[:, :, :, 1:P].rearrange("p g b t -> p (g b) t"),
                                       gr1[:, :, :, 1:P].rearrange("p g b t -> p (g b) t"),
                                       gt1[:, :, :, 1:P].rearrange("p g b t -> p (g b) t"), ALU.subtract)\
                        .then_inc(S["gparts_ready"], 1)
                    due(pool, S["gam_ready"], GR * B, a1, GR * B)
                    due(pool, S["PV_done"], NS, a1 + -2, NS)
                    pool.tensor_tensor(free3(qg[a1.side][:, :, :, :]), free3(qT[a1.side][:, :, :, :]),
                                       free3(gam[a1.side][:, :, :, :]), ALU.mult).then_inc(S["qg_ready"], 1)
                    block_diagonal(a1, 1)
                if has(a3):
                    due(pool, S["pos_ready"], 1, a3, 1)
                    due(pool, S["xn2_ready"], B, a3, B)
                    for b in range(B):
                        for k in range(TOPK):
                            settle(pool)
                            pool.indirect_dma_start(
                                xs_d[:, :], bass.IndirectOffsetOnAxis(
                                    ap=posi[a3.side][:, b * TOPK + k:b * TOPK + k + 1], axis=0),
                                xn2[a3.side][:, b, :], None).then_inc(scattered[a3.side], 16)
                if a3.fixed and a3.index == 1:
                    pool.wait_ge(s_wmax, 1)
                    pool.partition_all_reduce(wmax[:, 1, 0:HEAD], wmax[:, 0, 0:HEAD], P, RMAX).then_inc(s_wall, 1)
            run_bodies(pool, body)
            pool.wait_ge(s_pad, 1)
            for e in range(E):
                settle(pool)
                pool.indirect_dma_start(xs_d[:, :], bass.IndirectOffsetOnAxis(ap=pad_row[:, e:e + 1], axis=0),
                                        zrow[:, :], None).then_inc(s_padded, 16)

        def tensor_a(pe):
            mm = nc.tensor.matmul
            pe.wait_ge(s_init, CONSTANTS)
            pe.wait_ge(S["wraw_loaded"], 16 * (5 + 2 * HEADS))
            for n in range(5):
                for k in range(KC):
                    for g in range(GR):
                        last = nc.tensor.transpose(bank[n][:, k * D + g * P:k * D + (g + 1) * P],
                                                   wraw[:, n, g, k * P:(k + 1) * P], ident[:, :])
                last.then_inc(S["wT_done"], 1)
            pe.wait_ge(S["wT_ready"], 5)
            pe.wait_ge(s_vinit, 5)

            def project(i, n, dst, done):
                for g in range(GR):
                    for k in range(KC):
                        last = mm(dst[:, g * B * P:(g + 1) * B * P], wT[:, n, k, g * P:(g + 1) * P],
                                  xnT[i.side][:, k, :], start=(k == 0), stop=(k == KC - 1))
                last.then_inc(S[done], 1)

            def where(s):
                return s * B // NS, (s % (NS // B)) // (NS // B // GR), s % (GH // SETH)

            def scores(i, s):
                b, g, q = where(s)
                due(pe, S["gparts_ready"], 1, i, 1)
                due(pe, S["decay_ready"], NS, i, s - 1)
                for h in range(SETH):
                    last = mm(pG[s % 2][:, h * P:(h + 1) * P], sel[:, q * SETH + h, :], gparts[i.side][:, g, b, :],
                              start=True, stop=True)
                last.then_inc(S["gbc_done"], 1)
                due(pe, S["kT_ready"], 1, i, 1)
                due(pe, S["qbd_ready"], GR * B, i, b * GR + g + 1)
                due(pe, S["probs_ready"], NS, i, s - 1)
                mm(pA[s % 2][:, :], kT[i.side][:, g, b, :],
                   qbd[:, b, g, q * SETH:(q + 1) * SETH, :].rearrange("p h t -> p (h t)"),
                   start=True, stop=True).then_inc(S["A_done"], 1)

            def attend(i, s):
                b, g, q = where(s)
                col = (b * GR + g) * P
                if s == 0:
                    due(pe, S["yT_ready"], 1, i + -1, 1)
                    due(pe, S["qg_ready"], 1, i, 1)
                    due(pe, S["state_ready"], GR * B, i + -1, GR * B)
                    due(pe, S["v_ready"], B, i, B)
                if q == 0:
                    mm(pY[:, col:col + P], state[:, b, g, :], qg[i.side][:, g, b, :], start=True, stop=False,
                       skip_group_check=True)
                due(pe, S["probs_ready"], NS, i, s + 1)
                for h in range(SETH):
                    head = q * SETH + h
                    r = head // 2 * 2 * DH
                    lo = DH if head % 2 == 0 else 0
                    last = mm(pY[r:r + 2 * DH, col:col + P],
                              vp[i.side][:, b, g * GH + head, lo:lo + 2 * DH], probs[s % 2][:, h, :],
                              start=False, stop=(head % 2 == 1), skip_group_check=True)
                last.then_inc(S["PV_done"], 1)

            def body(i):
                a1, a2, a3 = i + 1, i, i + -1
                A1, A2, A3 = has(a1), has(a2), has(a3)
                if A3:
                    due(pe, S["yT_ready"], 1, a3, 1)
                    if A2:
                        due(pe, S["v_ready"], B, a2, B)
                    due(pe, S["ln_ready"], B, a3 + -1, B)
                    for b in range(B):
                        for g in range(GR):
                            last = mm(X0[:, b * D:(b + 1) * D], yT[a3.side][:, b, g, :], wT[:, 3, g, :],
                                      start=(g == 0), stop=(g == GR - 1))
                    last.then_inc(S["o_done"], 1)
                if A2:
                    due(pe, S["kT_ready"], 1, a2, 1)
                    due(pe, S["um_ready"], 1, a2 + -1, 1)
                    for b in range(B):
                        for g in range(GR):
                            last = nc.tensor.transpose(pU[:, (b * GR + g) * P:(b * GR + g + 1) * P],
                                                       kT[a2.side][:, g, b, :], ident[:, :])
                    last.then_inc(S["ktok_done"], 1)
                    scores(a2, 0)
                    scores(a2, 1)
                if A1:
                    due(pe, S["xn_ready"], B, a1, B)
                    due(pe, S["pos_ready"], 1, a1 + -3, 1)
                    for k in range(KC):
                        for b in range(B):
                            last = nc.tensor.transpose(X1[:, (k * B + b) * P:(k * B + b + 1) * P],
                                                       xn[:, b, k * P:(k + 1) * P], ident[:, :])
                    last.then_inc(S["xT_done"], 1)
                if A2:
                    attend(a2, 0)
                    scores(a2, 2)
                if A1:
                    due(pe, S["xnT_ready"], 1, a1, 1)
                    due(pe, S["ln_ready"], B, a1 + -2, B)
                    if not A3 and a1.index > 0:
                        due(pe, S["v_ready"], B, a1 + -1, B)
                    project(a1, 0, X0, "q_done")
                if A2:
                    attend(a2, 1)
                    scores(a2, 3)
                if A1:
                    project(a1, 1, X1, "k_done")
                if A2:
                    attend(a2, 2)
                    scores(a2, 4)
                if A1:
                    due(pe, S["qT_ready"], 1, a1, 1)
                    project(a1, 4, X0, "g_done")
                if A2:
                    attend(a2, 3)
                    scores(a2, 5)
                if A3:
                    due(pe, S["xn2_ready"], B, a3, B)
                    if A1:
                        due(pe, S["kT_ready"], 1, a1, 1)
                    due(pe, S["pos_ready"], 1, a3 + -1, 1)
                    for k in range(KC):
                        for b in range(B):
                            last = nc.tensor.transpose(X1[:, (k * B + b) * P:(k * B + b + 1) * P],
                                                       xn2[a3.side][:, b, k * P:(k + 1) * P], ident[:, :])
                    last.then_inc(S["xn2T_done"], 1)
                if A1:
                    due(pe, S["eg_ready"], GR, a1, GR)
                    for b in range(B):
                        for k in range(KC):
                            last = mm(X0[:, b * D:(b + 1) * D], xnT[a1.side][:, k, b * P:(b + 1) * P], wT[:, 2, k, :],
                                      start=(k == 0), stop=(k == KC - 1))
                    last.then_inc(S["v_done"], 1)
                if A2:
                    attend(a2, 4)
                    scores(a2, 6)
                if A3:
                    due(pe, S["xn2T_ready"], 1, a3, 1)
                    if A1:
                        due(pe, S["kT_ready"], 1, a1, 1)
                    for b in range(B):
                        for k in range(KC):
                            last = mm(X1[:, b * E:(b + 1) * E], xn2T[:, k, b * P:(b + 1) * P], gw[:, k, :],
                                      start=(k == 0), stop=(k == KC - 1))
                    last.then_inc(S["gate_done"], 1)
                if A2:
                    attend(a2, 5)
                    scores(a2, 7)
                    attend(a2, 6)
                if A3:
                    due(pe, S["chosen_ready"], B, a3, B)
                    due(pe, S["csum_ready"], 2, a3 + -1, 2)
                    for b in range(B):
                        r = X1[:, (B + b) * E:(B + b + 1) * E]
                        mm(r, later[:, :], chosen[:, b, :], start=True, stop=False)
                        for before in range(b):
                            mm(r, ones[:, :], chosen[:, before, :], start=False, stop=False)
                        last = mm(r, ones[:, :], csum[:, :], start=False, stop=True)
                    last.then_inc(S["prefix_done"], 1)
                if A2:
                    attend(a2, 7)
                    due(pe, S["kd_ready"], NS, a2, NS)
                    for b in range(B):
                        for g in range(GR):
                            last = mm(pU[:, (b * GR + g) * P:(b * GR + g + 1) * P], kd[:, b, g, :],
                                      vp[a2.side][:, b, g * GH:(g + 1) * GH, DH:2 * DH], start=True, stop=True)
                    last.then_inc(S["U_done"], 1)
            run_bodies(pe, body)
            pe.wait_ge(S["csum_ready"], 2 * C)
            pe.wait_ge(S["pos_ready"], C)
            mm(X1[:, 0:E], ones[:, :], csum[:, :], start=True, stop=True).then_inc(s_total, 1)

        def largest(first, end):
            late_ = int(first > 0)
            nc.vector.wait_ge(s_w[late_], 16 * 3 * (end - first))
            nc.vector.tensor_reduce(wmax[:, 0, first:end], W[:, first:end].rearrange("p e m n -> p e (m n)"), AX_X,
                                    ALU.max, apply_absolute_value=True).then_inc(s_wmax, 1)

        def scales(link, dve, first, end):
            V = nc.vector
            dve.wait_ge(s_wall, 1 + int(first > 0))
            at = slice(first, end)
            link(V.tensor_scalar(wmax[:, 0, at], wmax[:, 1, at], 1e-30, None, ALU.max))
            link(V.tensor_scalar(wmax[:, 1, at].bitcast(I32), wmax[:, 0, at].bitcast(I32), 0x7F800000, None,
                                 ALU.bitwise_and))
            link(V.tensor_scalar(w_scale[:, 0, at], wmax[:, 1, at], 4.0, None, ALU.mult))
            link(V.reciprocal(w_scale[:, 1, at], w_scale[:, 0, at]))
            link(V.tensor_tensor(w_scale[:, 2, at], w_scale[:, 0, at], w_scale[:, 0, at], ALU.mult))
            V.tensor_tensor(w_scale[:, 2, at], w_scale[:, 2, at], w_scale[:, 0, at], ALU.mult).then_inc(s_scale, 1)

        def vector_a(dve):
            V = nc.vector
            V.memset(zeros[:, :], 0.0).then_inc(s_vinit, 1)
            V.memset(state[:, :, :, :], 0.0).then_inc(s_vinit, 1)
            V.memset(csum[:, :], 0.0).then_inc(s_vinit, 1)
            for n in range(2):
                V.memset(vp[n][:, :, :, :], 0.0)
                V.memset(gparts[n][:, :, :, :], 0.0)
            dve.wait_ge(s_init, CONSTANTS)
            V.tensor_reduce(part_mask[:, :], tmp8[:, :, :], AX_X, ALU.add).then_inc(s_vinit, 1)
            dve.wait_ge(S["wraw_loaded"], 16 * (5 + 2 * HEADS))
            V.tensor_scalar(nbg[:, :], nbg[:, :], -1.0, None, ALU.mult).then_inc(s_vinit, 1)
            dve.wait_ge(s_vinit, 5)

            def where(s):
                return s * B // NS, (s % (NS // B)) // (NS // B // GR), s % (GH // SETH)

            chains = {n: sem(f"dve_{n}_chain") for n in ("s1", "so", "s2", "S", "top", "wt", "pos")}

            def stat(i, key, src, st, mv, ready):
                for b in range(B):
                    V.bn_stats(st[:, b, :], src[b]).then_inc(chains[key], 1)
                for b in range(B):
                    due(dve, chains[key], B, i, b + 1)
                    settle(dve)
                    V.bn_aggr(mv[:, b, :], st[:, b, :]).then_inc(S[ready], 1)

            def normalise(dst, src, mv, rs, ready):
                for b in range(B):
                    V.tensor_scalar(dst[:, b, :], src[b], mv[:, b, 0:1], rs[:, b:b + 1], ALU.subtract, ALU.mult)\
                     .then_inc(S[ready], 1)

            def scan(i, s):
                due(dve, S["gbc_done"], NS, i, s + 1)
                due(dve, S["kd_ready"], NS, i, s - 1)
                V.tensor_tensor_scan(free2(decay[s % 2][:, :, :]), pG[s % 2][:, :], free2(diag4[:, :, :]), 0.0,
                                     ALU.mult, ALU.add).then_inc(S["decay_ready"], 1)

            def weigh(i, s):
                b, g, q = where(s)
                due(dve, S["decay_ready"], NS, i, s + 1)
                due(dve, S["A_done"], NS, i, s + 1)
                due(dve, S["PV_done"], NS, i, s - 1)
                V.tensor_tensor(free2(probs[s % 2][:, :, :]), pA[s % 2][:, :], free2(decay[s % 2][:, :, :]), ALU.mult)\
                 .then_inc(S["probs_ready"], 1)
                if s == 0:
                    due(dve, S["ktok_done"], 1, i, 1)
                    due(dve, S["U_done"], 1, i + -1, 1)
                hs = slice(q * SETH * DH, (q + 1) * SETH * DH)
                V.tensor_tensor(kd[:, b, g, hs].rearrange("p (h d) -> p h d", d=DH),
                                pU[:, (b * GR + g) * P:(b * GR + g + 1) * P][:, hs].rearrange("p (h d) -> p h d", d=DH),
                                decay[s % 2][:, :, P - 1:P].broadcast_to([P, SETH, DH]), ALU.mult)\
                 .then_inc(S["kd_ready"], 1)

            def feature(i, src, ready, e_ready, dst, e):
                due(dve, S[e_ready], 1, i, 1)
                V.scalar_tensor_tensor(free3(dst[i.side][:, :, :, :]), src[:, :], 1.0, e[:, :], ALU.add, ALU.max)\
                 .then_inc(S[ready], 1)

            def body(i):
                a1, a2, a3 = i + 1, i, i + -1
                A1, A2, A3 = has(a1), has(a2), has(a3)
                if A3:
                    due(dve, S["o_done"], 1, a3, 1)
                    due(dve, S["rstdo_ready"], 2, a3 + -1, 1)
                    due(dve, S["ln_ready"], B, a3 + -1, B)
                    stat(a3, "so", [X0[:, b * D:(b + 1) * D] for b in range(B)], sto, mvo, "o_stats")
                if A1:
                    due_dma(dve, x_loaded, a1)
                    due(dve, S["rstd1_ready"], 2, a1 + -2, 1)
                    due(dve, S["xn_ready"], B, a1 + -1, B)
                    stat(a1, "s1", [x_in[a1.side][:, b, :] for b in range(B)], st1, mv1[a1.side], "xn_stats")
                if A2:
                    scan(a2, 0)
                    scan(a2, 1)
                if A1:
                    due(dve, S["rstd1_ready"], 2, a1, 2)
                    due(dve, S["xn_stats"], B, a1, B)
                    due(dve, S["xT_done"], 1, a1 + -1, 1)
                    normalise(xn, [x_in[a1.side][:, b, :] for b in range(B)], mv1[a1.side], rs1[a1.side], "xn_ready")
                if A2:
                    weigh(a2, 0)
                if A3:
                    due(dve, S["rstdo_ready"], 2, a3, 2)
                    due(dve, S["x1_ready"], 1, a3 + -1, 1)
                    due(dve, S["o_stats"], B, a3, B)
                    normalise(ln_o, [X0[:, b * D:(b + 1) * D] for b in range(B)], mvo, rso, "ln_ready")
                if A2:
                    scan(a2, 2)
                    weigh(a2, 1)
                if A3:
                    due(dve, S["x1_ready"], 1, a3, 1)
                    due(dve, S["rstd2_ready"], 2, a3 + -1, 1)
                    due(dve, S["xn2_ready"], B, a3 + -1, B)
                    stat(a3, "s2", [x1[a3.side][:, b, :] for b in range(B)], st2, mv2, "x1_stats")
                if A2:
                    scan(a2, 3)
                    weigh(a2, 2)
                if A1:
                    due(dve, S["qbd_ready"], GR * B, a1 + -2, GR * B)
                    due(dve, S["qg_ready"], 1, a1 + -2, 1)
                    feature(a1, X0, "qT_ready", "eq_ready", qT, ef[0])
                if A3:
                    due(dve, S["rstd2_ready"], 2, a3, 2)
                    due(dve, S["x1_stats"], B, a3, B)
                    due_dma(dve, xs_stored, a3 + -2)
                    due_dma(dve, scattered, a3 + -2, B * TOPK)
                    due(dve, S["xn2T_done"], 1, a3 + -2, 1)
                    normalise(xn2[a3.side], [x1[a3.side][:, b, :] for b in range(B)], mv2, rs2, "xn2_ready")
                if A2:
                    scan(a2, 4)
                    weigh(a2, 3)
                if A1:
                    due(dve, S["A_done"], NS, a1 + -2, NS)
                    due(dve, S["ktok_done"], 1, a1 + -2, 1)
                    feature(a1, X1, "kT_ready", "ek_ready", kT, ef[1])
                if A2:
                    scan(a2, 5)
                    weigh(a2, 4)
                if A1:
                    due(dve, S["eg_ready"], GR, a1, GR)
                    V.tensor_scalar(free3(eg[:, :, :, :]), free3(eg[:, :, :, :]), 1.0, None, ALU.add)\
                     .then_inc(S["g1_ready"], 1)
                    due(dve, S["g1_ready"], 1, a1, 1)
                    due(dve, S["gpool"], 4, a1 + -1, 2)
                    due(dve, S["ghi_ready"], 1, a1 + -1, 1)
                    V.reciprocal(free3(gT[:, :, :, :]), free3(eg[:, :, :, :])).then_inc(S["gT_ready"], 1)
                    due(dve, S["gT_ready"], 1, a1, 1)
                if A2:
                    scan(a2, 6)
                    weigh(a2, 5)
                if A1:
                    due(dve, S["qg_ready"], 1, a1 + -2, 1)
                    for g in range(GR):
                        for b in range(B):
                            V.tensor_tensor_scan(gam[a1.side][:, g, b, :], gT[:, g, b, :], zeros[:, :], 1.0,
                                                 ALU.mult, ALU.add).then_inc(S["gam_ready"], 1)
                if A3:
                    due(dve, S["gate_done"], 1, a3, 1)
                    t = chains["top"]
                    V.tensor_copy(free2(lg[:, :, :]), X1[:, 0:B * E]).then_inc(t, 1)
                    due(dve, t, 4 + 3 * B, a3, 1)
                    for b in range(B):
                        settle(dve)
                        V.max(mx[:, b, :], lg[:, b, :]).then_inc(t, 1)
                    for b in range(B):
                        due(dve, t, 4 + 3 * B, a3, 2 + b)
                        settle(dve)
                        V.max_index(mi[:, b, :], mx[:, b, :], lg[:, b, :]).then_inc(t, 1)
                    due(dve, S["ew_ready"], 1, a3 + -1, 1)
                    V.tensor_tensor(dv[:, :], mx[:, :, 1], mx[:, :, 0], ALU.subtract).then_inc(S["top_ready"], 1)
                    due(dve, t, 4 + 3 * B, a3, 1 + 2 * B)
                    V.tensor_copy(mif[:, :, :], mi[:, :, :]).then_inc(t, 1)
                    due(dve, t, 4 + 3 * B, a3, 2 + 2 * B)
                    due(dve, S["pos_ready"], 1, a3 + -1, 1)
                    for b in range(B):
                        for k in range(TOPK):
                            V.tensor_scalar(oh[:, b, k, :], iota8[:, :], mif[:, b, k:k + 1], None, ALU.is_equal)\
                             .then_inc(t, 1)
                    due(dve, S["prefix_done"], 1, a3 + -1, 1)
                    due(dve, S["csum_ready"], 2, a3 + -1, 2)
                    for b in range(B):
                        due(dve, t, 4 + 3 * B, a3, 2 + 2 * B + TOPK * B)
                        V.tensor_tensor(chosen[:, b, :], oh[:, b, 0, :], oh[:, b, 1, :], ALU.add)\
                         .then_inc(S["chosen_ready"], 1)
                if A2:
                    scan(a2, 7)
                    weigh(a2, 6)
                if A3:
                    c = chains["wt"]
                    due(dve, S["ew_ready"], 1, a3, 1)
                    V.tensor_scalar(wtmp[:, 0, :], ew[:, :], 1.0, None, ALU.add).then_inc(c, 1)
                    due(dve, c, 3, a3, 1)
                    V.reciprocal(wtmp[:, 1, :], wtmp[:, 0, :]).then_inc(c, 1)
                    due(dve, c, 3, a3, 2)
                    V.tensor_copy(wts_all[:, bass.ds(a3.index, 1), :, 0], wtmp[:, 1, :].unsqueeze(1)).then_inc(c, 1)
                    V.tensor_tensor(wts_all[:, bass.ds(a3.index, 1), :, 1], wtmp[:, 1, :].unsqueeze(1),
                                    ew[:, :].unsqueeze(1), ALU.mult).then_inc(S["wts_ready"], 1)
                if A2:
                    weigh(a2, 7)
                if A3:
                    due(dve, S["prefix_done"], 1, a3, 1)
                    due(dve, S["chosen_ready"], B, a3, B)
                    c = chains["pos"]
                    N = 3 + B * TOPK
                    V.tensor_tensor(slot[:, :, :], X1[:, B * E:2 * B * E].rearrange("p (b e) -> p b e", e=E),
                                    capoff[:, :].unsqueeze(1).broadcast_to([P, B, E]), ALU.add).then_inc(c, 1)
                    V.tensor_tensor(csum[:, :], csum[:, :], chosen[:, 0, :], ALU.add).then_inc(S["csum_ready"], 1)
                    due(dve, S["csum_ready"], 2, a3, 1)
                    V.tensor_tensor(csum[:, :], csum[:, :], chosen[:, 1, :], ALU.add).then_inc(S["csum_ready"], 1)
                    due(dve, c, N, a3, 1)
                    for b in range(B):
                        for k in range(TOPK):
                            V.tensor_tensor_reduce(out=oh[:, b, k, :], in0=oh[:, b, k, :], in1=slot[:, b, :],
                                                   scale=1.0, scalar=0.0, op0=ALU.mult, op1=ALU.add,
                                                   accum_out=posf[:, b * TOPK + k:b * TOPK + k + 1]).then_inc(c, 1)
                    due(dve, c, N, a3, 1 + B * TOPK)
                    due_dma(dve, scattered, a3 + -2, B * TOPK)
                    V.tensor_copy(place_all[:, bass.ds(a3.index, 1), :], posf[:, :].unsqueeze(1)).then_inc(c, 1)
                    V.tensor_copy(choice_all[:, bass.ds(a3.index, 1), :].rearrange("p c (b k) -> p (c b) k", b=B),
                                  mif[:, :, 0:TOPK]).then_inc(c, 1)
                    V.tensor_copy(posi[a3.side][:, :], posf[:, :]).then_inc(S["pos_ready"], 1)
                if A2:
                    c = chains["S"]
                    due(dve, S["U_done"], 1, a2, 1)
                    due(dve, S["state_ready"], GR * B, a2 + -1, GR * B)
                    V.tensor_tensor(um[:, :, :, :].rearrange("p b g (h d) -> p (b g) h d", d=DH),
                                    pU[:, :].rearrange("p (a h d) -> p a h d", a=B * GR, d=DH),
                                    hmask[:, :].unsqueeze(1).unsqueeze(3).broadcast_to([P, B * GR, GH, DH]), ALU.mult)\
                     .then_inc(S["um_ready"], 1)
                    due(dve, S["um_ready"], 1, a2, 1)
                    due(dve, S["gam_ready"], GR * B, a2, GR * B)
                    for b in range(B):
                        for g in range(GR):
                            V.scalar_tensor_tensor(state[:, b, g, :], state[:, b, g, :],
                                                   gam[a2.side][:, g, b, P - 1:P], um[:, b, g, :],
                                                   ALU.mult, ALU.add).then_inc(S["state_ready"], 1)
                if a3.fixed and a3.index == 1:
                    largest(0, HEAD)
            run_bodies(dve, body)

            n = [0]

            def link(ins):
                n[0] += 1
                ins.then_inc(dve_chain, 1)
                dve.wait_ge(dve_chain, n[0])

            dve.wait_ge(s_total, 1)
            link(V.tensor_copy(total[:, :], X1[:, 0:E]))
            link(V.tensor_tensor(slot[:, 0, :], total[:, :], capoff[:, :], ALU.add))
            link(V.tensor_scalar(slot[:, 1, :], slot[:, 0, :], rowid[:, :], None, ALU.add))
            V.tensor_copy(pad_row[:, :], slot[:, 1, :]).then_inc(s_pad, 1)
            scales(link, dve, 0, HEAD)

            link(V.tensor_scalar(te[:, 0, :], total[:, :], (P - 1) / 2.0, 1.0 / P, ALU.add, ALU.mult))
            link(V.tensor_copy(te_i[:, :], te[:, 0, :]))
            link(V.tensor_copy(te[:, 1, :], te_i[:, :]))
            link(V.memset(te[:, 2, :], 0.0))
            link(V.tensor_tensor_scan(te[:, 3, :], te[:, 1, :], te[:, 2, :], 0.0, ALU.add, ALU.add))
            link(V.tensor_tensor(te[:, 0, :], te[:, 3, :], te[:, 1, :], ALU.subtract))
            link(V.tensor_scalar(te[:, 2, :], te[:, 0, :], float(ST), None, ALU.add))
            link(V.scalar_tensor_tensor(te[:, 4, :], te[:, 2, :], float(P), capoff[:, :], ALU.mult, ALU.subtract))
            n_all = C * B * TOPK
            link(V.tensor_tensor(found[:, :, :], choice_all[:, :, :].rearrange("p c n -> p (c n)").unsqueeze(2)
                                 .broadcast_to([P, n_all, E]),
                                 iota8[:, :].unsqueeze(1).broadcast_to([P, n_all, E]), ALU.is_equal))
            link(V.tensor_tensor(found[:, :, :], found[:, :, :],
                                 te[:, 4, :].unsqueeze(1).broadcast_to([P, n_all, E]), ALU.mult))
            link(V.tensor_reduce(choice_all[:, :, :].rearrange("p c n -> p (c n)"), found[:, :, :], AX_X, ALU.add))
            link(V.tensor_tensor(place_all[:, :, :], place_all[:, :, :], choice_all[:, :, :], ALU.add))
            link(V.tensor_copy(pos_all[:, :, :], place_all[:, :, :]))
            end, tiles = te[0:1, 3, :], te[0:1, 1, :]
            link(V.tensor_tensor(tg[:, 0], tile_f[:, :].unsqueeze(2).broadcast_to([1, RT, E]),
                                 end.unsqueeze(1).broadcast_to([1, RT, E]), ALU.is_ge))
            link(V.tensor_reduce(tb[:, 0, :], tg[:, 0], AX_X, ALU.add))
            link(V.tensor_tensor(tg[:, 1], tg[:, 0], tiles.unsqueeze(1).broadcast_to([1, RT, E]), ALU.mult))
            link(V.tensor_reduce(tb[:, 1, :], tg[:, 1], AX_X, ALU.add))
            link(V.tensor_tensor(tb[:, 2, :], tile_f[:, :], tb[:, 1, :], ALU.subtract))
            link(V.tensor_scalar(tb[:, 3, :], tb[:, 0, :], float(CAP), None, ALU.mult))
            link(V.scalar_tensor_tensor(tb[:, 4, :], tb[:, 2, :], float(P), tb[:, 3, :], ALU.mult, ALU.add))
            link(V.tensor_scalar(tb[:, 5, :], tb[:, 0, :], float(E), None, ALU.is_lt))
            link(V.tensor_tensor(tb[:, 6, :], tb[:, 4, :], tb[:, 5, :], ALU.mult))
            link(V.tensor_scalar(tb[:, 0, :], tb[:, 0, :], 1.0, None, ALU.add))
            link(V.tensor_tensor(tb[:, 0, :], tb[:, 0, :], tb[:, 5, :], ALU.mult))
            link(V.tensor_copy(tab[:, 0, ST:NT], tb[:, 0, :]))
            V.tensor_copy(tab[:, 1, ST:NT], tb[:, 6, :]).then_inc(s_tab, 1)

        phase_a.close()

        phase_b = ExitStack()

        def sc(name, shape, dt=F32):
            return phase_b.enter_context(nc.sbuf_tensor(name, shape, dt))

        wtmp_b = [sc(f"wtmp_b{n}", [P, MW]) for n in range(2)]
        wtmp_p = sc("wtmp_p", [P, 3, MW])
        xt = [sc(f"xt{n}", [P, D]) for n in range(2)]
        xh = [sc(f"xh{n}", [P, KC, P], F16) for n in range(2)]
        xl = [sc(f"xl{n}", [P, KC, P], F16) for n in range(2)]
        sl = [sc(f"sl{n}", [P, H]) for n in range(2)]
        gg = [sc(f"gg{n}", [P, H]) for n in range(2)]
        gh = [sc(f"gh{n}", [P, HC, P], F16) for n in range(2)]
        gl = [sc(f"gl{n}", [P, HC, P], F16) for n in range(2)]
        yo = [sc(f"yo{n}", [P, D]) for n in range(2)]
        gi = sc("gi", [P, B * TOPK], U32)
        ya = [[sc(f"ya{b}{k}", [P, D]) for k in range(TOPK)] for b in range(B)]
        ysh = [sc(f"ysh{b}", [P, D]) for b in range(B)]
        x1c = [sc(f"x1c{b}", [P, D]) for b in range(B)]
        cmb = [sc(f"cmb{b}", [P, D]) for b in range(B)]
        lnc = [sc(f"lnc{b}", [P, D]) for b in range(B)]
        oc = [sc(f"oc{b}", [P, D]) for b in range(B)]
        stc = sc("stc", [P, B, 6])
        mvc = sc("mvc", [P, B, 2])
        vec = sc("vec", [P, B])
        rsc = sc("rsc", [P, B])

        pT, pH1, pH2, pGT, pYB = bank[0], bank[1:3], bank[3:5], bank[5], bank[6:8]
        namesB = ("late_chain pool_split experts_split w_scaled w_high w_low xtT_done xh_ready xl_ready h1_done h2_done silu_ready gg_ready ggT_done"
                  " gh_ready gl_ready y_done yo_ready").split()
        T = {n: sem("b_" + n) for n in namesB}
        xt_loaded = [sem(f"xt_loaded{n}") for n in range(2)]
        yo_stored = [sem(f"yo_stored{n}") for n in range(2)]

        HOOK = ST // 4

        def run_tiles(eng, body, midway=None, before_routed=None):
            for t in range(-2, 4):
                body(Step.of(t))
            with eng.Fori(2, HOOK) as j:
                body(Step(j, 0))
                body(Step(j, 1))
            if midway:
                midway()
            with eng.Fori(HOOK, ST // 2 - 1) as j:
                body(Step(j, 0))
                body(Step(j, 1))
            if before_routed:
                before_routed()
            eng.wait_ge(s_tab, 1)
            with eng.Fori(ST // 2 - 1, NT // 2 - 1) as j:
                body(Step(j, 0))
                body(Step(j, 1))
            for t in range(NT - 2, NT + 2):
                body(Step.of(t))

        def is_tile(t):
            return not t.fixed or 0 <= t.index < NT

        def entry(eng, row, t, most):
            return eng.value_load(tab[0:1, row, bass.ds(t.index, 1)], min_val=0, max_val=most)

        def expert_of(eng, t):
            if t.fixed and t.index < ST:
                return bass.ds(0, 1)
            return bass.ds(entry(eng, 0, t, E), 1)

        def sync_b(sp):
            for n in range(2):
                sp.wait_ge(xs_stored[n], 16 * C // 2)
                sp.wait_ge(x1_stored[n], 16 * C // 2)
                sp.wait_ge(scattered[n], 16 * B * TOPK * C // 2)
            sp.wait_ge(s_padded, 16 * E)

            def body(t):
                if is_tile(t + 2):
                    due(sp, T["xtT_done"], 1, t, 1)
                    row = entry(sp, 1, t + 2, SHARED + TOK - P)
                    sp.dma_start(xt[t.side][:, :], xs_d[bass.ds(row, P), :]).then_inc(xt_loaded[t.side], 16)
                if is_tile(t + -2):
                    due(sp, T["yo_ready"], 1, t + -2, 1)
                    sp.dma_start(ys_d[bass.ds((t + -2).index * P, P), :], yo[t.side][:, :])\
                      .then_inc(yo_stored[t.side], 16)
            run_tiles(sp, body)

        def tensor_b(pe):
            mm = nc.tensor.matmul
            pe.wait_ge(T["w_low"], 3)

            def turn_x(t):
                due_dma(pe, xt_loaded, t)
                for k in range(KC):
                    last = nc.tensor.transpose(pT[:, k * P:(k + 1) * P], xt[t.side][:, k * P:(k + 1) * P], ident[:, :])
                last.then_inc(T["xtT_done"], 1)

            def turn_g(t):
                due(pe, T["gg_ready"], 1, t, 1)
                for c in range(HC):
                    last = nc.tensor.transpose(pGT[:, c * P:(c + 1) * P], gg[t.side][:, c * P:(c + 1) * P], ident[:, :])
                last.then_inc(T["ggT_done"], 1)

            def hidden(t, e, m, dst, done, between=None):
                n = 0
                for k in range(KC):
                    if k == 1 and between is not None:
                        between()
                    for a, s in ((xh, 0), (xh, 1), (xl, 0)):
                        last = mm(dst[t.side][:, :], a[t.side][:, k, :],
                                  W16[:, e, m, s, k * H:(k + 1) * H], start=(n == 0), stop=(n == 3 * KC - 1))
                        n += 1
                last.then_inc(T[done], 1)

            def project(t, e):
                due(pe, T["gl_ready"], 1, t, 1)
                n = 0
                for c in range(HC):
                    for a, s in ((gh, 0), (gh, 1), (gl, 0)):
                        last = mm(pYB[t.side][:, 0:D], a[t.side][:, c, :],
                                  W16[:, e, 2, s, c * D:(c + 1) * D], start=(n == 0), stop=(n == 3 * HC - 1))
                        n += 1
                last.then_inc(T["y_done"], 1)

            def body(t):
                if is_tile(t):
                    e = expert_of(pe, t)
                if is_tile(t + -2):
                    e_before = expert_of(pe, t + -2)
                if is_tile(t):
                    due(pe, T["xl_ready"], 1, t, 1)
                    hidden(t, e, 0, pH1, "h1_done", between=lambda: transposes(t))
                else:
                    transposes(t)
                if is_tile(t):
                    hidden(t, e, 1, pH2, "h2_done")
                if is_tile(t + -2):
                    project(t + -2, e_before)

            def transposes(t):
                due(pe, T["yo_ready"], 1, t + -4, 1)
                if is_tile(t + -1):
                    turn_g(t + -1)
                if is_tile(t + 1):
                    turn_x(t + 1)
            run_tiles(pe, body, before_routed=lambda: pe.wait_ge(T["experts_split"], E))

        def scalar_b(act):
            for m in range(3):
                act.wait_ge(T["w_scaled"], m + 1)
                act.activation(W16[:, 0, m, 0, :], wtmp_b[m % 2][:, :], ACT.Copy).then_inc(T["w_high"], 1)

            def body(t):
                if is_tile(t + -1):
                    u = t + -1
                    due(act, T["ggT_done"], 1, u, 1)
                    due(act, T["y_done"], 1, u + -2, 1)
                    act.activation(gh[u.side][:, :, :].rearrange("p c t -> p (c t)"), pGT[:, :], ACT.Copy)\
                       .then_inc(T["gh_ready"], 1)
                if is_tile(t + 1):
                    u = t + 1
                    due(act, T["xtT_done"], 1, u, 1)
                    due(act, T["h2_done"], 1, u + -2, 1)
                    act.activation(xh[u.side][:, :, :].rearrange("p k t -> p (k t)"), pT[:, 0:D], ACT.Copy)\
                       .then_inc(T["xh_ready"], 1)
                if is_tile(t):
                    e = expert_of(act, t)
                    due(act, T["h1_done"], 1, t, 1)
                    due(act, T["gg_ready"], 1, t + -2, 1)
                    act.activation(sl[t.side][:, :], pH1[t.side][:, :], ACT.Silu, scale=w_scale[:, 0, e])\
                       .then_inc(T["silu_ready"], 1)
            act.wait_ge(s_scale, 1)
            run_tiles(act, body)

        def vector_b(dve):
            V = nc.vector
            dve.wait_ge(s_scale, 1)
            for m in range(3):
                V.tensor_scalar(wtmp_b[m % 2][:, :], W[:, 0, m, :], w_scale[:, 1, 0:1], None, ALU.mult)\
                 .then_inc(T["w_scaled"], 1)
                dve.wait_ge(T["w_high"], m + 1)
                dve.wait_ge(T["w_scaled"], m + 1)
                V.tensor_tensor(W16[:, 0, m, 1, :], wtmp_b[m % 2][:, :], W16[:, 0, m, 0, :], ALU.subtract)\
                 .then_inc(T["w_low"], 1)

            n = [0]

            def link(ins):
                n[0] += 1
                ins.then_inc(T["late_chain"], 1)
                dve.wait_ge(T["late_chain"], n[0])

            def late_scale():
                largest(HEAD, NE)
                scales(link, dve, HEAD, NE)

            def body(t):
                if is_tile(t + -1):
                    u = t + -1
                    due(dve, T["gh_ready"], 1, u, 1)
                    due(dve, T["y_done"], 1, u + -2, 1)
                    V.tensor_tensor(gl[u.side][:, :, :].rearrange("p c t -> p (c t)"), pGT[:, :],
                                    gh[u.side][:, :, :].rearrange("p c t -> p (c t)"), ALU.subtract)\
                     .then_inc(T["gl_ready"], 1)
                if is_tile(t + 1):
                    u = t + 1
                    due(dve, T["xh_ready"], 1, u, 1)
                    due(dve, T["h2_done"], 1, u + -2, 1)
                    V.tensor_tensor(xl[u.side][:, :, :].rearrange("p k t -> p (k t)"), pT[:, 0:D],
                                    xh[u.side][:, :, :].rearrange("p k t -> p (k t)"), ALU.subtract)\
                     .then_inc(T["xl_ready"], 1)
                if is_tile(t):
                    e = expert_of(dve, t)
                    due(dve, T["silu_ready"], 1, t, 1)
                    due(dve, T["h2_done"], 1, t, 1)
                    due(dve, T["ggT_done"], 1, t + -2, 1)
                    V.scalar_tensor_tensor(gg[t.side][:, :], sl[t.side][:, :], w_scale[:, 1, e], pH2[t.side][:, :],
                                           ALU.mult, ALU.mult).then_inc(T["gg_ready"], 1)
                if is_tile(t + -2):
                    u = t + -2
                    e = expert_of(dve, u)
                    due(dve, T["y_done"], 1, u, 1)
                    due_dma(dve, yo_stored, u + -2)
                    V.tensor_scalar(yo[u.side][:, :], pYB[u.side][:, 0:D], w_scale[:, 2, e], None, ALU.mult)\
                     .then_inc(T["yo_ready"], 1)
            run_tiles(dve, body, midway=late_scale)

        def pool_b(pool):
            def split(e):
                whole = W[:, e].rearrange("p m n -> p (m n)")
                if e > 1:
                    pool.wait_ge(T["experts_split"], e - 1)
                pool.tensor_tensor(wtmp_p[:, :, :].rearrange("p m n -> p (m n)"), whole,
                                   w_scale[:, 1, e:e + 1].broadcast_to([P, 3 * MW]), ALU.mult).then_inc(T["pool_split"], 1)
                pool.wait_ge(T["pool_split"], 2 * e - 1)
                settle(pool)
                pool.tensor_copy(W16[:, e, :, 0, :], wtmp_p[:, :, :]).then_inc(T["pool_split"], 1)
                pool.wait_ge(T["pool_split"], 2 * e)
                pool.tensor_tensor(W16[:, e, :, 1, :], wtmp_p[:, :, :], W16[:, e, :, 0, :], ALU.subtract)\
                    .then_inc(T["experts_split"], 1)

            pool.wait_ge(s_scale, 1)
            for e in range(1, HEAD):
                split(e)
            pool.wait_ge(s_wmax, 2)
            pool.partition_all_reduce(wmax[:, 1, HEAD:NE], wmax[:, 0, HEAD:NE], P, RMAX).then_inc(s_wall, 1)
            pool.wait_ge(s_scale, 2)
            for e in range(HEAD, NE):
                split(e)

        namesC = "gi_ready ya_read mix1 mix2 stat1 stats_ready vare rstd_ready lnc_ready oc_ready".split()
        U = {n: sem("c_" + n) for n in namesC}
        ysh_loaded = [sem(f"ysh_loaded{b}") for b in range(B)]
        x1_loaded = [sem(f"x1_loaded{b}") for b in range(B)]
        ya_loaded = [sem(f"ya_loaded{b}") for b in range(B)]
        out_stored = [sem(f"out_stored{b}") for b in range(B)]
        out_rows = out.rearrange("b s d -> (b s) d")

        def turns(eng, body):
            body(0)
            with eng.Fori(1, C) as c:
                body(c)

        def due_c(eng, sem_, per, c, k):
            if isinstance(c, int) and c * per + k <= 0:
                return
            eng.wait_ge(sem_, c * per + k)

        def sync_c(sp):
            for n in range(2):
                sp.wait_ge(yo_stored[n], 16 * NT // 2)

            def body(c):
                for b in range(B):
                    due_c(sp, U["mix1"], B, c - 1, b + 1)
                    sp.dma_start(ysh[b][:, :], ys_d[bass.ds(c * P + b * SEQ, P), :]).then_inc(ysh_loaded[b], 16)
                    due_c(sp, U["oc_ready"], B, c - 1, b + 1)
                    sp.dma_start(x1c[b][:, :], x1_d[bass.ds(c * P + b * SEQ, P), :]).then_inc(x1_loaded[b], 16)
                for b in range(B):
                    due_c(sp, U["oc_ready"], B, c, b + 1)
                    sp.dma_start(out_rows[bass.ds(c * P + b * SEQ, P), :], oc[b][:, :]).then_inc(out_stored[b], 16)
            turns(sp, body)
            for b in range(B):
                sp.wait_ge(out_stored[b], 16 * C)

        def pool_c(pool):
            for n in range(2):
                pool.wait_ge(yo_stored[n], 16 * NT // 2)

            def body(c):
                due_c(pool, U["gi_ready"], 1, c, 1)
                for b in range(B):
                    due_c(pool, U["mix2"], B, c - 1, b + 1)
                    for k in range(TOPK):
                        settle(pool)
                        pool.indirect_dma_start(ya[b][k][:, :], None, ys_d[:, :], bass.IndirectOffsetOnAxis(
                            ap=gi[:, b * TOPK + k:b * TOPK + k + 1], axis=0)).then_inc(ya_loaded[b], 16)
                due_c(pool, U["stats_ready"], B, c, B)
                settle(pool)
                pool.tensor_scalar(vec[:, :], mvc[:, :, 1], EPS, None, ALU.add).then_inc(U["vare"], 1)
                due_c(pool, U["vare"], 1, c, 1)
                due_c(pool, U["lnc_ready"], B, c - 1, B)
                pool.tensor_tensor(rsc[:, :], vec[:, :], half_neg[:, 0:B], ALU.pow).then_inc(U["rstd_ready"], 1)
                for b in range(B):
                    due_c(pool, U["lnc_ready"], B, c, b + 1)
                    due_c(pool, x1_loaded[b], 16, c, 16)
                    due_c(pool, out_stored[b], 16, c - 1, 16)
                    pool.tensor_tensor(oc[b][:, :], lnc[b][:, :], x1c[b][:, :], ALU.add).then_inc(U["oc_ready"], 1)
            turns(pool, body)

        def vector_c(dve):
            V = nc.vector

            def body(c):
                for b in range(B):
                    due_c(dve, ya_loaded[b], 16 * TOPK, c - 1, 16 * TOPK)
                V.tensor_copy(gi[:, :].unsqueeze(1), pos_all[:, bass.ds(c, 1), :]).then_inc(U["gi_ready"], 1)
                for b in range(B):
                    due_c(dve, ya_loaded[b], 16 * TOPK, c, 16 * TOPK)
                    due_c(dve, ysh_loaded[b], 16, c, 16)
                    due_c(dve, U["lnc_ready"], B, c - 1, b + 1)
                    V.scalar_tensor_tensor(cmb[b][:, :], ya[b][0][:, :], wts_all[:, bass.ds(c, 1), b, 0],
                                           ysh[b][:, :], ALU.mult, ALU.add).then_inc(U["mix1"], 1)
                    due_c(dve, U["mix1"], B, c, b + 1)
                    V.scalar_tensor_tensor(cmb[b][:, :], ya[b][1][:, :], wts_all[:, bass.ds(c, 1), b, 1],
                                           cmb[b][:, :], ALU.mult, ALU.add).then_inc(U["mix2"], 1)
                    due_c(dve, U["mix2"], B, c, b + 1)
                    V.bn_stats(stc[:, b, :], cmb[b][:, :]).then_inc(U["stat1"], 1)
                    due_c(dve, U["stat1"], B, c, b + 1)
                    due_c(dve, U["vare"], 1, c - 1, 1)
                    settle(dve)
                    V.bn_aggr(mvc[:, b, :], stc[:, b, :]).then_inc(U["stats_ready"], 1)
                due_c(dve, U["rstd_ready"], 1, c, 1)
                for b in range(B):
                    due_c(dve, U["stats_ready"], B, c, b + 1)
                    due_c(dve, U["oc_ready"], B, c - 1, b + 1)
                    V.tensor_scalar(lnc[b][:, :], cmb[b][:, :], mvc[:, b, 0:1], rsc[:, b:b + 1],
                                    ALU.subtract, ALU.mult).then_inc(U["lnc_ready"], 1)
            turns(dve, body)

        phase_b.close()

        with nc.Block() as block:
            @block.sync
            def _(sp):
                sync_a(sp)
                sync_b(sp)
                sync_c(sp)

            @block.scalar
            def _(act):
                scalar_a(act)
                scalar_b(act)

            @block.gpsimd
            def _(pool):
                pool_a(pool)
                pool_b(pool)
                pool_c(pool)

            @block.vector
            def _(dve):
                vector_a(dve)
                vector_b(dve)
                vector_c(dve)

            @block.tensor
            def _(pe):
                tensor_a(pe)
                tensor_b(pe)


_INS = ['L0_attn_x', 'L0_attn_Wq', 'L0_attn_Wk', 'L0_attn_Wv', 'L0_attn_Wo', 'L0_attn_Wg', 'L0_attn_bg',
        'L0_ffn_gate_w', 'L0_ffn_ew1', 'L0_ffn_ew2', 'L0_ffn_ew3', 'L0_ffn_sw1', 'L0_ffn_sw2', 'L0_ffn_sw3']
_OUTS = [((2, 2048, 256), 'float32')]


def kernel(**inputs):
    import numpy as _np
    import concourse.bacc as _bacc
    from concourse import mybir as _mybir
    from concourse.bass_utils import run_bass_kernel_spmd as _run

    nc = _bacc.Bacc("TRN2", target_bir_lowering=False, num_devices=1)
    arrays, args = {}, []
    for name in _INS:
        a = _np.ascontiguousarray(inputs[name])
        arrays[f"in_{name}_dram"] = a
        args.append(nc.dram_tensor(f"in_{name}_dram", a.shape, _mybir.dt.from_np(a.dtype), kind="ExternalInput").ap())
    for i, (shape, dtype) in enumerate(_OUTS):
        dt = _mybir.dt.from_np(_np.dtype(dtype))
        args.append(nc.dram_tensor(f"out_{i}_dram", shape, dt, kind="ExternalOutput").ap())
    sandwich_kernel(nc, *args)
    r = _run(nc, [arrays], core_ids=[0])
    return r.results[0]["out_0_dram"]
```

```python
from contextlib import ExitStack

import concourse.bass as bass
from concourse import mybir

ALU = mybir.AluOpType
ACT = mybir.ActivationFunctionType
F32 = mybir.dt.float32
F16 = mybir.dt.float16
BF16 = mybir.dt.bfloat16
U32 = mybir.dt.uint32
I32 = mybir.dt.int32
AX_X = mybir.AxisListType.X
RMAX = bass.bass_isa.ReduceOp.max
EPS = 1e-5


class Step:

    def __init__(self, half, side, kind=None):
        self.half, self.side, self.kind = half, side, kind

    @staticmethod
    def of(i):
        return Step(i // 2, i % 2)

    def __add__(self, d):
        q = self.side + d
        return Step(self.half + q // 2, q % 2, self.kind)

    @property
    def index(self):
        return self.half * 2 + self.side

    @property
    def fixed(self):
        return isinstance(self.half, int)


def due(eng, sem, per, step, k):
    n = step.index * per + k
    if step.fixed and n <= 0:
        return
    eng.wait_ge(sem, n)


def due_dma(eng, sems, step, n=1):
    if step.fixed and step.half < 0:
        return
    eng.wait_ge(sems[step.side], (step.half + 1) * (16 * n))


def sandwich_kernel(nc, x, Wq, Wk, Wv, Wo, Wg, bg, gate_w, ew1, ew2, ew3, sw1, sw2, sw3, out):
    P = 128
    B, SEQ, D = x.shape
    HEADS = Wg.shape[0]
    DH = D // HEADS
    SCALE = float(DH) ** -0.5
    KC = D // P
    GH = P // DH
    GR = HEADS // GH
    SETH = 4
    NS = B * HEADS // SETH
    C = SEQ // P
    TOK = B * SEQ
    E = gate_w.shape[1]
    TOPK = 2
    H = ew1.shape[2]
    HC = H // P
    NE = E + 1
    HEAD = 6
    MW = KC * H
    CAP = TOK + P
    SHARED = E * CAP
    ROWS = SHARED + TOK
    ST = TOK // P
    RT = TOPK * TOK // P + E
    VW = 3 * DH
    NT = ST + RT
    EARLY = 12
    T0 = EARLY + RT
    assert (B, GR, KC, TOPK) == (2, 2, 2, 2) and C % 2 == 0 and HC * D == MW and RT % 2 == 0
    assert C * B <= 256
    assert EARLY % 4 == 0 and 8 < EARLY < C

    ctx = ExitStack()
    with ctx:
        def sem(name):
            return ctx.enter_context(nc.semaphore(name))

        def sb(name, shape, dt=F32):
            return ctx.enter_context(nc.sbuf_tensor(name, shape, dt))

        xs_d = nc.dram_tensor("xs_scratch", [ROWS, D], F32).ap()
        ys_d = nc.dram_tensor("ys_scratch", [RT * P, D], F32).ap()
        x1_d = nc.dram_tensor("x1_scratch", [TOK, D], F32).ap()

        bank = [ctx.enter_context(nc.psum_tensor(f"bank{n}", [P, 512], F32)) for n in range(8)]

        W = sb("W", [P, NE, 3, MW])
        W16 = W[:].rearrange("p e m n -> p (e m n)").bitcast(F16).rearrange(
            "p (e m s n) -> p e m s n", e=NE, m=3, s=2)
        ident = sb("ident", [P, P])
        half_neg = sb("half_neg", [P, 2])
        wts_all = sb("wts_all", [P, C, B, TOPK])
        pos_all = sb("pos_all", [P, C, B * TOPK], U32)
        wmax = sb("wmax", [P, 2, NE])
        w_scale = sb("w_scale", [P, 3, NE])
        tab = sb("tab", [1, 2, RT], I32)
        choice_all = sb("choice_all", [P, C, B * TOPK])
        place_all = sb("place_all", [P, C, B * TOPK])
        iota8 = sb("iota8", [P, E])
        capoff = sb("capoff", [P, E])
        rowid = sb("rowid", [P, 1])
        total = sb("total", [P, E])
        pad_row = sb("pad_row", [P, E], U32)
        zrow = sb("zrow", [P, D])
        tile_f = sb("tile_f", [1, RT])
        te = sb("te", [P, 5, E])
        te_i = sb("te_i", [P, E], I32)
        tb = sb("tb", [1, 8, RT])
        tg = sb("tg", [1, 2, RT, E])
        found = sb("found", [P, C * B * TOPK, E])
        wpart = sb("wpart", [P, HEAD, 3])

        s_w = [sem(f"s_w_loaded{n}") for n in range(2)]
        s_init = sem("s_init")
        s_vinit = sem("s_vinit")
        dve_chain = sem("dve_chain")

        phase_a = ExitStack()

        def sa(name, shape, dt=F32):
            return phase_a.enter_context(nc.sbuf_tensor(name, shape, dt))

        late = W[:, HEAD:NE].rearrange("p e m n -> p (e m n)")
        taken = [0]

        def in_late(*shape):
            n = 1
            for d in shape:
                n *= d
            taken[0] += n
            assert taken[0] <= (NE - HEAD) * 3 * MW
            ap = late[:, taken[0] - n:taken[0]]
            if len(shape) == 3:
                return ap.rearrange("p (a b c) -> p a b c", a=shape[0], b=shape[1])
            return ap.rearrange("p (a b c d) -> p a b c d", a=shape[0], b=shape[1], c=shape[2])

        qbd = in_late(B, GR, GH, P)
        wraw = qbd.rearrange("p b g h t -> p (b g h t)")[:, 0:5 * GR * D].rearrange(
            "p (n g d) -> p n g d", n=5, g=GR)
        wT = sa("wT", [P, 5, KC, D])
        gw = sa("gw", [P, KC, E])
        hbg = sa("hbg", [P, GR])
        sel = sa("sel", [P, GH, P], BF16)
        diag4 = sa("diag4", [P, SETH, P])
        later = sa("later", [P, P], BF16)
        ones = sa("ones", [P, P], BF16)
        hmask = sa("hmask", [P, GH])
        tmp8 = sa("tmp8", [P, 2, GH])
        part_mask = sa("part_mask", [P, 2])
        zeros = sa("zeros", [P, P])

        x_in = [sa(f"x_in{n}", [P, B, D]) for n in range(2)]
        x_res = [sa(f"x_res{n}", [P, B, D]) for n in range(2)]
        st1 = sa("st1", [P, B, 6])
        mv1 = [sa(f"mv1_{n}", [P, B, 2]) for n in range(2)]
        ve = sa("ve", [P, 3, B])
        rs1 = [sa(f"rs1_{n}", [P, B]) for n in range(2)]
        xn = sa("xn", [P, B, D])
        xnT_ = sa("xnT", [P, 2, KC, B * P])
        xnT = [xnT_[:, n] for n in range(2)]
        rneg = sa("rneg", [P, GR * B * P])
        ef_ = sa("ef", [P, 2, GR * B * P])
        ef = [ef_[:, n] for n in range(2)]
        wtmp_b = [ef_[:, :, :].rearrange("p n t -> p (n t)"), xnT_[:, :, :, :].rearrange("p n k t -> p (n k t)")]
        qT = [sa(f"qT{n}", [P, GR, B, P]) for n in range(2)]
        kT = [sa(f"kT{n}", [P, GR, B, P]) for n in range(2)]
        eg = sa("eg", [P, GR, B, P])
        gT = sa("gT", [P, GR, B, P])
        ghi = sa("ghi", [P, GR, B, P], BF16)
        gt1 = sa("gt1", [P, GR, B, P])
        gr1 = sa("gr1", [P, GR, B, P])
        gparts = [sa(f"gparts{n}", [P, GR, B, P], BF16) for n in range(2)]
        gam = [in_late(GR, B, P) for n in range(2)]
        qg = [in_late(GR, B, P) for n in range(2)]
        vp = [in_late(B, HEADS, VW) for n in range(2)]
        decay = [sa(f"decay{n}", [P, SETH, P]) for n in range(2)]
        probs = [sa(f"probs{n}", [P, SETH, P]) for n in range(2)]
        kd = sa("kd", [P, B, GR, P])
        um = sa("um", [P, B, GR, P])
        state = sa("state", [P, B, GR, P])
        yT = [sa(f"yT{n}", [P, B, GR, P]) for n in range(2)]
        sto = sa("sto", [P, B, 6])
        mvo = sa("mvo", [P, B, 2])
        rso = sa("rso", [P, B])
        ln_o = sa("ln_o", [P, B, D])
        x1 = [sa(f"x1_{n}", [P, B, D]) for n in range(2)]
        st2 = sa("st2", [P, B, 6])
        mv2 = sa("mv2", [P, B, 2])
        rs2 = sa("rs2", [P, B])
        xn2 = [sa(f"xn2_{n}", [P, B, D]) for n in range(2)]
        xn2T = sa("xn2T", [P, KC, B * P])
        lg = sa("lg", [P, B, E])
        mx = sa("mx", [P, B, 8])
        mi = sa("mi", [P, B, 8], U32)
        mif = sa("mif", [P, B, 8])
        dv = sa("dv", [P, B])
        ew = sa("ew", [P, B])
        wtmp = sa("wtmp", [P, 2, B])
        oh = sa("oh", [P, B, TOPK, E])
        chosen = sa("chosen", [P, B, E], BF16)
        csum = sa("csum", [P, E], BF16)
        slot = sa("slot", [P, B, E])
        posf = sa("posf", [P, B * TOPK])
        posi = [sa(f"posi{n}", [P, B * TOPK], U32) for n in range(2)]

        pA, pG, pY, pU, X0, X1 = bank[0:2], bank[2:4], bank[4], bank[5], bank[6], bank[7]

        names = ("wraw_loaded wT_done wT_ready xn_stats rstd1_ready xn_ready xT_done xnT_ready q_done rq_ready"
                 " eq_ready qT_ready k_done rk_ready ek_ready kT_ready g_done eg_ready gT_ready ghi_ready"
                 " gpool gparts_ready gam_ready qg_ready qbd_ready v_done v_ready ktok_done gbc_done decay_ready"
                 " A_done probs_ready kd_ready PV_done U_done um_ready state_ready yT_ready o_done o_stats"
                 " rstdo_ready ln_ready x1_ready x1_stats rstd2_ready xn2_ready xn2T_done xn2T_ready gate_done"
                 " top_ready ew_ready chosen_ready prefix_done pos_ready wts_ready csum_ready pool_chain").split()
        S = {n: sem(n) for n in names}
        CONSTANTS = 24
        x_loaded = [sem(f"x_loaded{n}") for n in range(2)]
        xr_loaded = [sem(f"xr_loaded{n}") for n in range(2)]
        x1_stored = [sem(f"x1_stored{n}") for n in range(2)]
        xs_stored = [sem(f"xs_stored{n}") for n in range(2)]
        scattered = [sem(f"scattered{n}") for n in range(2)]
        s_total = sem("s_total")
        s_totals = sem("s_totals")
        s_pad = sem("s_pad_rows")
        s_padded = sem("s_padded")
        s_wmax = sem("s_wmax")
        s_wall = sem("s_wmax_all")
        s_scale = sem("s_scale")
        s_tab = sem("s_table")
        s_wpart = sem("s_wmax_parts")
        s_place = sem("s_place")
        w_scaled, w_high, w_low = sem("w_scaled"), sem("w_high"), sem("w_low")

        x_by_step = x.rearrange("b (c p) d -> c p b d", p=P)
        x1_by_step = x1_d.rearrange("(b c p) d -> c p b d", b=B, p=P)
        xs_by_step = xs_d[SHARED:SHARED + TOK, :].rearrange("(b c p) d -> c p b d", b=B, p=P)

        def settle(eng):
            eng.nop(nofuse=True)

        def free2(ap):
            return ap.rearrange("p a b -> p (a b)")

        def free3(ap):
            return ap.rearrange("p a b c -> p (a b c)")

        FIRST, LAST = -2, C + 1
        LOOP = (3, C - 3)
        TURNS = (LOOP[1] - LOOP[0]) // 2
        assert HEAD - TURNS < C - 1 - LOOP[1]

        def run_bodies(eng, body):
            for i in range(FIRST, LOOP[0]):
                body(Step.of(i))
            with eng.Fori(LOOP[0] // 2, LOOP[1] // 2) as j:
                body(Step(j, 1))
                body(Step(j + 1, 0))
            for i in range(LOOP[1], LAST + 1):
                body(Step.of(i))

        def has(step):
            return not step.fixed or 0 <= step.index < C

        def sync_a(sp):
            for n, w in enumerate((Wq, Wk, Wv, Wo)):
                sp.dma_start(wraw[:, n], w.rearrange("(g p) d -> p g d", p=P)).then_inc(S["wraw_loaded"], 16)
            for g in range(GR):
                heads = slice(g * GH, (g + 1) * GH)
                sp.dma_start(wraw[:, 4, g, :], Wg[heads, :].unsqueeze(1).broadcast_to([GH, DH, D]))\
                  .then_inc(S["wraw_loaded"], 16)
                sp.dma_start(hbg[:, g:g + 1], bg[heads].unsqueeze(1).unsqueeze(2).broadcast_to([GH, DH, 1]))\
                  .then_inc(S["wraw_loaded"], 16)
            sp.dma_start(gw[:, :, :], gate_w.rearrange("(k p) e -> p k e", p=P)).then_inc(S["wraw_loaded"], 16)

            def body(i):
                a0, a3 = i + 2, i + -1
                if has(a0):
                    due(sp, S["xn_ready"], B, a0 + -2, B)
                    sp.dma_start(x_in[a0.side][:, :, :], x_by_step[a0.index]).then_inc(x_loaded[a0.side], 16)
                if has(a3):
                    due(sp, S["x1_ready"], 1, a3 + -2, 1)
                    sp.dma_start(x_res[a3.side][:, :, :], x_by_step[a3.index]).then_inc(xr_loaded[a3.side], 16)
                    due(sp, S["x1_ready"], 1, a3, 1)
                    sp.dma_start(x1_by_step[a3.index], x1[a3.side][:, :, :]).then_inc(x1_stored[a3.side], 16)
                    due(sp, S["xn2_ready"], B, a3, B)
                    sp.dma_start(xs_by_step[a3.index], xn2[a3.side][:, :, :]).then_inc(xs_stored[a3.side], 16)
            run_bodies(sp, body)

        def load_experts(act, first, end):
            for e in range(first, end):
                src = (ew1[e - 1], ew2[e - 1], ew3[e - 1]) if e else (sw1, sw2, sw3)
                for m in range(3):
                    act.dma_start(W[:, e, m, :].rearrange("p (c n) -> p c n", c=KC if m < 2 else HC),
                                  src[m].rearrange("(c p) n -> p c n", p=P)).then_inc(s_w[int(e >= HEAD)], 16)

        def scalar_a(act):
            act.wait_ge(S["wraw_loaded"], 16 * (5 + 2 * GR))
            load_experts(act, 0, HEAD)
            act.wait_ge(S["wT_done"], 5)
            for n in range(5):
                act.activation(free2(wT[:, n]), bank[n][:, :], ACT.Copy, scale=SCALE if n == 0 else 1.0)\
                   .then_inc(S["wT_ready"], 1)

            def feature(i, src, done, r_ready, e_ready, used, dst):
                due(act, S[done], 1, i, 1)
                due(act, S["ek_ready" if done == "q_done" else "eq_ready"], 1,
                    i + -1 if done == "q_done" else i, 1)
                act.activation(rneg[:, :], src[:, :], ACT.Relu, scale=-1.0).then_inc(S[r_ready], 1)
                due(act, S[r_ready], 1, i, 1)
                due(act, S[used], 1, i + -1, 1)
                act.activation(dst[:, :], rneg[:, :], ACT.Exp, scale=-1.0).then_inc(S[e_ready], 1)

            def body(i):
                a1, a2, a3 = i + 1, i, i + -1
                if has(a1):
                    due(act, S["xT_done"], 1, a1, 1)
                    due(act, S["v_done"], 1, a1 + -2, 1)
                    act.activation(free2(xnT[a1.side][:, :, :]), X1[:, :], ACT.Copy).then_inc(S["xnT_ready"], 1)
                    feature(a1, X0, "q_done", "rq_ready", "eq_ready", "qT_ready", ef[0])
                    feature(a1, X1, "k_done", "rk_ready", "ek_ready", "kT_ready", ef[1])
                    due(act, S["g_done"], 1, a1, 1)
                    due(act, S["gT_ready"], 1, a1 + -1, 1)
                    for g in range(GR):
                        act.activation(eg[:, g].rearrange("p b t -> p (b t)"), X0[:, g * B * P:(g + 1) * B * P],
                                       ACT.Tanh, bias=hbg[:, g:g + 1], scale=0.5).then_inc(S["eg_ready"], 1)
                if has(a3):
                    due(act, S["xn2T_done"], 1, a3, 1)
                    due(act, S["gate_done"], 1, a3 + -1, 1)
                    act.activation(free2(xn2T[:, :, :]), X1[:, :], ACT.Copy).then_inc(S["xn2T_ready"], 1)
                if has(a1):
                    due(act, S["v_done"], 1, a1, 1)
                    due(act, S["U_done"], 1, a1 + -2, 1)
                    for b in range(B):
                        act.activation(vp[a1.side][:, b, :, DH:2 * DH],
                                       X0[:, b * D:(b + 1) * D].rearrange("p (h j) -> p h j", j=DH), ACT.Copy)\
                           .then_inc(S["v_ready"], 1)
                    due(act, S["gT_ready"], 1, a1, 1)
                    due(act, S["gpool"], 4, a1 + -1, 1)
                    act.activation(free3(ghi[:, :, :, :]), free3(gT[:, :, :, :]), ACT.Copy)\
                       .then_inc(S["ghi_ready"], 1)
                if has(a3):
                    due(act, S["top_ready"], 1, a3, 1)
                    due(act, S["wts_ready"], 1, a3 + -1, 1)
                    act.activation(ew[:, :], dv[:, :], ACT.Exp).then_inc(S["ew_ready"], 1)
                if has(a2):
                    due(act, S["PV_done"], NS, a2, NS)
                    due(act, S["o_done"], 1, a2 + -2, 1)
                    act.activation(free3(yT[a2.side][:, :, :, :]), pY[:, :], ACT.Copy).then_inc(S["yT_ready"], 1)
                if a2.fixed and a2.index == C - 1:
                    for m in range(3):
                        act.wait_ge(w_scaled, m + 1)
                        act.activation(W16[:, 0, m, 0, :], wtmp_b[m % 2], ACT.Copy).then_inc(w_high, 1)
            run_bodies(act, body)
            act.wait_ge(S["U_done"], C)
            act.wait_ge(S["state_ready"], C * GR * B)
            load_experts(act, HEAD, NE)

        def pool_a(pool):
            made = [0]

            def link(ins):
                made[0] += 1
                ins.then_inc(s_init, 1)
                pool.wait_ge(s_init, made[0])

            link(pool.memset(ident[:, :], 0.0))
            link(pool.affine_select(out=ident[:, :], in_=ident[:, :], compare_op=ALU.not_equal, fill=1.0,
                                    base=0, pattern=[[-1, P]], channel_multiplier=1))
            link(pool.memset(ones[:, :], 1.0))
            link(pool.memset(half_neg[:, :], -0.5))
            link(pool.memset(diag4[:, :, :], 0.0))
            link(pool.affine_select(out=diag4[:, :, :], in_=diag4[:, :, :], compare_op=ALU.not_equal, fill=1.0,
                                    base=0, pattern=[[0, SETH], [-1, P]], channel_multiplier=1))
            link(pool.affine_select(out=later[:, :], in_=ones[:, :], compare_op=ALU.is_gt, fill=0.0,
                                    base=0, pattern=[[1, P]], channel_multiplier=-1))
            link(pool.memset(sel[:, :, :], 1.0))
            link(pool.affine_select(out=sel[:, :, :], in_=sel[:, :, :], compare_op=ALU.is_ge, fill=0.0,
                                    base=0, pattern=[[-DH, GH], [0, P]], channel_multiplier=1))
            link(pool.affine_select(out=sel[:, :, :], in_=sel[:, :, :], compare_op=ALU.is_ge, fill=0.0,
                                    base=2, pattern=[[DH, GH], [0, P]], channel_multiplier=-1))
            for dst, low in ((hmask[:, :], 0), (tmp8[:, 0], 1), (tmp8[:, 1], 2)):
                link(pool.memset(dst, 1.0))
                link(pool.affine_select(out=dst, in_=dst, compare_op=ALU.is_ge, fill=0.0,
                                        base=-low, pattern=[[-DH, GH]], channel_multiplier=1))
                link(pool.affine_select(out=dst, in_=dst, compare_op=ALU.is_ge, fill=0.0,
                                        base=DH - 1, pattern=[[DH, GH]], channel_multiplier=-1))
            link(pool.iota(iota8[:, :], pattern=[[1, E]], base=0, channel_multiplier=0,
                           allow_small_or_imprecise_dtypes=True))
            link(pool.iota(capoff[:, :], pattern=[[CAP, E]], base=0, channel_multiplier=0,
                           allow_small_or_imprecise_dtypes=True))
            link(pool.iota(rowid[:, :], pattern=[[0, 1]], base=0, channel_multiplier=1,
                           allow_small_or_imprecise_dtypes=True))
            link(pool.iota(tile_f[:, :], pattern=[[1, RT]], base=0, channel_multiplier=0,
                           allow_small_or_imprecise_dtypes=True))
            link(pool.memset(zrow[:, :], 0.0))
            assert made[0] == CONSTANTS

            def rstd(dst, mv, col, per, i, stats, ready, used):
                due(pool, S[stats], B, i, B)
                settle(pool)
                pool.tensor_scalar(ve[:, col, :], mv[:, :, 1], EPS, None, ALU.add).then_inc(S["pool_chain"], 1)
                due(pool, S["pool_chain"], 3, i, per)
                due(pool, S[used], B, i + -1, B)
                pool.tensor_tensor(dst[:, :], ve[:, col, :], half_neg[:, 0:B], ALU.pow).then_inc(S[ready], 1)

            def block_diagonal(i, b):
                due(pool, S["qT_ready"], 1, i, 1)
                due(pool, S["A_done"], NS, i + -1, (b + 1) * NS // B)
                for g in range(GR):
                    pool.tensor_tensor(qbd[:, b, g], qT[i.side][:, g, b].unsqueeze(1).broadcast_to([P, GH, P]),
                                       hmask[:, :].unsqueeze(2).broadcast_to([P, GH, P]), ALU.mult)\
                        .then_inc(S["qbd_ready"], 1)

            pool.wait_ge(s_vinit, 5)

            def body(i):
                a0, a1, a3, a4 = i + 2, i + 1, i + -1, i + -2

                def rstd1():
                    due(pool, S["xn_stats"], B, a0, B)
                    settle(pool)
                    pool.tensor_scalar(ve[:, 0, :], mv1[a0.side][:, :, 1], EPS, None, ALU.add)\
                        .then_inc(S["rstd1_ready"], 1)
                    due(pool, S["rstd1_ready"], 2, a0, 1)
                    due(pool, S["xn_ready"], B, a0 + -2, B)
                    pool.tensor_tensor(rs1[a0.side][:, :], ve[:, 0, :], half_neg[:, 0:B], ALU.pow)\
                        .then_inc(S["rstd1_ready"], 1)

                if has(a3):
                    due(pool, S["o_stats"], B, a3, B)
                    settle(pool)
                    pool.tensor_scalar(ve[:, 1, :], mvo[:, :, 1], EPS, None, ALU.add).then_inc(S["rstdo_ready"], 1)
                    due(pool, S["rstdo_ready"], 2, a3, 1)
                    due(pool, S["ln_ready"], B, a3 + -1, B)
                    pool.tensor_tensor(rso[:, :], ve[:, 1, :], half_neg[:, 0:B], ALU.pow)\
                        .then_inc(S["rstdo_ready"], 1)
                if has(a0):
                    rstd1()
                if has(a3):
                    due(pool, S["ln_ready"], B, a3, B)
                    due_dma(pool, xr_loaded, a3)
                    due_dma(pool, x1_stored, a3 + -2)
                    due(pool, S["xn2_ready"], B, a3 + -2, B)
                    pool.tensor_tensor(free2(x1[a3.side][:, :, :]), free2(ln_o[:, :, :]),
                                       free2(x_res[a3.side][:, :, :]), ALU.add).then_inc(S["x1_ready"], 1)
                    due(pool, S["x1_stats"], B, a3, B)
                    settle(pool)
                    pool.tensor_scalar(ve[:, 2, :], mv2[:, :, 1], EPS, None, ALU.add).then_inc(S["rstd2_ready"], 1)
                    due(pool, S["rstd2_ready"], 2, a3, 1)
                    due(pool, S["xn2_ready"], B, a3 + -1, B)
                    pool.tensor_tensor(rs2[:, :], ve[:, 2, :], half_neg[:, 0:B], ALU.pow)\
                        .then_inc(S["rstd2_ready"], 1)
                if has(a4):
                    due(pool, S["pos_ready"], 1, a4, 1)
                    due(pool, S["xn2_ready"], B, a4, B)
                    for b in range(B):
                        for k in range(TOPK):
                            settle(pool)
                            pool.indirect_dma_start(
                                xs_d[:, :], bass.IndirectOffsetOnAxis(
                                    ap=posi[a4.side][:, b * TOPK + k:b * TOPK + k + 1], axis=0),
                                xn2[a4.side][:, b, :], None).then_inc(scattered[a4.side], 16)
                if has(a1):
                    block_diagonal(a1, 0)
                    due(pool, S["ghi_ready"], 1, a1, 1)
                    settle(pool)
                    pool.tensor_scalar(free3(gt1[:, :, :, :]), free3(ghi[:, :, :, :]), part_mask[:, 0:1], None,
                                       ALU.mult).then_inc(S["gpool"], 1)
                    due(pool, S["gpool"], 4, a1, 1)
                    pool.tensor_tensor(free3(gr1[:, :, :, :]), free3(gT[:, :, :, :]), free3(gt1[:, :, :, :]),
                                       ALU.subtract).then_inc(S["gpool"], 1)
                    due(pool, S["gpool"], 4, a1, 2)
                    due(pool, S["gbc_done"], NS, a1 + -2, NS)
                    gp = gparts[a1.side]
                    settle(pool)
                    pool.tensor_copy(gp[:, :, :, 1:P].rearrange("p g b t -> p (g b) t"),
                                     gr1[:, :, :, 1:P].rearrange("p g b t -> p (g b) t")).then_inc(S["gpool"], 1)
                    due(pool, S["gpool"], 4, a1, 3)
                    settle(pool)
                    pool.tensor_scalar(gt1[:, :, :, 1:P].rearrange("p g b t -> p (g b) t"),
                                       gp[:, :, :, 1:P].rearrange("p g b t -> p (g b) t"), part_mask[:, 1:2], None,
                                       ALU.mult).then_inc(S["gpool"], 1)
                    due(pool, S["gpool"], 4, a1, 4)
                    pool.tensor_tensor(gp[:, :, :, 1:P].rearrange("p g b t -> p (g b) t"),
                                       gr1[:, :, :, 1:P].rearrange("p g b t -> p (g b) t"),
                                       gt1[:, :, :, 1:P].rearrange("p g b t -> p (g b) t"), ALU.subtract)\
                        .then_inc(S["gparts_ready"], 1)
                    due(pool, S["gam_ready"], GR * B, a1, GR * B)
                    due(pool, S["PV_done"], NS, a1 + -2, NS)
                    pool.tensor_tensor(free3(qg[a1.side][:, :, :, :]), free3(qT[a1.side][:, :, :, :]),
                                       free3(gam[a1.side][:, :, :, :]), ALU.mult).then_inc(S["qg_ready"], 1)
                    block_diagonal(a1, 1)
                if i.fixed and i.index == C - 1:
                    pool.wait_ge(s_wmax, 1)
                    pool.partition_all_reduce(wmax[:, 1, 0:HEAD], wmax[:, 0, 0:HEAD], P, RMAX).then_inc(s_wall, 1)
            run_bodies(pool, body)
            pool.wait_ge(s_pad, 1)
            for e in range(E):
                settle(pool)
                pool.indirect_dma_start(xs_d[:, :], bass.IndirectOffsetOnAxis(ap=pad_row[:, e:e + 1], axis=0),
                                        zrow[:, :], None).then_inc(s_padded, 16)

        def tensor_a(pe):
            mm = nc.tensor.matmul
            pe.wait_ge(s_init, CONSTANTS)
            pe.wait_ge(S["wraw_loaded"], 16 * (5 + 2 * GR))
            for n in range(5):
                for k in range(KC):
                    for g in range(GR):
                        last = nc.tensor.transpose(bank[n][:, k * D + g * P:k * D + (g + 1) * P],
                                                   wraw[:, n, g, k * P:(k + 1) * P], ident[:, :])
                last.then_inc(S["wT_done"], 1)
            pe.wait_ge(S["wT_ready"], 5)
            pe.wait_ge(s_vinit, 5)

            def project(i, n, dst, done):
                for g in range(GR):
                    for k in range(KC):
                        last = mm(dst[:, g * B * P:(g + 1) * B * P], wT[:, n, k, g * P:(g + 1) * P],
                                  xnT[i.side][:, k, :], start=(k == 0), stop=(k == KC - 1))
                last.then_inc(S[done], 1)

            def where(s):
                return s * B // NS, (s % (NS // B)) // (NS // B // GR), s % (GH // SETH)

            def scores(i, s):
                b, g, q = where(s)
                due(pe, S["gparts_ready"], 1, i, 1)
                due(pe, S["decay_ready"], NS, i, s - 1)
                for h in range(SETH):
                    last = mm(pG[s % 2][:, h * P:(h + 1) * P], sel[:, q * SETH + h, :], gparts[i.side][:, g, b, :],
                              start=True, stop=True)
                last.then_inc(S["gbc_done"], 1)
                due(pe, S["kT_ready"], 1, i, 1)
                due(pe, S["qbd_ready"], GR * B, i, b * GR + g + 1)
                due(pe, S["probs_ready"], NS, i, s - 1)
                mm(pA[s % 2][:, :], kT[i.side][:, g, b, :],
                   qbd[:, b, g, q * SETH:(q + 1) * SETH, :].rearrange("p h t -> p (h t)"),
                   start=True, stop=True).then_inc(S["A_done"], 1)

            def attend(i, s):
                b, g, q = where(s)
                col = (b * GR + g) * P
                if s == 0:
                    due(pe, S["yT_ready"], 1, i + -1, 1)
                    due(pe, S["qg_ready"], 1, i, 1)
                    due(pe, S["state_ready"], GR * B, i + -1, GR * B)
                    due(pe, S["v_ready"], B, i, B)
                if q == 0:
                    mm(pY[:, col:col + P], state[:, b, g, :], qg[i.side][:, g, b, :], start=True, stop=False,
                       skip_group_check=True)
                due(pe, S["probs_ready"], NS, i, s + 1)
                for h in range(SETH):
                    head = q * SETH + h
                    r = head // 2 * 2 * DH
                    lo = DH if head % 2 == 0 else 0
                    last = mm(pY[r:r + 2 * DH, col:col + P],
                              vp[i.side][:, b, g * GH + head, lo:lo + 2 * DH], probs[s % 2][:, h, :],
                              start=False, stop=(head % 2 == 1), skip_group_check=True)
                last.then_inc(S["PV_done"], 1)

            def body(i):
                a1, a2, a3 = i + 1, i, i + -1
                A1, A2, A3 = has(a1), has(a2), has(a3)
                if A3:
                    due(pe, S["yT_ready"], 1, a3, 1)
                    if A2:
                        due(pe, S["v_ready"], B, a2, B)
                    due(pe, S["ln_ready"], B, a3 + -1, B)
                    for b in range(B):
                        for g in range(GR):
                            last = mm(X0[:, b * D:(b + 1) * D], yT[a3.side][:, b, g, :], wT[:, 3, g, :],
                                      start=(g == 0), stop=(g == GR - 1))
                    last.then_inc(S["o_done"], 1)
                if A2:
                    due(pe, S["kT_ready"], 1, a2, 1)
                    due(pe, S["um_ready"], 1, a2 + -1, 1)
                    for b in range(B):
                        for g in range(GR):
                            last = nc.tensor.transpose(pU[:, (b * GR + g) * P:(b * GR + g + 1) * P],
                                                       kT[a2.side][:, g, b, :], ident[:, :])
                    last.then_inc(S["ktok_done"], 1)
                    scores(a2, 0)
                    scores(a2, 1)
                if A1:
                    due(pe, S["xn_ready"], B, a1, B)
                    due(pe, S["pos_ready"], 1, a1 + -3, 1)
                    for k in range(KC):
                        for b in range(B):
                            last = nc.tensor.transpose(X1[:, (k * B + b) * P:(k * B + b + 1) * P],
                                                       xn[:, b, k * P:(k + 1) * P], ident[:, :])
                    last.then_inc(S["xT_done"], 1)
                if A2:
                    attend(a2, 0)
                    scores(a2, 2)
                if A1:
                    due(pe, S["xnT_ready"], 1, a1, 1)
                    due(pe, S["ln_ready"], B, a1 + -2, B)
                    if not A3 and a1.index > 0:
                        due(pe, S["v_ready"], B, a1 + -1, B)
                    project(a1, 0, X0, "q_done")
                if A2:
                    attend(a2, 1)
                    scores(a2, 3)
                if A1:
                    project(a1, 1, X1, "k_done")
                if A2:
                    attend(a2, 2)
                    scores(a2, 4)
                if A1:
                    due(pe, S["qT_ready"], 1, a1, 1)
                    project(a1, 4, X0, "g_done")
                if A2:
                    attend(a2, 3)
                    scores(a2, 5)
                if A3:
                    due(pe, S["xn2_ready"], B, a3, B)
                    if A1:
                        due(pe, S["kT_ready"], 1, a1, 1)
                    due(pe, S["pos_ready"], 1, a3 + -1, 1)
                    for k in range(KC):
                        for b in range(B):
                            last = nc.tensor.transpose(X1[:, (k * B + b) * P:(k * B + b + 1) * P],
                                                       xn2[a3.side][:, b, k * P:(k + 1) * P], ident[:, :])
                    last.then_inc(S["xn2T_done"], 1)
                if A1:
                    due(pe, S["eg_ready"], GR, a1, GR)
                    for b in range(B):
                        for k in range(KC):
                            last = mm(X0[:, b * D:(b + 1) * D], xnT[a1.side][:, k, b * P:(b + 1) * P], wT[:, 2, k, :],
                                      start=(k == 0), stop=(k == KC - 1))
                    last.then_inc(S["v_done"], 1)
                if A2:
                    attend(a2, 4)
                    scores(a2, 6)
                if A3:
                    due(pe, S["xn2T_ready"], 1, a3, 1)
                    if A1:
                        due(pe, S["kT_ready"], 1, a1, 1)
                    for b in range(B):
                        for k in range(KC):
                            last = mm(X1[:, b * E:(b + 1) * E], xn2T[:, k, b * P:(b + 1) * P], gw[:, k, :],
                                      start=(k == 0), stop=(k == KC - 1))
                    last.then_inc(S["gate_done"], 1)
                if A2:
                    attend(a2, 5)
                    scores(a2, 7)
                    attend(a2, 6)
                    attend(a2, 7)
                    due(pe, S["kd_ready"], NS, a2, NS)
                    for b in range(B):
                        for g in range(GR):
                            last = mm(pU[:, (b * GR + g) * P:(b * GR + g + 1) * P], kd[:, b, g, :],
                                      vp[a2.side][:, b, g * GH:(g + 1) * GH, DH:2 * DH], start=True, stop=True)
                    last.then_inc(S["U_done"], 1)
                if A3:
                    due(pe, S["chosen_ready"], B, a3, B)
                    due(pe, S["csum_ready"], 2, a3 + -1, 2)
                    for b in range(B):
                        r = X1[:, (B + b) * E:(B + b + 1) * E]
                        mm(r, later[:, :], chosen[:, b, :], start=True, stop=False)
                        for before in range(b):
                            mm(r, ones[:, :], chosen[:, before, :], start=False, stop=False)
                        last = mm(r, ones[:, :], csum[:, :], start=False, stop=True)
                    last.then_inc(S["prefix_done"], 1)
            run_bodies(pe, body)
            pe.wait_ge(S["csum_ready"], 2 * C)
            pe.wait_ge(S["pos_ready"], C)
            mm(X1[:, 0:E], ones[:, :], csum[:, :], start=True, stop=True).then_inc(s_total, 1)

        def scales(link, dve, first, end):
            V = nc.vector
            dve.wait_ge(s_wall, 1 + int(first > 0))
            at = slice(first, end)
            link(V.tensor_scalar(wmax[:, 0, at], wmax[:, 1, at], 1e-30, None, ALU.max))
            link(V.tensor_scalar(wmax[:, 1, at].bitcast(I32), wmax[:, 0, at].bitcast(I32), 0x7F800000, None,
                                 ALU.bitwise_and))
            link(V.tensor_scalar(w_scale[:, 0, at], wmax[:, 1, at], 4.0, None, ALU.mult))
            link(V.reciprocal(w_scale[:, 1, at], w_scale[:, 0, at]))
            link(V.tensor_tensor(w_scale[:, 2, at], w_scale[:, 0, at], w_scale[:, 0, at], ALU.mult))
            V.tensor_tensor(w_scale[:, 2, at], w_scale[:, 2, at], w_scale[:, 0, at], ALU.mult).then_inc(s_scale, 1)

        def vector_a(dve):
            V = nc.vector
            V.memset(zeros[:, :], 0.0).then_inc(s_vinit, 1)
            V.memset(state[:, :, :, :], 0.0).then_inc(s_vinit, 1)
            V.memset(csum[:, :], 0.0).then_inc(s_vinit, 1)
            for n in range(2):
                V.memset(vp[n][:, :, :, :], 0.0)
                V.memset(gparts[n][:, :, :, :], 0.0)
            dve.wait_ge(s_init, CONSTANTS)
            V.tensor_reduce(part_mask[:, :], tmp8[:, :, :], AX_X, ALU.add).then_inc(s_vinit, 1)
            dve.wait_ge(S["wraw_loaded"], 16 * (5 + 2 * GR))
            V.tensor_scalar(hbg[:, :], hbg[:, :], 0.5, None, ALU.mult).then_inc(s_vinit, 1)
            dve.wait_ge(s_vinit, 5)

            def where(s):
                return s * B // NS, (s % (NS // B)) // (NS // B // GR), s % (GH // SETH)

            chains = {n: sem(f"dve_{n}_chain") for n in ("s1", "so", "s2", "S", "top", "wt", "pos")}

            def stat(i, key, src, st, mv, ready):
                for b in range(B):
                    V.bn_stats(st[:, b, :], src[b]).then_inc(chains[key], 1)
                for b in range(B):
                    due(dve, chains[key], B, i, b + 1)
                    settle(dve)
                    V.bn_aggr(mv[:, b, :], st[:, b, :]).then_inc(S[ready], 1)

            def normalise(dst, src, mv, rs, ready):
                for b in range(B):
                    V.tensor_scalar(dst[:, b, :], src[b], mv[:, b, 0:1], rs[:, b:b + 1], ALU.subtract, ALU.mult)\
                     .then_inc(S[ready], 1)

            def scan(i, s):
                due(dve, S["gbc_done"], NS, i, s + 1)
                due(dve, S["kd_ready"], NS, i, s - 1)
                V.tensor_tensor_scan(free2(decay[s % 2][:, :, :]), pG[s % 2][:, :], free2(diag4[:, :, :]), 0.0,
                                     ALU.mult, ALU.add).then_inc(S["decay_ready"], 1)

            def weigh(i, s):
                b, g, q = where(s)
                due(dve, S["decay_ready"], NS, i, s + 1)
                due(dve, S["A_done"], NS, i, s + 1)
                due(dve, S["PV_done"], NS, i, s - 1)
                V.tensor_tensor(free2(probs[s % 2][:, :, :]), pA[s % 2][:, :], free2(decay[s % 2][:, :, :]), ALU.mult)\
                 .then_inc(S["probs_ready"], 1)
                if s == 0:
                    due(dve, S["ktok_done"], 1, i, 1)
                    due(dve, S["U_done"], 1, i + -1, 1)
                hs = slice(q * SETH * DH, (q + 1) * SETH * DH)
                V.tensor_tensor(kd[:, b, g, hs].rearrange("p (h d) -> p h d", d=DH),
                                pU[:, (b * GR + g) * P:(b * GR + g + 1) * P][:, hs].rearrange("p (h d) -> p h d", d=DH),
                                decay[s % 2][:, :, P - 1:P].broadcast_to([P, SETH, DH]), ALU.mult)\
                 .then_inc(S["kd_ready"], 1)

            def feature(i, src, ready, e_ready, dst, e):
                due(dve, S[e_ready], 1, i, 1)
                V.scalar_tensor_tensor(free3(dst[i.side][:, :, :, :]), src[:, :], 1.0, e[:, :], ALU.add, ALU.max)\
                 .then_inc(S[ready], 1)

            def body(i):
                a1, a2, a3 = i + 1, i, i + -1
                a0 = i + 2
                A0, A1, A2, A3 = has(a0), has(a1), has(a2), has(a3)
                if i.fixed and i.index == C - 1:
                    largest_of_parts()
                if A3:
                    due(dve, S["o_done"], 1, a3, 1)
                    due(dve, S["rstdo_ready"], 2, a3 + -1, 1)
                    due(dve, S["ln_ready"], B, a3 + -1, B)
                    stat(a3, "so", [X0[:, b * D:(b + 1) * D] for b in range(B)], sto, mvo, "o_stats")
                    if a3.fixed and a3.index == C - 1:
                        low(0)
                        scaled(2)
                if A0:
                    due_dma(dve, x_loaded, a0)
                    due(dve, S["rstd1_ready"], 2, a0 + -2, 1)
                    due(dve, S["xn_ready"], B, a0 + -1, B)
                    stat(a0, "s1", [x_in[a0.side][:, b, :] for b in range(B)], st1, mv1[a0.side], "xn_stats")
                if A2:
                    scan(a2, 0)
                    scan(a2, 1)
                if A2:
                    weigh(a2, 0)
                if A3:
                    due(dve, S["rstdo_ready"], 2, a3, 2)
                    due(dve, S["x1_ready"], 1, a3 + -1, 1)
                    due(dve, S["o_stats"], B, a3, B)
                    normalise(ln_o, [X0[:, b * D:(b + 1) * D] for b in range(B)], mvo, rso, "ln_ready")
                    if a3.fixed and a3.index == C - 1:
                        low(1)
                if A2:
                    scan(a2, 2)
                    weigh(a2, 1)
                if A3:
                    due(dve, S["x1_ready"], 1, a3, 1)
                    due(dve, S["rstd2_ready"], 2, a3 + -1, 1)
                    due(dve, S["xn2_ready"], B, a3 + -1, B)
                    stat(a3, "s2", [x1[a3.side][:, b, :] for b in range(B)], st2, mv2, "x1_stats")
                    if a3.fixed and a3.index == C - 1:
                        low(2)
                if A2:
                    scan(a2, 3)
                    weigh(a2, 2)
                if A0:
                    due(dve, S["rstd1_ready"], 2, a0, 2)
                    due(dve, S["xn_stats"], B, a0, B)
                    due(dve, S["xT_done"], 1, a0 + -1, 1)
                    normalise(xn, [x_in[a0.side][:, b, :] for b in range(B)], mv1[a0.side], rs1[a0.side], "xn_ready")
                if A1:
                    due(dve, S["qbd_ready"], GR * B, a1 + -2, GR * B)
                    due(dve, S["qg_ready"], 1, a1 + -2, 1)
                    feature(a1, X0, "qT_ready", "eq_ready", qT, ef[0])
                if A3:
                    due(dve, S["rstd2_ready"], 2, a3, 2)
                    due(dve, S["x1_stats"], B, a3, B)
                    due_dma(dve, xs_stored, a3 + -2)
                    due_dma(dve, scattered, a3 + -2, B * TOPK)
                    due(dve, S["xn2T_done"], 1, a3 + -2, 1)
                    normalise(xn2[a3.side], [x1[a3.side][:, b, :] for b in range(B)], mv2, rs2, "xn2_ready")
                if A2:
                    scan(a2, 4)
                    weigh(a2, 3)
                if A1:
                    due(dve, S["A_done"], NS, a1 + -2, NS)
                    due(dve, S["ktok_done"], 1, a1 + -2, 1)
                    feature(a1, X1, "kT_ready", "ek_ready", kT, ef[1])
                if A2:
                    scan(a2, 5)
                    weigh(a2, 4)
                if A1:
                    due(dve, S["eg_ready"], GR, a1, GR)
                    due(dve, S["gpool"], 4, a1 + -1, 2)
                    due(dve, S["ghi_ready"], 1, a1 + -1, 1)
                    V.tensor_scalar(free3(gT[:, :, :, :]), free3(eg[:, :, :, :]), 0.5, 0.5, ALU.mult, ALU.add)\
                     .then_inc(S["gT_ready"], 1)
                    due(dve, S["gT_ready"], 1, a1, 1)
                if A2:
                    scan(a2, 6)
                    weigh(a2, 5)
                if A1:
                    due(dve, S["qg_ready"], 1, a1 + -2, 1)
                    for g in range(GR):
                        for b in range(B):
                            V.tensor_tensor_scan(gam[a1.side][:, g, b, :], gT[:, g, b, :], zeros[:, :], 1.0,
                                                 ALU.mult, ALU.add).then_inc(S["gam_ready"], 1)
                top = chains["top"]
                if A3:
                    due(dve, S["gate_done"], 1, a3, 1)
                    V.tensor_copy(free2(lg[:, :, :]), X1[:, 0:B * E]).then_inc(top, 1)
                if A2:
                    scan(a2, 7)
                if A3:
                    due(dve, top, 4 + 3 * B, a3, 1)
                    for b in range(B):
                        settle(dve)
                        V.max(mx[:, b, :], lg[:, b, :]).then_inc(top, 1)
                if A2:
                    weigh(a2, 6)
                if A3:
                    for b in range(B):
                        due(dve, top, 4 + 3 * B, a3, 2 + b)
                        settle(dve)
                        V.max_index(mi[:, b, :], mx[:, b, :], lg[:, b, :]).then_inc(top, 1)
                    due(dve, S["ew_ready"], 1, a3 + -1, 1)
                    V.tensor_tensor(dv[:, :], mx[:, :, 1], mx[:, :, 0], ALU.subtract).then_inc(S["top_ready"], 1)
                if A2:
                    weigh(a2, 7)
                if A3:
                    due(dve, top, 4 + 3 * B, a3, 1 + 2 * B)
                    V.tensor_copy(mif[:, :, :], mi[:, :, :]).then_inc(top, 1)
                    due(dve, top, 4 + 3 * B, a3, 2 + 2 * B)
                    due(dve, S["pos_ready"], 1, a3 + -1, 1)
                    for b in range(B):
                        for k in range(TOPK):
                            V.tensor_scalar(oh[:, b, k, :], iota8[:, :], mif[:, b, k:k + 1], None, ALU.is_equal)\
                             .then_inc(top, 1)
                    wt = chains["wt"]
                    due(dve, S["ew_ready"], 1, a3, 1)
                    V.tensor_scalar(wtmp[:, 0, :], ew[:, :], 1.0, None, ALU.add).then_inc(wt, 1)
                    due(dve, S["prefix_done"], 1, a3 + -1, 1)
                    due(dve, S["csum_ready"], 2, a3 + -1, 2)
                    for b in range(B):
                        due(dve, top, 4 + 3 * B, a3, 2 + 2 * B + TOPK * B)
                        V.tensor_tensor(chosen[:, b, :], oh[:, b, 0, :], oh[:, b, 1, :], ALU.add)\
                         .then_inc(S["chosen_ready"], 1)
                    due(dve, wt, 3, a3, 1)
                    V.reciprocal(wtmp[:, 1, :], wtmp[:, 0, :]).then_inc(wt, 1)
                if A2:
                    c = chains["S"]
                    due(dve, S["U_done"], 1, a2, 1)
                    due(dve, S["state_ready"], GR * B, a2 + -1, GR * B)
                    V.tensor_tensor(um[:, :, :, :].rearrange("p b g (h d) -> p (b g) h d", d=DH),
                                    pU[:, :].rearrange("p (a h d) -> p a h d", a=B * GR, d=DH),
                                    hmask[:, :].unsqueeze(1).unsqueeze(3).broadcast_to([P, B * GR, GH, DH]), ALU.mult)\
                     .then_inc(S["um_ready"], 1)
                    due(dve, S["um_ready"], 1, a2, 1)
                    due(dve, S["gam_ready"], GR * B, a2, GR * B)
                    for b in range(B):
                        for g in range(GR):
                            V.scalar_tensor_tensor(state[:, b, g, :], state[:, b, g, :],
                                                   gam[a2.side][:, g, b, P - 1:P], um[:, b, g, :],
                                                   ALU.mult, ALU.add).then_inc(S["state_ready"], 1)
                if A3:
                    due(dve, wt, 3, a3, 2)
                    V.tensor_copy(wts_all[:, bass.ds(a3.index, 1), :, 0], wtmp[:, 1, :].unsqueeze(1)).then_inc(wt, 1)
                    V.tensor_tensor(wts_all[:, bass.ds(a3.index, 1), :, 1], wtmp[:, 1, :].unsqueeze(1),
                                    ew[:, :].unsqueeze(1), ALU.mult).then_inc(S["wts_ready"], 1)
                if A3:
                    due(dve, S["prefix_done"], 1, a3, 1)
                    due(dve, S["chosen_ready"], B, a3, B)
                    c = chains["pos"]
                    N = 3 + B * TOPK
                    V.tensor_tensor(slot[:, :, :], X1[:, B * E:2 * B * E].rearrange("p (b e) -> p b e", e=E),
                                    capoff[:, :].unsqueeze(1).broadcast_to([P, B, E]), ALU.add).then_inc(c, 1)
                    V.tensor_tensor(csum[:, :], csum[:, :], chosen[:, 0, :], ALU.add).then_inc(S["csum_ready"], 1)
                    due(dve, S["csum_ready"], 2, a3, 1)
                    V.tensor_tensor(csum[:, :], csum[:, :], chosen[:, 1, :], ALU.add).then_inc(S["csum_ready"], 1)
                    due(dve, c, N, a3, 1)
                    for b in range(B):
                        for k in range(TOPK):
                            V.tensor_tensor_reduce(out=oh[:, b, k, :], in0=oh[:, b, k, :], in1=slot[:, b, :],
                                                   scale=1.0, scalar=0.0, op0=ALU.mult, op1=ALU.add,
                                                   accum_out=posf[:, b * TOPK + k:b * TOPK + k + 1]).then_inc(c, 1)
                    due(dve, c, N, a3, 1 + B * TOPK)
                    due_dma(dve, scattered, a3 + -2, B * TOPK)
                    V.tensor_copy(place_all[:, bass.ds(a3.index, 1), :], posf[:, :].unsqueeze(1)).then_inc(c, 1)
                    V.tensor_copy(choice_all[:, bass.ds(a3.index, 1), :].rearrange("p c (b k) -> p (c b) k", b=B),
                                  mif[:, :, 0:TOPK]).then_inc(c, 1)
                    V.tensor_copy(posi[a3.side][:, :], posf[:, :]).then_inc(S["pos_ready"], 1)
                if a2.fixed and a2.index == C - 1:
                    scales(link, dve, 0, HEAD)
                    dve.wait_ge(s_scale, 1)
                    dve.wait_ge(S["v_done"], C)
                    dve.wait_ge(S["kT_ready"], C)
                    scaled(0)
                    scaled(1)
                def largest_of(e, at):
                    V.tensor_reduce(wpart[:, e, at], W[:, e, at, :], AX_X, ALU.max, apply_absolute_value=True)\
                     .then_inc(s_wpart, 1)

                if not i.fixed:
                    largest_of(bass.ds(i.half - (LOOP[0] + 1 - i.side) // 2, 1), slice(0, 2) if i.side else slice(2, 3))
                elif i.index >= LOOP[1] and i.index - LOOP[1] + TURNS < HEAD:
                    largest_of(slice(i.index - LOOP[1] + TURNS, i.index - LOOP[1] + TURNS + 1), slice(0, 2))
                    largest_of(slice(i.index - LOOP[1] + TURNS, i.index - LOOP[1] + TURNS + 1), slice(2, 3))
                if i.fixed and i.index == LOOP[0] - 1:
                    dve.wait_ge(s_w[0], 16 * 3 * HEAD)

            n = [0]

            def link(ins):
                n[0] += 1
                ins.then_inc(dve_chain, 1)
                dve.wait_ge(dve_chain, n[0])

            def largest_of_parts():
                dve.wait_ge(s_wpart, 2 * HEAD)
                V.tensor_reduce(wmax[:, 0, 0:HEAD], wpart[:, :, :], AX_X, ALU.max).then_inc(s_wmax, 1)

            def scaled(m):
                if m >= 2:
                    dve.wait_ge(w_low, m - 1)
                V.tensor_scalar(wtmp_b[m % 2], W[:, 0, m, :], w_scale[:, 1, 0:1], None, ALU.mult)\
                 .then_inc(w_scaled, 1)

            def low(m):
                dve.wait_ge(w_high, m + 1)
                V.tensor_tensor(W16[:, 0, m, 1, :], wtmp_b[m % 2], W16[:, 0, m, 0, :], ALU.subtract)\
                 .then_inc(w_low, 1)

            run_bodies(dve, body)

            dve.wait_ge(s_total, 1)
            link(V.tensor_copy(total[:, :], X1[:, 0:E]))
            link(V.tensor_tensor(slot[:, 0, :], total[:, :], capoff[:, :], ALU.add))
            link(V.tensor_scalar(slot[:, 1, :], slot[:, 0, :], rowid[:, :], None, ALU.add))
            V.tensor_copy(pad_row[:, :], slot[:, 1, :]).then_inc(s_pad, 1)

        phase_a.close()

        phase_b = ExitStack()

        def sc(name, shape, dt=F32):
            return phase_b.enter_context(nc.sbuf_tensor(name, shape, dt))

        wtmp_p = sc("wtmp_p", [P, 3, MW])
        xt = [sc(f"xt{n}", [P, D]) for n in range(2)]
        xh = [sc(f"xh{n}", [P, KC, P], F16) for n in range(2)]
        xl = [sc(f"xl{n}", [P, KC, P], F16) for n in range(2)]
        sl = [sc(f"sl{n}", [P, H]) for n in range(2)]
        gg = [sc(f"gg{n}", [P, H]) for n in range(2)]
        gh = [sc(f"gh{n}", [P, HC, P], F16) for n in range(2)]
        gl = [sc(f"gl{n}", [P, HC, P], F16) for n in range(2)]
        yo = [sc(f"yo{n}", [P, D]) for n in range(2)]
        ysh = sc("ysh", [P, ST, D])
        gi = [sc(f"gi{n}", [P, B * TOPK], U32) for n in range(2)]
        ya = [[[sc(f"ya{n}_{b}{k}", [P, D]) for k in range(TOPK)] for b in range(B)] for n in range(2)]
        cmb = [sc(f"cmb{n}", [P, B, D]) for n in range(2)]
        lnc = [sc(f"lnc{n}", [P, B, D]) for n in range(2)]
        x1c = W[:, 1:NE].rearrange("p e m n -> p (e m n)")[:, 0:B * C * D].rearrange(
            "p (b c d) -> p b c d", b=B, c=C)
        stc = [sc(f"stc{n}", [P, B, 6]) for n in range(2)]
        mvc = [sc(f"mvc{n}", [P, B, 2]) for n in range(2)]
        vec = [sc(f"vec{n}", [P, B]) for n in range(2)]
        rsc = [sc(f"rsc{n}", [P, B]) for n in range(2)]
        shiftc = [sc(f"shiftc{n}", [P, B]) for n in range(2)]

        pT, pH1, pH2, pGT, pYB = bank[0], bank[1:3], bank[3:5], bank[5], bank[6:8]
        namesB = ("late_chain pool_split experts_split xtT_done xh_ready xl_ready h1_done h2_done"
                  " silu_ready gg_ready ggT_done gh_ready gl_ready y_done yo_ready").split()
        T = {n: sem("b_" + n) for n in namesB}
        xt_loaded = [sem(f"xt_loaded{n}") for n in range(2)]
        yo_stored = [sem(f"yo_stored{n}") for n in range(2)]
        namesC = "gi_ready mix1 mix2 stat1 stats_ready vare rstd_ready shift_ready lnc_ready oc_ready".split()
        U = {n: sem("c_" + n) for n in namesC}
        x1_loaded = [sem(f"x1_loaded{n}") for n in range(2)]
        ya_loaded = [sem(f"ya_loaded{n}") for n in range(2)]
        out_stored = sem("out_stored")

        MIX0 = RT + C + 3
        ENDS = MIX0 + C + 4

        def run_tiles(eng, body):
            def turns(first, end, kind):
                with eng.Fori(first, end) as j:
                    body(Step(j, 0, kind))
                    body(Step(j, 1, kind))

            def peeled(first, end):
                for t in range(first, end):
                    body(Step.of(t))

            peeled(-2, EARLY + 4)
            turns(EARLY // 2 + 2, T0 // 2 - 1, "routed")
            peeled(T0 - 2, T0 + 2)
            turns(T0 // 2 + 1, MIX0 // 2, "late")
            peeled(MIX0 // 2 * 2, MIX0 // 2 * 2 + 6)
            turns(MIX0 // 2 + 3, NT // 2 - 1, "mixed")
            peeled(NT - 2, ENDS)

        def is_tile(t):
            return not t.fixed or 0 <= t.index < NT

        def is_routed(t):
            return EARLY <= t.index < T0 if t.fixed else t.kind == "routed"

        def chunk(t):
            early = t.index < EARLY if t.fixed else t.kind == "early"
            return t.index if early else t.index - RT

        def is_step(c):
            return 0 <= c.index < C if c.fixed else c.kind == "mixed"

        def entry(eng, row, t, most):
            return eng.value_load(tab[0:1, row, bass.ds(t.index - EARLY, 1)], min_val=0, max_val=most)

        def expert_of(eng, t):
            if not is_routed(t):
                return bass.ds(0, 1)
            if t.fixed and t.index == EARLY:
                eng.wait_ge(s_tab, 1)
            return bass.ds(entry(eng, 0, t, E), 1)

        def sync_b(sp):
            for n in range(2):
                sp.wait_ge(xs_stored[n], 16 * C // 2)

            def body(t):
                if is_tile(t + 2):
                    u = t + 2
                    if is_routed(u):
                        if u.fixed and u.index == EARLY:
                            for n in range(2):
                                sp.wait_ge(scattered[n], 16 * B * TOPK * C // 2)
                            sp.wait_ge(s_padded, 16 * E)
                            sp.wait_ge(s_tab, 1)
                        e, row = entry(sp, 0, u, E), entry(sp, 1, u, SHARED - P)
                        sp.wait_ge(T["experts_split"], e)
                        settle(sp)
                    else:
                        row = chunk(u) * P + SHARED
                    due(sp, T["xtT_done"], 1, t, 1)
                    sp.dma_start(xt[t.side][:, :], xs_d[bass.ds(row, P), :]).then_inc(xt_loaded[t.side], 16)
                u = t + -2
                if is_tile(u) and is_routed(u):
                    due(sp, T["yo_ready"], 1, u, 1)
                    sp.dma_start(ys_d[bass.ds((u.index - EARLY) * P, P), :], yo[u.side][:, :])\
                      .then_inc(yo_stored[u.side], 16)
                c = t + -(MIX0 + 1)
                if c.fixed and c.index == 0:
                    sp.wait_ge(T["yo_ready"], T0)
                    for n in range(2):
                        sp.wait_ge(x1_stored[n], 16 * C // 2)
                if is_step(c) or is_step(c + -2):
                    due(sp, U["oc_ready"], 1, c + -2, 1)
                if is_step(c):
                    sp.dma_start(x1c[:, :, bass.ds(c.index, 1), :].rearrange("p b c d -> p (b c) d"),
                                 x1_by_step[c.index]).then_inc(x1_loaded[c.side], 16)
                if is_step(c + -2):
                    u = c + -2
                    sp.dma_start(out.rearrange("b (c p) d -> c p b d", p=P)[u.index],
                                 x1c[:, :, bass.ds(u.index, 1), :].rearrange("p b c d -> p (b c) d"))\
                      .then_inc(out_stored, 16)
            run_tiles(sp, body)
            sp.wait_ge(out_stored, 16 * C)

        def tensor_b(pe):
            mm = nc.tensor.matmul
            pe.wait_ge(w_low, 3)

            def turn_x(t):
                due_dma(pe, xt_loaded, t)
                for k in range(KC):
                    last = nc.tensor.transpose(pT[:, k * P:(k + 1) * P], xt[t.side][:, k * P:(k + 1) * P], ident[:, :])
                last.then_inc(T["xtT_done"], 1)

            def turn_g(t):
                due(pe, T["gg_ready"], 1, t, 1)
                for c in range(HC):
                    last = nc.tensor.transpose(pGT[:, c * P:(c + 1) * P], gg[t.side][:, c * P:(c + 1) * P], ident[:, :])
                last.then_inc(T["ggT_done"], 1)

            def hidden(t, e, m, dst, done, between=None):
                n = 0
                for k in range(KC):
                    if k == 1 and between is not None:
                        between()
                    for a, s in ((xh, 0), (xh, 1), (xl, 0)):
                        last = mm(dst[t.side][:, :], a[t.side][:, k, :],
                                  W16[:, e, m, s, k * H:(k + 1) * H], start=(n == 0), stop=(n == 3 * KC - 1))
                        n += 1
                last.then_inc(T[done], 1)

            def project(t, e):
                due(pe, T["gl_ready"], 1, t, 1)
                n = 0
                for c in range(HC):
                    for a, s in ((gh, 0), (gh, 1), (gl, 0)):
                        last = mm(pYB[t.side][:, 0:D], a[t.side][:, c, :],
                                  W16[:, e, 2, s, c * D:(c + 1) * D], start=(n == 0), stop=(n == 3 * HC - 1))
                        n += 1
                last.then_inc(T["y_done"], 1)

            def transposes(t):
                due(pe, T["yo_ready"], 1, t + -4, 1)
                if is_tile(t + -1):
                    turn_g(t + -1)
                if is_tile(t + 1):
                    turn_x(t + 1)

            def body(t):
                if t.fixed and t.index > NT + 1:
                    return
                if is_tile(t):
                    e = expert_of(pe, t)
                if is_tile(t + -2):
                    e_before = expert_of(pe, t + -2)
                if is_tile(t):
                    due(pe, T["xl_ready"], 1, t, 1)
                    hidden(t, e, 0, pH1, "h1_done", between=lambda: transposes(t))
                else:
                    transposes(t)
                if is_tile(t):
                    hidden(t, e, 1, pH2, "h2_done")
                if is_tile(t + -2):
                    project(t + -2, e_before)
            run_tiles(pe, body)

        def scalar_b(act):
            def body(t):
                if is_tile(t + -1):
                    u = t + -1
                    due(act, T["ggT_done"], 1, u, 1)
                    due(act, T["y_done"], 1, u + -2, 1)
                    act.activation(gh[u.side][:, :, :].rearrange("p c t -> p (c t)"), pGT[:, :], ACT.Copy)\
                       .then_inc(T["gh_ready"], 1)
                if is_tile(t + 1):
                    u = t + 1
                    due(act, T["xtT_done"], 1, u, 1)
                    due(act, T["h2_done"], 1, u + -2, 1)
                    act.activation(xh[u.side][:, :, :].rearrange("p k t -> p (k t)"), pT[:, 0:D], ACT.Copy)\
                       .then_inc(T["xh_ready"], 1)
                if is_tile(t):
                    e = expert_of(act, t)
                    due(act, T["h1_done"], 1, t, 1)
                    due(act, T["gg_ready"], 1, t + -2, 1)
                    act.activation(sl[t.side][:, :], pH1[t.side][:, :], ACT.Silu, scale=w_scale[:, 0, e])\
                       .then_inc(T["silu_ready"], 1)
                c = t + -(MIX0 + 1)
                if is_step(c):
                    due(act, U["shift_ready"], 1, c, 1)
                    due(act, U["oc_ready"], 1, c + -2, 1)
                    for b in range(B):
                        act.activation(lnc[c.side][:, b, :], cmb[c.side][:, b, :], ACT.Identity,
                                       bias=shiftc[c.side][:, b:b + 1], scale=rsc[c.side][:, b:b + 1])\
                           .then_inc(U["lnc_ready"], 1)
                if is_tile(t + -2):
                    u = t + -2
                    e = expert_of(act, u)
                    due(act, T["y_done"], 1, u, 1)
                    if is_routed(u):
                        due_dma(act, yo_stored, u + -(EARLY + 2))
                        dst = yo[u.side][:, :]
                    else:
                        dst = ysh[:, bass.ds(chunk(u), 1), :].rearrange("p a d -> p (a d)")
                    act.activation(dst, pYB[u.side][:, 0:D], ACT.Copy, scale=w_scale[:, 2, e])\
                       .then_inc(T["yo_ready"], 1)
            act.wait_ge(s_scale, 1)
            run_tiles(act, body)

        def vector_b(dve):
            V = nc.vector
            n = [0]

            def link(ins):
                n[0] += 1
                ins.then_inc(T["late_chain"], 1)
                dve.wait_ge(T["late_chain"], n[0])

            def tiles_of_experts():
                link(V.tensor_scalar(te[:, 0, :], total[:, :], (P - 1) / 2.0, 1.0 / P, ALU.add, ALU.mult))
                link(V.tensor_copy(te_i[:, :], te[:, 0, :]))
                link(V.tensor_copy(te[:, 1, :], te_i[:, :]))
                link(V.memset(te[:, 2, :], 0.0))
                link(V.tensor_tensor_scan(te[:, 3, :], te[:, 1, :], te[:, 2, :], 0.0, ALU.add, ALU.add))
                link(V.tensor_tensor(te[:, 0, :], te[:, 3, :], te[:, 1, :], ALU.subtract))
                link(V.scalar_tensor_tensor(te[:, 4, :], te[:, 0, :], float(P), capoff[:, :], ALU.mult, ALU.subtract))

            def expert_of_tiles():
                end, tiles = te[0:1, 3, :], te[0:1, 1, :]
                link(V.tensor_tensor(tg[:, 0], tile_f[:, :].unsqueeze(2).broadcast_to([1, RT, E]),
                                     end.unsqueeze(1).broadcast_to([1, RT, E]), ALU.is_ge))
                link(V.tensor_reduce(tb[:, 0, :], tg[:, 0], AX_X, ALU.add))
                link(V.tensor_tensor(tg[:, 1], tg[:, 0], tiles.unsqueeze(1).broadcast_to([1, RT, E]), ALU.mult))
                link(V.tensor_reduce(tb[:, 1, :], tg[:, 1], AX_X, ALU.add))

            def rows_of_tiles():
                link(V.tensor_tensor(tb[:, 2, :], tile_f[:, :], tb[:, 1, :], ALU.subtract))
                link(V.tensor_scalar(tb[:, 3, :], tb[:, 0, :], float(CAP), None, ALU.mult))
                link(V.scalar_tensor_tensor(tb[:, 4, :], tb[:, 2, :], float(P), tb[:, 3, :], ALU.mult, ALU.add))
                link(V.tensor_scalar(tb[:, 5, :], tb[:, 0, :], float(E), None, ALU.is_lt))
                link(V.tensor_tensor(tb[:, 6, :], tb[:, 4, :], tb[:, 5, :], ALU.mult))
                link(V.tensor_scalar(tb[:, 0, :], tb[:, 0, :], float(E - 1), 1.0, ALU.min, ALU.add))
                link(V.tensor_copy(tab[:, 0, :], tb[:, 0, :]))
                V.tensor_copy(tab[:, 1, :], tb[:, 6, :]).then_inc(s_tab, 1)

            def rows_of_choices():
                n_all = C * B * TOPK
                link(V.tensor_tensor(found[:, :, :], choice_all[:, :, :].rearrange("p c n -> p (c n)").unsqueeze(2)
                                     .broadcast_to([P, n_all, E]),
                                     iota8[:, :].unsqueeze(1).broadcast_to([P, n_all, E]), ALU.is_equal))
                link(V.tensor_tensor(found[:, :, :], found[:, :, :],
                                     te[:, 4, :].unsqueeze(1).broadcast_to([P, n_all, E]), ALU.mult))
                link(V.tensor_reduce(choice_all[:, :, :].rearrange("p c n -> p (c n)"), found[:, :, :], AX_X, ALU.add))
                link(V.tensor_tensor(place_all[:, :, :], place_all[:, :, :], choice_all[:, :, :], ALU.add))
                V.tensor_copy(pos_all[:, :, :], place_all[:, :, :]).then_inc(s_place, 1)

            def largest_of(e):
                if e == HEAD:
                    dve.wait_ge(s_w[1], 16 * 3 * (NE - HEAD))
                V.tensor_reduce(wmax[:, 0, e:e + 1], W[:, e].rearrange("p m n -> p (m n)").unsqueeze(1), AX_X, ALU.max,
                                apply_absolute_value=True).then_inc(s_wmax, 1)

            beside = [tiles_of_experts, expert_of_tiles, rows_of_tiles, rows_of_choices]
            beside += [lambda e=e: largest_of(e) for e in range(HEAD, NE)]
            beside += [lambda: scales(link, dve, HEAD, NE)]
            assert len(beside) <= EARLY - 2

            def mix(c):
                due_dma(dve, ya_loaded, c, B * TOPK)
                due(dve, T["yo_ready"], 1, c + (RT + C), 1)
                due(dve, U["lnc_ready"], B, c + -2, B)
                for b in range(B):
                    V.scalar_tensor_tensor(cmb[c.side][:, b, :], ya[c.side][b][0][:, :],
                                           wts_all[:, bass.ds(c.index, 1), b, 0],
                                           ysh[:, bass.ds(c.index + b * C, 1), :].rearrange("p c d -> p (c d)"),
                                           ALU.mult, ALU.add).then_inc(U["mix1"], 1)
                for b in range(B):
                    due(dve, U["mix1"], B, c, b + 1)
                    V.scalar_tensor_tensor(cmb[c.side][:, b, :], ya[c.side][b][1][:, :],
                                           wts_all[:, bass.ds(c.index, 1), b, 1],
                                           cmb[c.side][:, b, :], ALU.mult, ALU.add).then_inc(U["mix2"], 1)
                for b in range(B):
                    due(dve, U["mix2"], B, c, b + 1)
                    V.bn_stats(stc[c.side][:, b, :], cmb[c.side][:, b, :]).then_inc(U["stat1"], 1)
                for b in range(B):
                    due(dve, U["stat1"], B, c, b + 1)
                    if b == 0:
                        due(dve, U["shift_ready"], 1, c + -2, 1)
                    settle(dve)
                    V.bn_aggr(mvc[c.side][:, b, :], stc[c.side][:, b, :]).then_inc(U["stats_ready"], 1)
                due(dve, U["stats_ready"], B, c, B)
                due(dve, U["rstd_ready"], 1, c + -2, 1)
                V.tensor_scalar(vec[c.side][:, :], mvc[c.side][:, :, 1], EPS, None, ALU.add).then_inc(U["vare"], 1)

            def shift(c):
                due(dve, U["rstd_ready"], 1, c, 1)
                due(dve, U["lnc_ready"], B, c + -2, B)
                V.scalar_tensor_tensor(shiftc[c.side][:, :], mvc[c.side][:, :, 0], -1.0, rsc[c.side][:, :],
                                       ALU.mult, ALU.mult).then_inc(U["shift_ready"], 1)

            def residual(c):
                due(dve, U["lnc_ready"], B, c, B)
                due_dma(dve, x1_loaded, c)
                x_ = x1c[:, :, bass.ds(c.index, 1), :].rearrange("p b c d -> p (b c) d")
                V.tensor_tensor(x_, lnc[c.side][:, :, :], x_, ALU.add).then_inc(U["oc_ready"], 1)

            def body(t):
                if is_tile(t + -1):
                    u = t + -1
                    due(dve, T["gh_ready"], 1, u, 1)
                    due(dve, T["y_done"], 1, u + -2, 1)
                    V.tensor_tensor(gl[u.side][:, :, :].rearrange("p c t -> p (c t)"), pGT[:, :],
                                    gh[u.side][:, :, :].rearrange("p c t -> p (c t)"), ALU.subtract)\
                     .then_inc(T["gl_ready"], 1)
                if is_tile(t + 1):
                    u = t + 1
                    due(dve, T["xh_ready"], 1, u, 1)
                    due(dve, T["h2_done"], 1, u + -2, 1)
                    V.tensor_tensor(xl[u.side][:, :, :].rearrange("p k t -> p (k t)"), pT[:, 0:D],
                                    xh[u.side][:, :, :].rearrange("p k t -> p (k t)"), ALU.subtract)\
                     .then_inc(T["xl_ready"], 1)
                c = t + -MIX0
                if is_step(c + -1):
                    shift(c + -1)
                if is_step(c + -2):
                    residual(c + -2)
                if is_tile(t):
                    e = expert_of(dve, t)
                    due(dve, T["silu_ready"], 1, t, 1)
                    due(dve, T["h2_done"], 1, t, 1)
                    due(dve, T["ggT_done"], 1, t + -2, 1)
                    V.scalar_tensor_tensor(gg[t.side][:, :], sl[t.side][:, :], w_scale[:, 1, e], pH2[t.side][:, :],
                                           ALU.mult, ALU.mult).then_inc(T["gg_ready"], 1)
                if is_step(c):
                    mix(c)
                if t.fixed and 0 <= t.index < len(beside):
                    beside[t.index]()
            run_tiles(dve, body)

        def pool_b(pool):
            def split(e):
                whole = W[:, e].rearrange("p m n -> p (m n)")
                if e > 1:
                    pool.wait_ge(T["experts_split"], e - 1)
                pool.tensor_tensor(wtmp_p[:, :, :].rearrange("p m n -> p (m n)"), whole,
                                   w_scale[:, 1, e:e + 1].broadcast_to([P, 3 * MW]), ALU.mult).then_inc(T["pool_split"], 1)
                pool.wait_ge(T["pool_split"], 2 * e - 1)
                settle(pool)
                pool.tensor_copy(W16[:, e, :, 0, :], wtmp_p[:, :, :]).then_inc(T["pool_split"], 1)
                pool.wait_ge(T["pool_split"], 2 * e)
                pool.tensor_tensor(W16[:, e, :, 1, :], wtmp_p[:, :, :], W16[:, e, :, 0, :], ALU.subtract)\
                    .then_inc(T["experts_split"], 1)

            pool.wait_ge(s_scale, 1)
            split(1)
            pool.wait_ge(s_wmax, 1 + NE - HEAD)
            pool.partition_all_reduce(wmax[:, 1, HEAD:NE], wmax[:, 0, HEAD:NE], P, RMAX).then_inc(s_wall, 1)
            for e in range(2, HEAD):
                split(e)
            pool.wait_ge(s_scale, 2)
            for e in range(HEAD, NE):
                split(e)

        def pool_c(pool):
            for n in range(2):
                pool.wait_ge(yo_stored[n], 16 * RT // 2)
            pool.wait_ge(s_place, 1)

            def gather(c):
                due_dma(pool, ya_loaded, c + -2, B * TOPK)
                due(pool, U["mix2"], B, c + -2, B)
                settle(pool)
                pool.tensor_copy(gi[c.side][:, :].unsqueeze(1), pos_all[:, bass.ds(c.index, 1), :])\
                    .then_inc(U["gi_ready"], 1)
                due(pool, U["gi_ready"], 1, c, 1)
                for b in range(B):
                    for k in range(TOPK):
                        settle(pool)
                        pool.indirect_dma_start(ya[c.side][b][k][:, :], None, ys_d[:, :], bass.IndirectOffsetOnAxis(
                            ap=gi[c.side][:, b * TOPK + k:b * TOPK + k + 1], axis=0)).then_inc(ya_loaded[c.side], 16)

            def rstd(c):
                due(pool, U["vare"], 1, c, 1)
                due(pool, U["lnc_ready"], B, c + -2, B)
                pool.tensor_tensor(rsc[c.side][:, :], vec[c.side][:, :], half_neg[:, 0:B], ALU.pow)\
                    .then_inc(U["rstd_ready"], 1)

            def body(c):
                rstd(c)
                if not c.fixed or c.index + 2 < C:
                    gather(c + 2)

            for c in range(2):
                gather(Step.of(c))
            for c in range(2):
                body(Step.of(c))
            with pool.Fori(1, C // 2 - 1) as j:
                body(Step(j, 0))
                body(Step(j, 1))
            for c in range(C - 2, C):
                body(Step.of(c))

        phase_b.close()

        with nc.Block() as block:
            @block.sync
            def _(sp):
                sync_a(sp)
                sync_b(sp)

            @block.scalar
            def _(act):
                scalar_a(act)
                scalar_b(act)

            @block.gpsimd
            def _(pool):
                pool_a(pool)
                pool_b(pool)
                pool_c(pool)

            @block.vector
            def _(dve):
                vector_a(dve)
                vector_b(dve)

            @block.tensor
            def _(pe):
                tensor_a(pe)
                tensor_b(pe)


_INS = ['L0_attn_x', 'L0_attn_Wq', 'L0_attn_Wk', 'L0_attn_Wv', 'L0_attn_Wo', 'L0_attn_Wg', 'L0_attn_bg',
        'L0_ffn_gate_w', 'L0_ffn_ew1', 'L0_ffn_ew2', 'L0_ffn_ew3', 'L0_ffn_sw1', 'L0_ffn_sw2', 'L0_ffn_sw3']
_OUTS = [((2, 2048, 256), 'float32')]


def kernel(**inputs):
    import numpy as _np
    import concourse.bacc as _bacc
    from concourse import mybir as _mybir
    from concourse.bass_utils import run_bass_kernel_spmd as _run

    nc = _bacc.Bacc("TRN2", target_bir_lowering=False, num_devices=1)
    arrays, args = {}, []
    for name in _INS:
        a = _np.ascontiguousarray(inputs[name])
        arrays[f"in_{name}_dram"] = a
        args.append(nc.dram_tensor(f"in_{name}_dram", a.shape, _mybir.dt.from_np(a.dtype), kind="ExternalInput").ap())
    for i, (shape, dtype) in enumerate(_OUTS):
        dt = _mybir.dt.from_np(_np.dtype(dtype))
        args.append(nc.dram_tensor(f"out_{i}_dram", shape, dt, kind="ExternalOutput").ap())
    sandwich_kernel(nc, *args)
    r = _run(nc, [arrays], core_ids=[0])
    return r.results[0]["out_0_dram"]
```

```python
from contextlib import ExitStack

import concourse.bass as bass
from concourse import mybir

ALU = mybir.AluOpType
ACT = mybir.ActivationFunctionType
F32 = mybir.dt.float32
F16 = mybir.dt.float16
BF16 = mybir.dt.bfloat16
U32 = mybir.dt.uint32
I32 = mybir.dt.int32
AX_X = mybir.AxisListType.X
RMAX = bass.bass_isa.ReduceOp.max
EPS = 1e-5


class Step:

    def __init__(self, half, side, kind=None):
        self.half, self.side, self.kind = half, side, kind

    @staticmethod
    def of(i):
        return Step(i // 2, i % 2)

    def __add__(self, d):
        q = self.side + d
        return Step(self.half + q // 2, q % 2, self.kind)

    @property
    def index(self):
        return self.half * 2 + self.side

    @property
    def fixed(self):
        return isinstance(self.half, int)


def due(eng, sem, per, step, k):
    n = step.index * per + k
    if step.fixed and n <= 0:
        return
    eng.wait_ge(sem, n)


def due_dma(eng, sems, step, n=1):
    if step.fixed and step.half < 0:
        return
    eng.wait_ge(sems[step.side], (step.half + 1) * (16 * n))


def sandwich_kernel(nc, x, Wq, Wk, Wv, Wo, Wg, bg, gate_w, ew1, ew2, ew3, sw1, sw2, sw3, out):
    P = 128
    B, SEQ, D = x.shape
    HEADS = Wg.shape[0]
    DH = D // HEADS
    SCALE = float(DH) ** -0.5
    KC = D // P
    GH = P // DH
    GR = HEADS // GH
    SETH = 4
    NS = B * HEADS // SETH
    C = SEQ // P
    TOK = B * SEQ
    E = gate_w.shape[1]
    TOPK = 2
    H = ew1.shape[2]
    HC = H // P
    NE = E + 1
    HEAD = 6
    MW = KC * H
    CAP = TOK + P
    SHARED = E * CAP
    ROWS = SHARED + TOK
    ST = TOK // P
    RT = TOPK * TOK // P + E
    VW = 3 * DH
    NT = ST + RT
    EARLY = 12
    T0 = EARLY + RT
    assert (B, GR, KC, TOPK) == (2, 2, 2, 2) and C % 2 == 0 and HC * D == MW and RT % 2 == 0
    assert C * B <= 256
    assert EARLY % 4 == 0 and 8 < EARLY < C

    ctx = ExitStack()
    with ctx:
        def sem(name):
            return ctx.enter_context(nc.semaphore(name))

        def sb(name, shape, dt=F32):
            return ctx.enter_context(nc.sbuf_tensor(name, shape, dt))

        xs_d = nc.dram_tensor("xs_scratch", [ROWS, D], F32).ap()
        ys_d = nc.dram_tensor("ys_scratch", [RT * P, D], F32).ap()
        x1_d = nc.dram_tensor("x1_scratch", [TOK, D], F32).ap()

        bank = [ctx.enter_context(nc.psum_tensor(f"bank{n}", [P, 512], F32)) for n in range(8)]

        W = sb("W", [P, NE, 3, MW])
        W16 = W[:].rearrange("p e m n -> p (e m n)").bitcast(F16).rearrange(
            "p (e m s n) -> p e m s n", e=NE, m=3, s=2)
        ident = sb("ident", [P, P])
        half_neg = sb("half_neg", [P, 2])
        wts_all = sb("wts_all", [P, C, B, TOPK])
        pos_all = sb("pos_all", [P, C, B * TOPK], U32)
        wmax = sb("wmax", [P, 2, NE])
        w_scale = sb("w_scale", [P, 3, NE])
        tab = sb("tab", [1, 2, RT], I32)
        choice_all = sb("choice_all", [P, C, B * TOPK])
        place_all = sb("place_all", [P, C, B * TOPK])
        iota8 = sb("iota8", [P, E])
        capoff = sb("capoff", [P, E])
        rowid = sb("rowid", [P, 1])
        total = sb("total", [P, E])
        pad_row = sb("pad_row", [P, E], U32)
        zrow = sb("zrow", [P, D])
        tile_f = sb("tile_f", [1, RT])
        te = sb("te", [P, 5, E])
        te_i = sb("te_i", [P, E], I32)
        tb = sb("tb", [1, 8, RT])
        tg = sb("tg", [1, 2, RT, E])
        found = sb("found", [P, C * B * TOPK, E])
        wpart = sb("wpart", [P, HEAD, 3])

        s_w = [sem(f"s_w_loaded{n}") for n in range(2)]
        s_init = sem("s_init")
        s_vinit = sem("s_vinit")
        dve_chain = sem("dve_chain")

        phase_a = ExitStack()

        def sa(name, shape, dt=F32):
            return phase_a.enter_context(nc.sbuf_tensor(name, shape, dt))

        late = W[:, HEAD:NE].rearrange("p e m n -> p (e m n)")
        taken = [0]

        def in_late(*shape):
            n = 1
            for d in shape:
                n *= d
            taken[0] += n
            assert taken[0] <= (NE - HEAD) * 3 * MW
            ap = late[:, taken[0] - n:taken[0]]
            if len(shape) == 3:
                return ap.rearrange("p (a b c) -> p a b c", a=shape[0], b=shape[1])
            return ap.rearrange("p (a b c d) -> p a b c d", a=shape[0], b=shape[1], c=shape[2])

        qbd = in_late(B, GR, GH, P)
        wraw = qbd.rearrange("p b g h t -> p (b g h t)")[:, 0:5 * GR * D].rearrange(
            "p (n g d) -> p n g d", n=5, g=GR)
        wT = sa("wT", [P, 5, KC, D])
        gw = sa("gw", [P, KC, E])
        hbg = sa("hbg", [P, GR])
        sel = sa("sel", [P, GH, P], BF16)
        diag4 = sa("diag4", [P, SETH, P])
        later = sa("later", [P, P], BF16)
        ones = sa("ones", [P, P], BF16)
        hmask = sa("hmask", [P, GH])
        tmp8 = sa("tmp8", [P, 2, GH])
        part_mask = sa("part_mask", [P, 2])
        zeros = sa("zeros", [P, P])

        x_in = [sa(f"x_in{n}", [P, B, D]) for n in range(2)]
        x_res = [sa(f"x_res{n}", [P, B, D]) for n in range(2)]
        st1 = sa("st1", [P, B, 6])
        mv1 = [sa(f"mv1_{n}", [P, B, 2]) for n in range(2)]
        ve = sa("ve", [P, 3, B])
        nm = sa("nm", [P, 3, B])
        rs1 = [sa(f"rs1_{n}", [P, B]) for n in range(2)]
        sh1 = [sa(f"sh1_{n}", [P, B]) for n in range(2)]
        xn = sa("xn", [P, B, D])
        xnT_ = sa("xnT", [P, 2, KC, B * P])
        xnT = [xnT_[:, n] for n in range(2)]
        rneg = sa("rneg", [P, GR * B * P])
        ef_ = sa("ef", [P, 2, GR * B * P])
        ef = [ef_[:, n] for n in range(2)]
        wtmp_b = [ef_[:, :, :].rearrange("p n t -> p (n t)"), xnT_[:, :, :, :].rearrange("p n k t -> p (n k t)")]
        qT = [sa(f"qT{n}", [P, GR, B, P]) for n in range(2)]
        kT = [sa(f"kT{n}", [P, GR, B, P]) for n in range(2)]
        eg = sa("eg", [P, GR, B, P])
        gT = sa("gT", [P, GR, B, P])
        ghi = sa("ghi", [P, GR, B, P], BF16)
        gt1 = sa("gt1", [P, GR, B, P])
        gr1 = sa("gr1", [P, GR, B, P])
        gparts = [sa(f"gparts{n}", [P, GR, B, P], BF16) for n in range(2)]
        gam = [in_late(GR, B, P) for n in range(2)]
        qg = [in_late(GR, B, P) for n in range(2)]
        vp = [in_late(B, HEADS, VW) for n in range(2)]
        decay = [sa(f"decay{n}", [P, SETH, P]) for n in range(2)]
        probs = [sa(f"probs{n}", [P, SETH, P]) for n in range(2)]
        kd = sa("kd", [P, B, GR, P])
        um = sa("um", [P, B, GR, P])
        state = sa("state", [P, B, GR, P])
        yT = [sa(f"yT{n}", [P, B, GR, P]) for n in range(2)]
        sto = sa("sto", [P, B, 6])
        mvo = sa("mvo", [P, B, 2])
        rso = sa("rso", [P, B])
        sho = sa("sho", [P, B])
        ln_o = sa("ln_o", [P, B, D])
        x1 = [sa(f"x1_{n}", [P, B, D]) for n in range(2)]
        st2 = sa("st2", [P, B, 6])
        mv2 = sa("mv2", [P, B, 2])
        rs2 = sa("rs2", [P, B])
        sh2 = sa("sh2", [P, B])
        xn2 = [sa(f"xn2_{n}", [P, B, D]) for n in range(2)]
        xn2T = sa("xn2T", [P, KC, B * P])
        lg = sa("lg", [P, B, E])
        mx = sa("mx", [P, B, 8])
        mi = sa("mi", [P, B, 8], U32)
        mif = sa("mif", [P, B, 8])
        dv = sa("dv", [P, B])
        ew = sa("ew", [P, B])
        wtmp = sa("wtmp", [P, 2, B])
        oh = sa("oh", [P, B, TOPK, E])
        chosen = sa("chosen", [P, B, E], BF16)
        csum = sa("csum", [P, E], BF16)
        slot = sa("slot", [P, B, E])
        posf = sa("posf", [P, B * TOPK])
        posi = [sa(f"posi{n}", [P, B * TOPK], U32) for n in range(2)]

        pA, pG, pY, pU, X0, X1 = bank[0:2], bank[2:4], bank[4], bank[5], bank[6], bank[7]

        names = ("wraw_loaded wT_done wT_ready xn_stats rstd1_ready xn_ready xT_done xnT_ready q_done rq_ready"
                 " eq_ready qT_ready k_done rk_ready ek_ready kT_ready g_done eg_ready gT_ready ghi_ready"
                 " gmask_ready grest_ready gmid_ready gparts_ready gam_ready qg_ready qbd_ready v_done v_ready ktok_done gbc_done decay_ready"
                 " A_done probs_ready kd_ready PV_done U_done um_ready state_ready yT_ready o_done o_stats"
                 " rstdo_ready ln_ready x1_ready x1_stats rstd2_ready xn2_ready xn2T_done xn2T_ready gate_done"
                 " top_ready ew_ready chosen_ready prefix_done pos_ready wts_ready csum_ready pool_chain").split()
        S = {n: sem(n) for n in names}
        CONSTANTS = 24
        x_loaded = [sem(f"x_loaded{n}") for n in range(2)]
        xr_loaded = [sem(f"xr_loaded{n}") for n in range(2)]
        x1_stored = [sem(f"x1_stored{n}") for n in range(2)]
        xs_stored = [sem(f"xs_stored{n}") for n in range(2)]
        scattered = [sem(f"scattered{n}") for n in range(2)]
        s_total = sem("s_total")
        s_totals = sem("s_totals")
        s_pad = sem("s_pad_rows")
        s_padded = sem("s_padded")
        s_wmax = sem("s_wmax")
        s_wall = sem("s_wmax_all")
        s_scale = sem("s_scale")
        s_tab = sem("s_table")
        s_wpart = sem("s_wmax_parts")
        s_place = sem("s_place")
        w_scaled, w_high, w_low = sem("w_scaled"), sem("w_high"), sem("w_low")

        x_by_step = x.rearrange("b (c p) d -> c p b d", p=P)
        x1_by_step = x1_d.rearrange("(b c p) d -> c p b d", b=B, p=P)
        xs_by_step = xs_d[SHARED:SHARED + TOK, :].rearrange("(b c p) d -> c p b d", b=B, p=P)

        def settle(eng):
            eng.nop(nofuse=True)

        def free2(ap):
            return ap.rearrange("p a b -> p (a b)")

        def free3(ap):
            return ap.rearrange("p a b c -> p (a b c)")

        FIRST, LAST = -2, C + 1
        LOOP = (3, C - 3)
        TURNS = (LOOP[1] - LOOP[0]) // 2
        assert HEAD - TURNS < C - 1 - LOOP[1]

        def run_bodies(eng, body):
            for i in range(FIRST, LOOP[0]):
                body(Step.of(i))
            with eng.Fori(LOOP[0] // 2, LOOP[1] // 2) as j:
                body(Step(j, 1))
                body(Step(j + 1, 0))
            for i in range(LOOP[1], LAST + 1):
                body(Step.of(i))

        def has(step):
            return not step.fixed or 0 <= step.index < C

        def load_experts(eng, first, end):
            for e in range(first, end):
                src = (ew1[e - 1], ew2[e - 1], ew3[e - 1]) if e else (sw1, sw2, sw3)
                for m in range(3):
                    eng.dma_start(W[:, e, m, :].rearrange("p (c n) -> p c n", c=KC if m < 2 else HC),
                                  src[m].rearrange("(c p) n -> p c n", p=P)).then_inc(s_w[int(e >= HEAD)], 16)

        def sync_a(sp):
            for n, w in enumerate((Wq, Wk, Wv, Wo)):
                sp.dma_start(wraw[:, n], w.rearrange("(g p) d -> p g d", p=P)).then_inc(S["wraw_loaded"], 16)
            for g in range(GR):
                heads = slice(g * GH, (g + 1) * GH)
                sp.dma_start(wraw[:, 4, g, :], Wg[heads, :].unsqueeze(1).broadcast_to([GH, DH, D]))\
                  .then_inc(S["wraw_loaded"], 16)
                sp.dma_start(hbg[:, g:g + 1], bg[heads].unsqueeze(1).unsqueeze(2).broadcast_to([GH, DH, 1]))\
                  .then_inc(S["wraw_loaded"], 16)
            sp.dma_start(gw[:, :, :], gate_w.rearrange("(k p) e -> p k e", p=P)).then_inc(S["wraw_loaded"], 16)

            def body(i):
                a0, a3 = i + 2, i + -1
                if has(a0):
                    due(sp, S["xn_ready"], B, a0 + -2, B)
                    sp.dma_start(x_in[a0.side][:, :, :], x_by_step[a0.index]).then_inc(x_loaded[a0.side], 16)
                if has(a3):
                    due(sp, S["x1_ready"], 1, a3 + -2, 1)
                    sp.dma_start(x_res[a3.side][:, :, :], x_by_step[a3.index]).then_inc(xr_loaded[a3.side], 16)
                    due(sp, S["x1_ready"], 1, a3, 1)
                    sp.dma_start(x1_by_step[a3.index], x1[a3.side][:, :, :]).then_inc(x1_stored[a3.side], 16)
                    due(sp, S["xn2_ready"], B, a3, B)
                    sp.dma_start(xs_by_step[a3.index], xn2[a3.side][:, :, :]).then_inc(xs_stored[a3.side], 16)
                if i.fixed and 0 <= i.index < LOOP[0]:
                    load_experts(sp, i.index * HEAD // LOOP[0], (i.index + 1) * HEAD // LOOP[0])
            run_bodies(sp, body)

        def scalar_a(act):
            act.wait_ge(S["wT_done"], 5)
            for n in range(5):
                act.activation(free2(wT[:, n]), bank[n][:, :], ACT.Copy, scale=SCALE if n == 0 else 1.0)\
                   .then_inc(S["wT_ready"], 1)

            def feature(i, src, done, r_ready, e_ready, used, dst):
                due(act, S[done], 1, i, 1)
                due(act, S["ek_ready" if done == "q_done" else "eq_ready"], 1,
                    i + -1 if done == "q_done" else i, 1)
                act.activation(rneg[:, :], src[:, :], ACT.Relu, scale=-1.0).then_inc(S[r_ready], 1)
                due(act, S[r_ready], 1, i, 1)
                due(act, S[used], 1, i + -1, 1)
                act.activation(dst[:, :], rneg[:, :], ACT.Exp, scale=-1.0).then_inc(S[e_ready], 1)

            def high(m):
                act.wait_ge(w_scaled, m + 1)
                act.activation(W16[:, 0, m, 0, :], wtmp_b[m % 2], ACT.Copy).then_inc(w_high, 1)

            def normalise(dst, src, rs, sh, ready):
                for b in range(B):
                    act.activation(dst[:, b, :], src[b], ACT.Identity, bias=sh[:, b:b + 1], scale=rs[:, b:b + 1])\
                       .then_inc(S[ready], 1)

            def body(i):
                a0, a1, a2, a3 = i + 2, i + 1, i, i + -1
                if has(a1):
                    due(act, S["xT_done"], 1, a1, 1)
                    due(act, S["v_done"], 1, a1 + -2, 1)
                    act.activation(free2(xnT[a1.side][:, :, :]), X1[:, :], ACT.Copy).then_inc(S["xnT_ready"], 1)
                if has(a3):
                    if a3.fixed and a3.index == C - 1:
                        high(0)
                    due(act, S["rstdo_ready"], 4, a3, 4)
                    due(act, S["x1_ready"], 1, a3 + -1, 1)
                    normalise(ln_o, [X0[:, b * D:(b + 1) * D] for b in range(B)], rso, sho, "ln_ready")
                    if a3.fixed and a3.index == C - 1:
                        high(1)
                        high(2)
                if has(a1):
                    feature(a1, X1, "q_done", "rq_ready", "eq_ready", "qT_ready", ef[0])
                    feature(a1, X0, "k_done", "rk_ready", "ek_ready", "kT_ready", ef[1])
                if has(a0):
                    due(act, S["rstd1_ready"], 4, a0, 4)
                    due(act, S["xT_done"], 1, a0 + -1, 1)
                    normalise(xn, [x_in[a0.side][:, b, :] for b in range(B)], rs1[a0.side], sh1[a0.side], "xn_ready")
                if has(a3):
                    due(act, S["rstd2_ready"], 4, a3, 4)
                    due_dma(act, xs_stored, a3 + -2)
                    due_dma(act, scattered, a3 + -2, B * TOPK)
                    due(act, S["xn2T_done"], 1, a3 + -2, 1)
                    normalise(xn2[a3.side], [x1[a3.side][:, b, :] for b in range(B)], rs2, sh2, "xn2_ready")
                if has(a1):
                    due(act, S["g_done"], 1, a1, 1)
                    due(act, S["gT_ready"], 1, a1 + -1, 1)
                    for g in range(GR):
                        act.activation(eg[:, g].rearrange("p b t -> p (b t)"), X1[:, g * B * P:(g + 1) * B * P],
                                       ACT.Tanh, bias=hbg[:, g:g + 1], scale=0.5).then_inc(S["eg_ready"], 1)
                if has(a1):
                    due(act, S["v_done"], 1, a1, 1)
                    due(act, S["U_done"], 1, a1 + -2, 1)
                    for b in range(B):
                        act.activation(vp[a1.side][:, b, :, DH:2 * DH],
                                       X0[:, b * D:(b + 1) * D].rearrange("p (h j) -> p h j", j=DH), ACT.Copy)\
                           .then_inc(S["v_ready"], 1)
                if has(a3):
                    due(act, S["xn2T_done"], 1, a3, 1)
                    due(act, S["gate_done"], 1, a3 + -1, 1)
                    act.activation(free2(xn2T[:, :, :]), X1[:, :], ACT.Copy).then_inc(S["xn2T_ready"], 1)
                if has(a1):
                    gp = gparts[a1.side]
                    due(act, S["gT_ready"], 1, a1, 1)
                    due(act, S["gmask_ready"], 2, a1 + -1, 1)
                    act.activation(free3(ghi[:, :, :, :]), free3(gT[:, :, :, :]), ACT.Copy)\
                       .then_inc(S["ghi_ready"], 1)
                    due(act, S["ghi_ready"], 1, a1, 1)
                    due(act, S["gparts_ready"], 1, a1 + -1, 1)
                    act.activation(free3(gt1[:, :, :, :]), free3(ghi[:, :, :, :]), ACT.Copy,
                                   scale=part_mask[:, 0:1]).then_inc(S["gmask_ready"], 1)
                    due(act, S["grest_ready"], 1, a1, 1)
                    due(act, S["gbc_done"], NS, a1 + -2, NS)
                    act.activation(gp[:, :, :, 1:P].rearrange("p g b t -> p (g b) t"),
                                   gr1[:, :, :, 1:P].rearrange("p g b t -> p (g b) t"), ACT.Copy)\
                       .then_inc(S["gmid_ready"], 1)
                    due(act, S["gmid_ready"], 1, a1, 1)
                    act.activation(gt1[:, :, :, 1:P].rearrange("p g b t -> p (g b) t"),
                                   gp[:, :, :, 1:P].rearrange("p g b t -> p (g b) t"), ACT.Copy,
                                   scale=part_mask[:, 1:2]).then_inc(S["gmask_ready"], 1)
                if has(a3):
                    due(act, S["top_ready"], 1, a3, 1)
                    due(act, S["wts_ready"], 1, a3 + -1, 1)
                    act.activation(ew[:, :], dv[:, :], ACT.Exp).then_inc(S["ew_ready"], 1)
                if has(a2):
                    due(act, S["PV_done"], NS, a2, NS)
                    due(act, S["o_done"], 1, a2 + -2, 1)
                    act.activation(free3(yT[a2.side][:, :, :, :]), pY[:, :], ACT.Copy).then_inc(S["yT_ready"], 1)
            run_bodies(act, body)
            act.wait_ge(S["PV_done"], C * NS)
            act.wait_ge(S["state_ready"], (C - 1) * GR * B)
            load_experts(act, HEAD, NE)

        def pool_a(pool):
            made = [0]

            def link(ins):
                made[0] += 1
                ins.then_inc(s_init, 1)
                pool.wait_ge(s_init, made[0])

            link(pool.memset(ident[:, :], 0.0))
            link(pool.affine_select(out=ident[:, :], in_=ident[:, :], compare_op=ALU.not_equal, fill=1.0,
                                    base=0, pattern=[[-1, P]], channel_multiplier=1))
            link(pool.memset(ones[:, :], 1.0))
            link(pool.memset(half_neg[:, :], -0.5))
            link(pool.memset(diag4[:, :, :], 0.0))
            link(pool.affine_select(out=diag4[:, :, :], in_=diag4[:, :, :], compare_op=ALU.not_equal, fill=1.0,
                                    base=0, pattern=[[0, SETH], [-1, P]], channel_multiplier=1))
            link(pool.affine_select(out=later[:, :], in_=ones[:, :], compare_op=ALU.is_gt, fill=0.0,
                                    base=0, pattern=[[1, P]], channel_multiplier=-1))
            link(pool.memset(sel[:, :, :], 1.0))
            link(pool.affine_select(out=sel[:, :, :], in_=sel[:, :, :], compare_op=ALU.is_ge, fill=0.0,
                                    base=0, pattern=[[-DH, GH], [0, P]], channel_multiplier=1))
            link(pool.affine_select(out=sel[:, :, :], in_=sel[:, :, :], compare_op=ALU.is_ge, fill=0.0,
                                    base=2, pattern=[[DH, GH], [0, P]], channel_multiplier=-1))
            for dst, low in ((hmask[:, :], 0), (tmp8[:, 0], 1), (tmp8[:, 1], 2)):
                link(pool.memset(dst, 1.0))
                link(pool.affine_select(out=dst, in_=dst, compare_op=ALU.is_ge, fill=0.0,
                                        base=-low, pattern=[[-DH, GH]], channel_multiplier=1))
                link(pool.affine_select(out=dst, in_=dst, compare_op=ALU.is_ge, fill=0.0,
                                        base=DH - 1, pattern=[[DH, GH]], channel_multiplier=-1))
            link(pool.iota(iota8[:, :], pattern=[[1, E]], base=0, channel_multiplier=0,
                           allow_small_or_imprecise_dtypes=True))
            link(pool.iota(capoff[:, :], pattern=[[CAP, E]], base=0, channel_multiplier=0,
                           allow_small_or_imprecise_dtypes=True))
            link(pool.iota(rowid[:, :], pattern=[[0, 1]], base=0, channel_multiplier=1,
                           allow_small_or_imprecise_dtypes=True))
            link(pool.iota(tile_f[:, :], pattern=[[1, RT]], base=0, channel_multiplier=0,
                           allow_small_or_imprecise_dtypes=True))
            link(pool.memset(zrow[:, :], 0.0))
            assert made[0] == CONSTANTS

            def rstd(rs, sh, mv, n, i, stats, ready, used):
                due(pool, S[stats], B, i, B)
                settle(pool)
                pool.tensor_scalar(ve[:, n, :], mv[:, :, 1], EPS, None, ALU.add).then_inc(S[ready], 1)
                pool.tensor_scalar(nm[:, n, :], mv[:, :, 0], -1.0, None, ALU.mult).then_inc(S[ready], 1)
                due(pool, S[ready], 4, i, 1)
                due(pool, S[used[0]], B, used[1], B)
                pool.tensor_tensor(rs[:, :], ve[:, n, :], half_neg[:, 0:B], ALU.pow).then_inc(S[ready], 1)
                due(pool, S[ready], 4, i, 3)
                pool.tensor_tensor(sh[:, :], nm[:, n, :], rs[:, :], ALU.mult).then_inc(S[ready], 1)

            def block_diagonal(i, b):
                due(pool, S["qT_ready"], 1, i, 1)
                due(pool, S["A_done"], NS, i + -1, (b + 1) * NS // B)
                for g in range(GR):
                    pool.tensor_tensor(qbd[:, b, g], qT[i.side][:, g, b].unsqueeze(1).broadcast_to([P, GH, P]),
                                       hmask[:, :].unsqueeze(2).broadcast_to([P, GH, P]), ALU.mult)\
                        .then_inc(S["qbd_ready"], 1)

            pool.wait_ge(s_vinit, 5)

            def body(i):
                a0, a1, a3, a4 = i + 2, i + 1, i + -1, i + -2

                if has(a3):
                    rstd(rso, sho, mvo, 1, a3, "o_stats", "rstdo_ready", ("ln_ready", a3 + -1))
                if has(a0):
                    rstd(rs1[a0.side], sh1[a0.side], mv1[a0.side], 0, a0, "xn_stats", "rstd1_ready",
                         ("xn_ready", a0 + -2))
                if has(a3):
                    due(pool, S["ln_ready"], B, a3, B)
                    due_dma(pool, xr_loaded, a3)
                    due_dma(pool, x1_stored, a3 + -2)
                    due(pool, S["xn2_ready"], B, a3 + -2, B)
                    pool.tensor_tensor(free2(x1[a3.side][:, :, :]), free2(ln_o[:, :, :]),
                                       free2(x_res[a3.side][:, :, :]), ALU.add).then_inc(S["x1_ready"], 1)
                    rstd(rs2, sh2, mv2, 2, a3, "x1_stats", "rstd2_ready", ("xn2_ready", a3 + -1))
                if has(a4):
                    due(pool, S["pos_ready"], 1, a4, 1)
                    due(pool, S["xn2_ready"], B, a4, B)
                    for b in range(B):
                        for k in range(TOPK):
                            settle(pool)
                            pool.indirect_dma_start(
                                xs_d[:, :], bass.IndirectOffsetOnAxis(
                                    ap=posi[a4.side][:, b * TOPK + k:b * TOPK + k + 1], axis=0),
                                xn2[a4.side][:, b, :], None).then_inc(scattered[a4.side], 16)
                if has(a1):
                    block_diagonal(a1, 0)
                    gp = gparts[a1.side]
                    due(pool, S["gmask_ready"], 2, a1, 1)
                    pool.tensor_tensor(free3(gr1[:, :, :, :]), free3(gT[:, :, :, :]), free3(gt1[:, :, :, :]),
                                       ALU.subtract).then_inc(S["grest_ready"], 1)
                    due(pool, S["gmask_ready"], 2, a1, 2)
                    pool.tensor_tensor(gp[:, :, :, 1:P].rearrange("p g b t -> p (g b) t"),
                                       gr1[:, :, :, 1:P].rearrange("p g b t -> p (g b) t"),
                                       gt1[:, :, :, 1:P].rearrange("p g b t -> p (g b) t"), ALU.subtract)\
                        .then_inc(S["gparts_ready"], 1)
                    due(pool, S["gam_ready"], GR * B, a1, GR * B)
                    due(pool, S["PV_done"], NS, a1 + -2, NS)
                    pool.tensor_tensor(free3(qg[a1.side][:, :, :, :]), free3(qT[a1.side][:, :, :, :]),
                                       free3(gam[a1.side][:, :, :, :]), ALU.mult).then_inc(S["qg_ready"], 1)
                    block_diagonal(a1, 1)
                if i.fixed and i.index == C - 1:
                    pool.wait_ge(s_wmax, 1)
                    pool.partition_all_reduce(wmax[:, 1, 0:HEAD], wmax[:, 0, 0:HEAD], P, RMAX).then_inc(s_wall, 1)
            run_bodies(pool, body)
            pool.wait_ge(s_pad, 1)
            for e in range(E):
                settle(pool)
                pool.indirect_dma_start(xs_d[:, :], bass.IndirectOffsetOnAxis(ap=pad_row[:, e:e + 1], axis=0),
                                        zrow[:, :], None).then_inc(s_padded, 16)

        def tensor_a(pe):
            mm = nc.tensor.matmul
            pe.wait_ge(s_init, 2)
            pe.wait_ge(S["wraw_loaded"], 16 * (5 + 2 * GR))
            for n in range(5):
                for k in range(KC):
                    for g in range(GR):
                        last = nc.tensor.transpose(bank[n][:, k * D + g * P:k * D + (g + 1) * P],
                                                   wraw[:, n, g, k * P:(k + 1) * P], ident[:, :])
                last.then_inc(S["wT_done"], 1)
            pe.wait_ge(S["wT_ready"], 5)
            pe.wait_ge(s_init, CONSTANTS)
            pe.wait_ge(s_vinit, 5)

            def project(i, n, dst, done):
                for g in range(GR):
                    for k in range(KC):
                        last = mm(dst[:, g * B * P:(g + 1) * B * P], wT[:, n, k, g * P:(g + 1) * P],
                                  xnT[i.side][:, k, :], start=(k == 0), stop=(k == KC - 1))
                last.then_inc(S[done], 1)

            def where(s):
                return s * B // NS, (s % (NS // B)) // (NS // B // GR), s % (GH // SETH)

            def scores(i, s):
                b, g, q = where(s)
                due(pe, S["gparts_ready"], 1, i, 1)
                due(pe, S["decay_ready"], NS, i, s - 1)
                for h in range(SETH):
                    last = mm(pG[s % 2][:, h * P:(h + 1) * P], sel[:, q * SETH + h, :], gparts[i.side][:, g, b, :],
                              start=True, stop=True)
                last.then_inc(S["gbc_done"], 1)
                due(pe, S["kT_ready"], 1, i, 1)
                due(pe, S["qbd_ready"], GR * B, i, b * GR + g + 1)
                due(pe, S["probs_ready"], NS, i, s - 1)
                mm(pA[s % 2][:, :], kT[i.side][:, g, b, :],
                   qbd[:, b, g, q * SETH:(q + 1) * SETH, :].rearrange("p h t -> p (h t)"),
                   start=True, stop=True).then_inc(S["A_done"], 1)

            def attend(i, s):
                b, g, q = where(s)
                col = (b * GR + g) * P
                if s == 0:
                    due(pe, S["yT_ready"], 1, i + -1, 1)
                    due(pe, S["qg_ready"], 1, i, 1)
                    due(pe, S["state_ready"], GR * B, i + -1, GR * B)
                    due(pe, S["v_ready"], B, i, B)
                if q == 0:
                    mm(pY[:, col:col + P], state[:, b, g, :], qg[i.side][:, g, b, :], start=True, stop=False,
                       skip_group_check=True)
                due(pe, S["probs_ready"], NS, i, s + 1)
                for h in range(SETH):
                    head = q * SETH + h
                    r = head // 2 * 2 * DH
                    lo = DH if head % 2 == 0 else 0
                    last = mm(pY[r:r + 2 * DH, col:col + P],
                              vp[i.side][:, b, g * GH + head, lo:lo + 2 * DH], probs[s % 2][:, h, :],
                              start=False, stop=(head % 2 == 1), skip_group_check=True)
                last.then_inc(S["PV_done"], 1)

            def body(i):
                a1, a2, a3 = i + 1, i, i + -1
                A1, A2, A3 = has(a1), has(a2), has(a3)
                if A3:
                    due(pe, S["yT_ready"], 1, a3, 1)
                    if A2:
                        due(pe, S["v_ready"], B, a2, B)
                    due(pe, S["ln_ready"], B, a3 + -1, B)
                    for b in range(B):
                        for g in range(GR):
                            last = mm(X0[:, b * D:(b + 1) * D], yT[a3.side][:, b, g, :], wT[:, 3, g, :],
                                      start=(g == 0), stop=(g == GR - 1))
                    last.then_inc(S["o_done"], 1)
                if A2:
                    due(pe, S["kT_ready"], 1, a2, 1)
                    due(pe, S["um_ready"], 1, a2 + -1, 1)
                    for b in range(B):
                        for g in range(GR):
                            last = nc.tensor.transpose(pU[:, (b * GR + g) * P:(b * GR + g + 1) * P],
                                                       kT[a2.side][:, g, b, :], ident[:, :])
                    last.then_inc(S["ktok_done"], 1)
                    scores(a2, 0)
                    scores(a2, 1)
                if A1:
                    due(pe, S["xn_ready"], B, a1, B)
                    due(pe, S["pos_ready"], 1, a1 + -3, 1)
                    for k in range(KC):
                        for b in range(B):
                            last = nc.tensor.transpose(X1[:, (k * B + b) * P:(k * B + b + 1) * P],
                                                       xn[:, b, k * P:(k + 1) * P], ident[:, :])
                    last.then_inc(S["xT_done"], 1)
                if A2:
                    attend(a2, 0)
                    scores(a2, 2)
                if A1:
                    due(pe, S["xnT_ready"], 1, a1, 1)
                    project(a1, 0, X1, "q_done")
                if A2:
                    attend(a2, 1)
                    scores(a2, 3)
                if A1:
                    due(pe, S["ln_ready"], B, a1 + -2, B)
                    if not A3 and a1.index > 0:
                        due(pe, S["v_ready"], B, a1 + -1, B)
                    project(a1, 1, X0, "k_done")
                if A2:
                    attend(a2, 2)
                    scores(a2, 4)
                if A1:
                    due(pe, S["qT_ready"], 1, a1, 1)
                    project(a1, 4, X1, "g_done")
                if A2:
                    attend(a2, 3)
                    scores(a2, 5)
                if A1:
                    due(pe, S["kT_ready"], 1, a1, 1)
                    for b in range(B):
                        for k in range(KC):
                            last = mm(X0[:, b * D:(b + 1) * D], xnT[a1.side][:, k, b * P:(b + 1) * P], wT[:, 2, k, :],
                                      start=(k == 0), stop=(k == KC - 1))
                    last.then_inc(S["v_done"], 1)
                if A3:
                    due(pe, S["xn2_ready"], B, a3, B)
                    if A1:
                        due(pe, S["eg_ready"], GR, a1, GR)
                    due(pe, S["pos_ready"], 1, a3 + -1, 1)
                    for k in range(KC):
                        for b in range(B):
                            last = nc.tensor.transpose(X1[:, (k * B + b) * P:(k * B + b + 1) * P],
                                                       xn2[a3.side][:, b, k * P:(k + 1) * P], ident[:, :])
                    last.then_inc(S["xn2T_done"], 1)
                if A2:
                    attend(a2, 4)
                    scores(a2, 6)
                if A3:
                    due(pe, S["xn2T_ready"], 1, a3, 1)
                    for b in range(B):
                        for k in range(KC):
                            last = mm(X1[:, b * E:(b + 1) * E], xn2T[:, k, b * P:(b + 1) * P], gw[:, k, :],
                                      start=(k == 0), stop=(k == KC - 1))
                    last.then_inc(S["gate_done"], 1)
                if A2:
                    attend(a2, 5)
                    scores(a2, 7)
                    attend(a2, 6)
                    attend(a2, 7)
                if A2 and not (a2.fixed and a2.index == C - 1):
                    due(pe, S["kd_ready"], NS, a2, NS)
                    for b in range(B):
                        for g in range(GR):
                            last = mm(pU[:, (b * GR + g) * P:(b * GR + g + 1) * P], kd[:, b, g, :],
                                      vp[a2.side][:, b, g * GH:(g + 1) * GH, DH:2 * DH], start=True, stop=True)
                    last.then_inc(S["U_done"], 1)
                if A3:
                    due(pe, S["chosen_ready"], B, a3, B)
                    due(pe, S["csum_ready"], 2, a3 + -1, 2)
                    for b in range(B):
                        r = X1[:, (B + b) * E:(B + b + 1) * E]
                        mm(r, later[:, :], chosen[:, b, :], start=True, stop=False)
                        for before in range(b):
                            mm(r, ones[:, :], chosen[:, before, :], start=False, stop=False)
                        last = mm(r, ones[:, :], csum[:, :], start=False, stop=True)
                    last.then_inc(S["prefix_done"], 1)
            run_bodies(pe, body)
            pe.wait_ge(S["csum_ready"], 2 * C)
            pe.wait_ge(S["pos_ready"], C)
            mm(X1[:, 0:E], ones[:, :], csum[:, :], start=True, stop=True).then_inc(s_total, 1)

        def scales(link, dve, first, end):
            V = nc.vector
            dve.wait_ge(s_wall, 1 + int(first > 0))
            at = slice(first, end)
            link(V.tensor_scalar(wmax[:, 0, at], wmax[:, 1, at], 1e-30, None, ALU.max))
            link(V.tensor_scalar(wmax[:, 1, at].bitcast(I32), wmax[:, 0, at].bitcast(I32), 0x7F800000, None,
                                 ALU.bitwise_and))
            link(V.tensor_scalar(w_scale[:, 0, at], wmax[:, 1, at], 4.0, None, ALU.mult))
            link(V.reciprocal(w_scale[:, 1, at], w_scale[:, 0, at]))
            link(V.tensor_tensor(w_scale[:, 2, at], w_scale[:, 0, at], w_scale[:, 0, at], ALU.mult))
            V.tensor_tensor(w_scale[:, 2, at], w_scale[:, 2, at], w_scale[:, 0, at], ALU.mult).then_inc(s_scale, 1)

        def vector_a(dve):
            V = nc.vector
            V.memset(zeros[:, :], 0.0).then_inc(s_vinit, 1)
            V.memset(state[:, :, :, :], 0.0).then_inc(s_vinit, 1)
            V.memset(csum[:, :], 0.0).then_inc(s_vinit, 1)
            for n in range(2):
                V.memset(vp[n][:, :, :, :], 0.0)
                V.memset(gparts[n][:, :, :, :], 0.0)
            dve.wait_ge(s_init, CONSTANTS)
            V.tensor_reduce(part_mask[:, :], tmp8[:, :, :], AX_X, ALU.add).then_inc(s_vinit, 1)
            dve.wait_ge(S["wraw_loaded"], 16 * (5 + 2 * GR))
            V.tensor_scalar(hbg[:, :], hbg[:, :], 0.5, None, ALU.mult).then_inc(s_vinit, 1)
            dve.wait_ge(s_vinit, 5)

            def where(s):
                return s * B // NS, (s % (NS // B)) // (NS // B // GR), s % (GH // SETH)

            chains = {n: sem(f"dve_{n}_chain") for n in ("s1", "so", "s2", "S", "top", "wt", "pos")}

            def stat(i, key, src, st, mv, ready):
                for b in range(B):
                    V.bn_stats(st[:, b, :], src[b]).then_inc(chains[key], 1)
                for b in range(B):
                    due(dve, chains[key], B, i, b + 1)
                    settle(dve)
                    V.bn_aggr(mv[:, b, :], st[:, b, :]).then_inc(S[ready], 1)

            def scan(i, s):
                due(dve, S["gbc_done"], NS, i, s + 1)
                due(dve, S["kd_ready"], NS, i, s - 1)
                V.tensor_tensor_scan(free2(decay[s % 2][:, :, :]), pG[s % 2][:, :], free2(diag4[:, :, :]), 0.0,
                                     ALU.mult, ALU.add).then_inc(S["decay_ready"], 1)

            def weigh(i, s):
                b, g, q = where(s)
                due(dve, S["decay_ready"], NS, i, s + 1)
                due(dve, S["A_done"], NS, i, s + 1)
                due(dve, S["PV_done"], NS, i, s - 1)
                V.tensor_tensor(free2(probs[s % 2][:, :, :]), pA[s % 2][:, :], free2(decay[s % 2][:, :, :]), ALU.mult)\
                 .then_inc(S["probs_ready"], 1)
                if s == 0:
                    due(dve, S["ktok_done"], 1, i, 1)
                    due(dve, S["U_done"], 1, i + -1, 1)
                hs = slice(q * SETH * DH, (q + 1) * SETH * DH)
                V.tensor_tensor(kd[:, b, g, hs].rearrange("p (h d) -> p h d", d=DH),
                                pU[:, (b * GR + g) * P:(b * GR + g + 1) * P][:, hs].rearrange("p (h d) -> p h d", d=DH),
                                decay[s % 2][:, :, P - 1:P].broadcast_to([P, SETH, DH]), ALU.mult)\
                 .then_inc(S["kd_ready"], 1)

            def feature(i, src, ready, e_ready, dst, e):
                due(dve, S[e_ready], 1, i, 1)
                V.scalar_tensor_tensor(free3(dst[i.side][:, :, :, :]), src[:, :], 1.0, e[:, :], ALU.add, ALU.max)\
                 .then_inc(S[ready], 1)

            def body(i):
                a1, a2, a3 = i + 1, i, i + -1
                a0 = i + 2
                A0, A1, A2, A3 = has(a0), has(a1), has(a2), has(a3)
                last_step = a2.fixed and a2.index == C - 1

                def largest_of(*matrices):
                    if not i.fixed:
                        e = bass.ds(i.half - (LOOP[0] + 1 - i.side) // 2, 1)
                    elif LOOP[1] <= i.index < LOOP[1] + HEAD - TURNS:
                        e = slice(i.index - LOOP[1] + TURNS, i.index - LOOP[1] + TURNS + 1)
                    else:
                        return
                    for m in matrices:
                        if i.fixed or m // 2 != i.side:
                            V.tensor_reduce(wpart[:, e, m:m + 1], W[:, e, m, :].unsqueeze(2), AX_X, ALU.max,
                                            apply_absolute_value=True).then_inc(s_wpart, 1)

                if i.fixed and i.index == C - 1:
                    largest_of_parts()
                if A2:
                    scan(a2, 0)
                    weigh(a2, 0)
                    scan(a2, 1)
                    weigh(a2, 1)
                if A3:
                    due(dve, S["o_done"], 1, a3, 1)
                    due(dve, S["rstdo_ready"], 4, a3 + -1, 2)
                    due(dve, S["ln_ready"], B, a3 + -1, B)
                    stat(a3, "so", [X0[:, b * D:(b + 1) * D] for b in range(B)], sto, mvo, "o_stats")
                    if a3.fixed and a3.index == C - 1:
                        dve.wait_ge(s_scale, 1)
                        dve.wait_ge(S["v_done"], C)
                        dve.wait_ge(S["kT_ready"], C)
                        scaled(0)
                        scaled(1)
                        low(0)
                        scaled(2)
                        low(1)
                if A0:
                    due_dma(dve, x_loaded, a0)
                    due(dve, S["rstd1_ready"], 4, a0 + -2, 2)
                    due(dve, S["xn_ready"], B, a0 + -1, B)
                    stat(a0, "s1", [x_in[a0.side][:, b, :] for b in range(B)], st1, mv1[a0.side], "xn_stats")
                if A2:
                    scan(a2, 2)
                    weigh(a2, 2)
                largest_of(0, 2)
                if A3:
                    due(dve, S["x1_ready"], 1, a3, 1)
                    due(dve, S["rstd2_ready"], 4, a3 + -1, 2)
                    due(dve, S["xn2_ready"], B, a3 + -1, B)
                    stat(a3, "s2", [x1[a3.side][:, b, :] for b in range(B)], st2, mv2, "x1_stats")
                    if a3.fixed and a3.index == C - 1:
                        low(2)
                if A1:
                    due(dve, S["qbd_ready"], GR * B, a1 + -2, GR * B)
                    due(dve, S["qg_ready"], 1, a1 + -2, 1)
                    feature(a1, X1, "qT_ready", "eq_ready", qT, ef[0])
                if A2:
                    scan(a2, 3)
                    weigh(a2, 3)
                if A2:
                    scan(a2, 4)
                    weigh(a2, 4)
                if A1:
                    due(dve, S["A_done"], NS, a1 + -2, NS)
                    due(dve, S["ktok_done"], 1, a1 + -2, 1)
                    feature(a1, X0, "kT_ready", "ek_ready", kT, ef[1])
                if A2:
                    scan(a2, 5)
                    weigh(a2, 5)
                if A1:
                    due(dve, S["eg_ready"], GR, a1, GR)
                    due(dve, S["grest_ready"], 1, a1 + -1, 1)
                    due(dve, S["ghi_ready"], 1, a1 + -1, 1)
                    V.tensor_scalar(free3(gT[:, :, :, :]), free3(eg[:, :, :, :]), 0.5, 0.5, ALU.mult, ALU.add)\
                     .then_inc(S["gT_ready"], 1)
                    due(dve, S["gT_ready"], 1, a1, 1)
                    due(dve, S["qg_ready"], 1, a1 + -2, 1)
                    for g in range(GR):
                        for b in range(B):
                            V.tensor_tensor_scan(gam[a1.side][:, g, b, :], gT[:, g, b, :], zeros[:, :], 1.0,
                                                 ALU.mult, ALU.add).then_inc(S["gam_ready"], 1)
                largest_of(1)
                if a2.fixed and a2.index == C - 1:
                    scales(link, dve, 0, HEAD)
                if A2:
                    scan(a2, 6)
                    weigh(a2, 6)
                top = chains["top"]
                if A3:
                    due(dve, S["gate_done"], 1, a3, 1)
                    V.tensor_copy(free2(lg[:, :, :]), X1[:, 0:B * E]).then_inc(top, 1)
                if A2:
                    scan(a2, 7)
                if A3:
                    due(dve, top, 3 + 2 * B, a3, 1)
                    for b in range(B):
                        settle(dve)
                        V.max(mx[:, b, :], lg[:, b, :]).then_inc(top, 1)
                if A3:
                    for b in range(B):
                        due(dve, top, 3 + 2 * B, a3, 2 + b)
                        settle(dve)
                        V.max_index(mi[:, b, :], mx[:, b, :], lg[:, b, :]).then_inc(top, 1)
                    due(dve, S["ew_ready"], 1, a3 + -1, 1)
                    V.tensor_tensor(dv[:, :], mx[:, :, 1], mx[:, :, 0], ALU.subtract).then_inc(S["top_ready"], 1)
                if A2:
                    weigh(a2, 7)
                if A3:
                    due(dve, top, 3 + 2 * B, a3, 1 + 2 * B)
                    V.tensor_copy(mif[:, :, :], mi[:, :, :]).then_inc(top, 1)
                    due(dve, top, 3 + 2 * B, a3, 2 + 2 * B)
                    due(dve, S["pos_ready"], 1, a3 + -1, 1)
                    V.tensor_tensor(oh[:, :, :, :], iota8[:, :].unsqueeze(1).unsqueeze(1).broadcast_to([P, B, TOPK, E]),
                                    mif[:, :, 0:TOPK].unsqueeze(3).broadcast_to([P, B, TOPK, E]), ALU.is_equal)\
                     .then_inc(top, 1)
                    wt = chains["wt"]
                    due(dve, S["ew_ready"], 1, a3, 1)
                    V.tensor_scalar(wtmp[:, 0, :], ew[:, :], 1.0, None, ALU.add).then_inc(wt, 1)
                    due(dve, S["prefix_done"], 1, a3 + -1, 1)
                    due(dve, S["csum_ready"], 2, a3 + -1, 2)
                    for b in range(B):
                        due(dve, top, 3 + 2 * B, a3, 3 + 2 * B)
                        V.tensor_tensor(chosen[:, b, :], oh[:, b, 0, :], oh[:, b, 1, :], ALU.add)\
                         .then_inc(S["chosen_ready"], 1)
                    due(dve, wt, 3, a3, 1)
                    V.reciprocal(wtmp[:, 1, :], wtmp[:, 0, :]).then_inc(wt, 1)
                if A2 and not last_step:
                    due(dve, S["U_done"], 1, a2, 1)
                    due(dve, S["state_ready"], GR * B, a2 + -1, GR * B)
                    V.tensor_tensor(um[:, :, :, :].rearrange("p b g (h d) -> p (b g) h d", d=DH),
                                    pU[:, :].rearrange("p (a h d) -> p a h d", a=B * GR, d=DH),
                                    hmask[:, :].unsqueeze(1).unsqueeze(3).broadcast_to([P, B * GR, GH, DH]), ALU.mult)\
                     .then_inc(S["um_ready"], 1)
                    due(dve, S["um_ready"], 1, a2, 1)
                    due(dve, S["gam_ready"], GR * B, a2, GR * B)
                    for b in range(B):
                        for g in range(GR):
                            V.scalar_tensor_tensor(state[:, b, g, :], state[:, b, g, :],
                                                   gam[a2.side][:, g, b, P - 1:P], um[:, b, g, :],
                                                   ALU.mult, ALU.add).then_inc(S["state_ready"], 1)
                if A3:
                    due(dve, wt, 3, a3, 2)
                    V.tensor_copy(wts_all[:, bass.ds(a3.index, 1), :, 0], wtmp[:, 1, :].unsqueeze(1)).then_inc(wt, 1)
                    V.tensor_tensor(wts_all[:, bass.ds(a3.index, 1), :, 1], wtmp[:, 1, :].unsqueeze(1),
                                    ew[:, :].unsqueeze(1), ALU.mult).then_inc(S["wts_ready"], 1)
                if A3:
                    due(dve, S["prefix_done"], 1, a3, 1)
                    due(dve, S["chosen_ready"], B, a3, B)
                    c = chains["pos"]
                    N = 5
                    V.tensor_tensor(slot[:, :, :], X1[:, B * E:2 * B * E].rearrange("p (b e) -> p b e", e=E),
                                    capoff[:, :].unsqueeze(1).broadcast_to([P, B, E]), ALU.add).then_inc(c, 1)
                    V.tensor_tensor(csum[:, :], csum[:, :], chosen[:, 0, :], ALU.add).then_inc(S["csum_ready"], 1)
                    due(dve, S["csum_ready"], 2, a3, 1)
                    V.tensor_tensor(csum[:, :], csum[:, :], chosen[:, 1, :], ALU.add).then_inc(S["csum_ready"], 1)
                    due(dve, c, N, a3, 1)
                    V.tensor_tensor(oh[:, :, :, :], oh[:, :, :, :],
                                    slot[:, :, :].unsqueeze(2).broadcast_to([P, B, TOPK, E]), ALU.mult).then_inc(c, 1)
                    due(dve, c, N, a3, 2)
                    V.tensor_reduce(posf[:, :], oh[:, :, :, :].rearrange("p b k e -> p (b k) e"), AX_X, ALU.add)\
                     .then_inc(c, 1)
                    due(dve, c, N, a3, 3)
                    due_dma(dve, scattered, a3 + -2, B * TOPK)
                    V.tensor_copy(place_all[:, bass.ds(a3.index, 1), :], posf[:, :].unsqueeze(1)).then_inc(c, 1)
                    V.tensor_copy(choice_all[:, bass.ds(a3.index, 1), :].rearrange("p c (b k) -> p (c b) k", b=B),
                                  mif[:, :, 0:TOPK]).then_inc(c, 1)
                    V.tensor_copy(posi[a3.side][:, :], posf[:, :]).then_inc(S["pos_ready"], 1)
                if i.fixed and i.index == LOOP[0] - 1:
                    dve.wait_ge(s_w[0], 16 * 3 * HEAD)

            n = [0]

            def link(ins):
                n[0] += 1
                ins.then_inc(dve_chain, 1)
                dve.wait_ge(dve_chain, n[0])

            def largest_of_parts():
                dve.wait_ge(s_wpart, 3 * HEAD)
                V.tensor_reduce(wmax[:, 0, 0:HEAD], wpart[:, :, :], AX_X, ALU.max).then_inc(s_wmax, 1)

            def scaled(m):
                if m >= 2:
                    dve.wait_ge(w_low, m - 1)
                V.tensor_scalar(wtmp_b[m % 2], W[:, 0, m, :], w_scale[:, 1, 0:1], None, ALU.mult)\
                 .then_inc(w_scaled, 1)

            def low(m):
                dve.wait_ge(w_high, m + 1)
                V.tensor_tensor(W16[:, 0, m, 1, :], wtmp_b[m % 2], W16[:, 0, m, 0, :], ALU.subtract)\
                 .then_inc(w_low, 1)

            run_bodies(dve, body)

            dve.wait_ge(s_total, 1)
            link(V.tensor_copy(total[:, :], X1[:, 0:E]))
            link(V.tensor_tensor(slot[:, 0, :], total[:, :], capoff[:, :], ALU.add))
            link(V.tensor_scalar(slot[:, 1, :], slot[:, 0, :], rowid[:, :], None, ALU.add))
            V.tensor_copy(pad_row[:, :], slot[:, 1, :]).then_inc(s_pad, 1)

        phase_a.close()

        phase_b = ExitStack()

        def sc(name, shape, dt=F32):
            return phase_b.enter_context(nc.sbuf_tensor(name, shape, dt))

        wtmp_p = sc("wtmp_p", [P, 3, MW])
        xt = [sc(f"xt{n}", [P, D]) for n in range(2)]
        xh = [sc(f"xh{n}", [P, KC, P], F16) for n in range(2)]
        xl = [sc(f"xl{n}", [P, KC, P], F16) for n in range(2)]
        sl = [sc(f"sl{n}", [P, H]) for n in range(2)]
        gg = [sc(f"gg{n}", [P, H]) for n in range(2)]
        gh = [sc(f"gh{n}", [P, HC, P], F16) for n in range(2)]
        gl = [sc(f"gl{n}", [P, HC, P], F16) for n in range(2)]
        yo = [sc(f"yo{n}", [P, D]) for n in range(2)]
        ysh = sc("ysh", [P, ST, D])
        gi = [sc(f"gi{n}", [P, B * TOPK], U32) for n in range(2)]
        ya = [[[sc(f"ya{n}_{b}{k}", [P, D]) for k in range(TOPK)] for b in range(B)] for n in range(2)]
        cmb = [sc(f"cmb{n}", [P, B, D]) for n in range(2)]
        lnc = [sc(f"lnc{n}", [P, B, D]) for n in range(2)]
        x1c = W[:, 1:NE].rearrange("p e m n -> p (e m n)")[:, 0:B * C * D].rearrange(
            "p (b c d) -> p b c d", b=B, c=C)
        stc = [sc(f"stc{n}", [P, B, 6]) for n in range(2)]
        mvc = [sc(f"mvc{n}", [P, B, 2]) for n in range(2)]
        vec = [sc(f"vec{n}", [P, B]) for n in range(2)]
        rsc = [sc(f"rsc{n}", [P, B]) for n in range(2)]
        shiftc = [sc(f"shiftc{n}", [P, B]) for n in range(2)]

        pT, pH1, pH2, pGT, pYB = bank[0], bank[1:3], bank[3:5], bank[5], bank[6:8]
        namesB = ("late_chain pool_split experts_split xtT_done xh_ready xl_ready h1_done h2_done"
                  " silu_ready gg_ready ggT_done gh_ready gl_ready y_done yo_ready").split()
        T = {n: sem("b_" + n) for n in namesB}
        xt_loaded = [sem(f"xt_loaded{n}") for n in range(2)]
        yo_stored = [sem(f"yo_stored{n}") for n in range(2)]
        namesC = "gi_ready mix1 mix2 stat1 stats_ready vare rstd_ready shift_ready lnc_ready oc_ready".split()
        U = {n: sem("c_" + n) for n in namesC}
        x1_loaded = [sem(f"x1_loaded{n}") for n in range(2)]
        ya_loaded = [sem(f"ya_loaded{n}") for n in range(2)]
        out_stored = sem("out_stored")

        assert B == 2 and RT % 2 == 0
        MIX0 = T0 + 5
        mix_body = [max(MIX0 + c, RT + B * c + B - 1 + 3) for c in range(C)]
        step_of_body = {t: c for c, t in enumerate(mix_body)}
        LOOPED = (MIX0 + 4) // 2 * 2
        assert all(step_of_body[t] == t - MIX0 for t in range(MIX0, NT - 2))
        ENDS = mix_body[-1] + 4

        def run_tiles(eng, body):
            def turns(first, end, kind):
                with eng.Fori(first, end) as j:
                    body(Step(j, 0, kind))
                    body(Step(j, 1, kind))

            def peeled(first, end):
                for t in range(first, end):
                    body(Step.of(t))

            peeled(-2, EARLY + 4)
            turns(EARLY // 2 + 2, T0 // 2 - 1, "routed")
            peeled(T0 - 2, LOOPED)
            turns(LOOPED // 2, NT // 2 - 1, "mixed")
            peeled(NT - 2, ENDS)

        def is_tile(t):
            return not t.fixed or 0 <= t.index < NT

        def is_routed(t):
            return EARLY <= t.index < T0 if t.fixed else t.kind == "routed"

        def place(t):
            early = t.fixed and t.index < EARLY
            return t.side, t.half if early else t.half - RT // 2

        def step_at(t):
            if not t.fixed:
                return t + -MIX0 if t.kind == "mixed" else None
            return Step.of(step_of_body[t.index]) if t.index in step_of_body else None

        def entry(eng, row, t, most):
            return eng.value_load(tab[0:1, row, bass.ds(t.index - EARLY, 1)], min_val=0, max_val=most)

        def expert_of(eng, t):
            if not is_routed(t):
                return bass.ds(0, 1)
            if t.fixed and t.index == EARLY:
                eng.wait_ge(s_tab, 1)
            return bass.ds(entry(eng, 0, t, E), 1)

        def sync_b(sp):
            for n in range(2):
                sp.wait_ge(xs_stored[n], 16 * C // 2)

            def body(t):
                if is_tile(t + 2):
                    u = t + 2
                    if is_routed(u):
                        if u.fixed and u.index == EARLY:
                            for n in range(2):
                                sp.wait_ge(scattered[n], 16 * B * TOPK * C // 2)
                            sp.wait_ge(s_padded, 16 * E)
                            sp.wait_ge(s_tab, 1)
                        e, row = entry(sp, 0, u, E), entry(sp, 1, u, SHARED - P)
                        sp.wait_ge(T["experts_split"], e)
                        settle(sp)
                    else:
                        b, c = place(u)
                        row = c * P + (SHARED + b * SEQ)
                    due(sp, T["xtT_done"], 1, t, 1)
                    sp.dma_start(xt[t.side][:, :], xs_d[bass.ds(row, P), :]).then_inc(xt_loaded[t.side], 16)
                u = t + -2
                if is_tile(u) and is_routed(u):
                    due(sp, T["yo_ready"], 1, u, 1)
                    sp.dma_start(ys_d[bass.ds((u.index - EARLY) * P, P), :], yo[u.side][:, :])\
                      .then_inc(yo_stored[u.side], 16)
                c, ended = step_at(t + -1), step_at(t + -3)
                if c and c.fixed and c.index == 0:
                    sp.wait_ge(T["yo_ready"], T0)
                    for n in range(2):
                        sp.wait_ge(x1_stored[n], 16 * C // 2)
                if c:
                    due(sp, U["oc_ready"], 1, c + -2, 1)
                    sp.dma_start(x1c[:, :, bass.ds(c.index, 1), :].rearrange("p b c d -> p (b c) d"),
                                 x1_by_step[c.index]).then_inc(x1_loaded[c.side], 16)
                if ended:
                    due(sp, U["oc_ready"], 1, ended, 1)
                    sp.dma_start(out.rearrange("b (c p) d -> c p b d", p=P)[ended.index],
                                 x1c[:, :, bass.ds(ended.index, 1), :].rearrange("p b c d -> p (b c) d"))\
                      .then_inc(out_stored, 16)
            run_tiles(sp, body)
            sp.wait_ge(out_stored, 16 * C)

        def tensor_b(pe):
            mm = nc.tensor.matmul
            pe.wait_ge(w_low, 3)

            def turn_x(t):
                due_dma(pe, xt_loaded, t)
                for k in range(KC):
                    last = nc.tensor.transpose(pT[:, k * P:(k + 1) * P], xt[t.side][:, k * P:(k + 1) * P], ident[:, :])
                last.then_inc(T["xtT_done"], 1)

            def turn_g(t):
                due(pe, T["gg_ready"], 1, t, 1)
                for c in range(HC):
                    last = nc.tensor.transpose(pGT[:, c * P:(c + 1) * P], gg[t.side][:, c * P:(c + 1) * P], ident[:, :])
                last.then_inc(T["ggT_done"], 1)

            def hidden(t, e, m, dst, done, between=None):
                n = 0
                for k in range(KC):
                    if k == 1 and between is not None:
                        between()
                    for a, s in ((xh, 0), (xh, 1), (xl, 0)):
                        last = mm(dst[t.side][:, :], a[t.side][:, k, :],
                                  W16[:, e, m, s, k * H:(k + 1) * H], start=(n == 0), stop=(n == 3 * KC - 1))
                        n += 1
                last.then_inc(T[done], 1)

            def project(t, e):
                due(pe, T["gl_ready"], 1, t, 1)
                n = 0
                for c in range(HC):
                    for a, s in ((gh, 0), (gh, 1), (gl, 0)):
                        last = mm(pYB[t.side][:, 0:D], a[t.side][:, c, :],
                                  W16[:, e, 2, s, c * D:(c + 1) * D], start=(n == 0), stop=(n == 3 * HC - 1))
                        n += 1
                last.then_inc(T["y_done"], 1)

            def transposes(t):
                due(pe, T["yo_ready"], 1, t + -4, 1)
                if is_tile(t + -1):
                    turn_g(t + -1)
                if is_tile(t + 1):
                    turn_x(t + 1)

            def body(t):
                if t.fixed and t.index > NT + 1:
                    return
                if is_tile(t):
                    e = expert_of(pe, t)
                if is_tile(t + -2):
                    e_before = expert_of(pe, t + -2)
                if is_tile(t):
                    due(pe, T["xl_ready"], 1, t, 1)
                    hidden(t, e, 0, pH1, "h1_done", between=lambda: transposes(t))
                else:
                    transposes(t)
                if is_tile(t):
                    hidden(t, e, 1, pH2, "h2_done")
                if is_tile(t + -2):
                    project(t + -2, e_before)
            run_tiles(pe, body)

        def scalar_b(act):
            def body(t):
                if is_tile(t + -1):
                    u = t + -1
                    due(act, T["ggT_done"], 1, u, 1)
                    due(act, T["y_done"], 1, u + -2, 1)
                    act.activation(gh[u.side][:, :, :].rearrange("p c t -> p (c t)"), pGT[:, :], ACT.Copy)\
                       .then_inc(T["gh_ready"], 1)
                if is_tile(t + 1):
                    u = t + 1
                    due(act, T["xtT_done"], 1, u, 1)
                    due(act, T["h2_done"], 1, u + -2, 1)
                    act.activation(xh[u.side][:, :, :].rearrange("p k t -> p (k t)"), pT[:, 0:D], ACT.Copy)\
                       .then_inc(T["xh_ready"], 1)
                if is_tile(t):
                    e = expert_of(act, t)
                    due(act, T["h1_done"], 1, t, 1)
                    due(act, T["gg_ready"], 1, t + -2, 1)
                    act.activation(sl[t.side][:, :], pH1[t.side][:, :], ACT.Silu, scale=w_scale[:, 0, e])\
                       .then_inc(T["silu_ready"], 1)
                if is_tile(t + -2):
                    u = t + -2
                    e = expert_of(act, u)
                    due(act, T["y_done"], 1, u, 1)
                    if is_routed(u):
                        due_dma(act, yo_stored, u + -(EARLY + 2))
                        dst = yo[u.side][:, :]
                    else:
                        b, c = place(u)
                        dst = ysh[:, bass.ds(c + b * C, 1), :].rearrange("p a d -> p (a d)")
                    act.activation(dst, pYB[u.side][:, 0:D], ACT.Copy, scale=w_scale[:, 2, e])\
                       .then_inc(T["yo_ready"], 1)
                c = step_at(t + -1)
                if c:
                    due(act, U["shift_ready"], 1, c, 1)
                    due(act, U["oc_ready"], 1, c + -2, 1)
                    for b in range(B):
                        act.activation(lnc[c.side][:, b, :], cmb[c.side][:, b, :], ACT.Identity,
                                       bias=shiftc[c.side][:, b:b + 1], scale=rsc[c.side][:, b:b + 1])\
                           .then_inc(U["lnc_ready"], 1)
            act.wait_ge(s_scale, 1)
            run_tiles(act, body)

        def vector_b(dve):
            V = nc.vector
            n = [0]

            def link(ins):
                n[0] += 1
                ins.then_inc(T["late_chain"], 1)
                dve.wait_ge(T["late_chain"], n[0])

            def tiles_of_experts():
                link(V.tensor_scalar(te[:, 0, :], total[:, :], (P - 1) / 2.0, 1.0 / P, ALU.add, ALU.mult))
                link(V.tensor_copy(te_i[:, :], te[:, 0, :]))
                link(V.tensor_copy(te[:, 1, :], te_i[:, :]))
                link(V.memset(te[:, 2, :], 0.0))
                link(V.tensor_tensor_scan(te[:, 3, :], te[:, 1, :], te[:, 2, :], 0.0, ALU.add, ALU.add))
                link(V.tensor_tensor(te[:, 0, :], te[:, 3, :], te[:, 1, :], ALU.subtract))
                link(V.scalar_tensor_tensor(te[:, 4, :], te[:, 0, :], float(P), capoff[:, :], ALU.mult, ALU.subtract))

            def expert_of_tiles():
                end, tiles = te[0:1, 3, :], te[0:1, 1, :]
                link(V.tensor_tensor(tg[:, 0], tile_f[:, :].unsqueeze(2).broadcast_to([1, RT, E]),
                                     end.unsqueeze(1).broadcast_to([1, RT, E]), ALU.is_ge))
                link(V.tensor_reduce(tb[:, 0, :], tg[:, 0], AX_X, ALU.add))
                link(V.tensor_tensor(tg[:, 1], tg[:, 0], tiles.unsqueeze(1).broadcast_to([1, RT, E]), ALU.mult))
                link(V.tensor_reduce(tb[:, 1, :], tg[:, 1], AX_X, ALU.add))

            def rows_of_tiles():
                link(V.tensor_tensor(tb[:, 2, :], tile_f[:, :], tb[:, 1, :], ALU.subtract))
                link(V.tensor_scalar(tb[:, 3, :], tb[:, 0, :], float(CAP), None, ALU.mult))
                link(V.scalar_tensor_tensor(tb[:, 4, :], tb[:, 2, :], float(P), tb[:, 3, :], ALU.mult, ALU.add))
                link(V.tensor_scalar(tb[:, 5, :], tb[:, 0, :], float(E), None, ALU.is_lt))
                link(V.tensor_tensor(tb[:, 6, :], tb[:, 4, :], tb[:, 5, :], ALU.mult))
                link(V.tensor_scalar(tb[:, 0, :], tb[:, 0, :], float(E - 1), 1.0, ALU.min, ALU.add))
                link(V.tensor_copy(tab[:, 0, :], tb[:, 0, :]))
                V.tensor_copy(tab[:, 1, :], tb[:, 6, :]).then_inc(s_tab, 1)

            def rows_of_choices():
                n_all = C * B * TOPK
                link(V.tensor_tensor(found[:, :, :], choice_all[:, :, :].rearrange("p c n -> p (c n)").unsqueeze(2)
                                     .broadcast_to([P, n_all, E]),
                                     iota8[:, :].unsqueeze(1).broadcast_to([P, n_all, E]), ALU.is_equal))
                link(V.tensor_tensor(found[:, :, :], found[:, :, :],
                                     te[:, 4, :].unsqueeze(1).broadcast_to([P, n_all, E]), ALU.mult))
                link(V.tensor_reduce(choice_all[:, :, :].rearrange("p c n -> p (c n)"), found[:, :, :], AX_X, ALU.add))
                link(V.tensor_tensor(place_all[:, :, :], place_all[:, :, :], choice_all[:, :, :], ALU.add))
                V.tensor_copy(pos_all[:, :, :], place_all[:, :, :]).then_inc(s_place, 1)

            def largest_of(e):
                if e == HEAD:
                    dve.wait_ge(s_w[1], 16 * 3 * (NE - HEAD))
                V.tensor_reduce(wmax[:, 0, e:e + 1], W[:, e].rearrange("p m n -> p (m n)").unsqueeze(1), AX_X, ALU.max,
                                apply_absolute_value=True).then_inc(s_wmax, 1)

            beside = [tiles_of_experts, expert_of_tiles, rows_of_tiles, rows_of_choices]
            beside += [lambda e=e: largest_of(e) for e in range(HEAD, NE)]
            beside += [lambda: scales(link, dve, HEAD, NE)]
            assert len(beside) <= EARLY - 2

            def mix(c, t):
                due_dma(dve, ya_loaded, c, B * TOPK)
                due(dve, T["yo_ready"], 1, t + -3, 1)
                due(dve, U["lnc_ready"], B, c + -2, B)
                for b in range(B):
                    V.scalar_tensor_tensor(cmb[c.side][:, b, :], ya[c.side][b][0][:, :],
                                           wts_all[:, bass.ds(c.index, 1), b, 0],
                                           ysh[:, bass.ds(c.index + b * C, 1), :].rearrange("p c d -> p (c d)"),
                                           ALU.mult, ALU.add).then_inc(U["mix1"], 1)
                for b in range(B):
                    due(dve, U["mix1"], B, c, b + 1)
                    V.scalar_tensor_tensor(cmb[c.side][:, b, :], ya[c.side][b][1][:, :],
                                           wts_all[:, bass.ds(c.index, 1), b, 1],
                                           cmb[c.side][:, b, :], ALU.mult, ALU.add).then_inc(U["mix2"], 1)
                for b in range(B):
                    due(dve, U["mix2"], B, c, b + 1)
                    V.bn_stats(stc[c.side][:, b, :], cmb[c.side][:, b, :]).then_inc(U["stat1"], 1)
                for b in range(B):
                    due(dve, U["stat1"], B, c, b + 1)
                    if b == 0:
                        due(dve, U["shift_ready"], 1, c + -2, 1)
                    settle(dve)
                    V.bn_aggr(mvc[c.side][:, b, :], stc[c.side][:, b, :]).then_inc(U["stats_ready"], 1)
                due(dve, U["stats_ready"], B, c, B)
                due(dve, U["rstd_ready"], 1, c + -2, 1)
                V.tensor_scalar(vec[c.side][:, :], mvc[c.side][:, :, 1], EPS, None, ALU.add).then_inc(U["vare"], 1)

            def shift(c):
                due(dve, U["rstd_ready"], 1, c, 1)
                due(dve, U["lnc_ready"], B, c + -2, B)
                V.scalar_tensor_tensor(shiftc[c.side][:, :], mvc[c.side][:, :, 0], -1.0, rsc[c.side][:, :],
                                       ALU.mult, ALU.mult).then_inc(U["shift_ready"], 1)

            def residual(c):
                due(dve, U["lnc_ready"], B, c, B)
                due_dma(dve, x1_loaded, c)
                x_ = x1c[:, :, bass.ds(c.index, 1), :].rearrange("p b c d -> p (b c) d")
                V.tensor_tensor(x_, lnc[c.side][:, :, :], x_, ALU.add).then_inc(U["oc_ready"], 1)

            def body(t):
                if is_tile(t + -1):
                    u = t + -1
                    due(dve, T["gh_ready"], 1, u, 1)
                    due(dve, T["y_done"], 1, u + -2, 1)
                    V.tensor_tensor(gl[u.side][:, :, :].rearrange("p c t -> p (c t)"), pGT[:, :],
                                    gh[u.side][:, :, :].rearrange("p c t -> p (c t)"), ALU.subtract)\
                     .then_inc(T["gl_ready"], 1)
                if is_tile(t + 1):
                    u = t + 1
                    due(dve, T["xh_ready"], 1, u, 1)
                    due(dve, T["h2_done"], 1, u + -2, 1)
                    V.tensor_tensor(xl[u.side][:, :, :].rearrange("p k t -> p (k t)"), pT[:, 0:D],
                                    xh[u.side][:, :, :].rearrange("p k t -> p (k t)"), ALU.subtract)\
                     .then_inc(T["xl_ready"], 1)
                if step_at(t + -1):
                    shift(step_at(t + -1))
                if is_tile(t):
                    e = expert_of(dve, t)
                    due(dve, T["silu_ready"], 1, t, 1)
                    due(dve, T["h2_done"], 1, t, 1)
                    due(dve, T["ggT_done"], 1, t + -2, 1)
                    V.scalar_tensor_tensor(gg[t.side][:, :], sl[t.side][:, :], w_scale[:, 1, e], pH2[t.side][:, :],
                                           ALU.mult, ALU.mult).then_inc(T["gg_ready"], 1)
                if step_at(t):
                    mix(step_at(t), t)
                if step_at(t + -2):
                    residual(step_at(t + -2))
                if t.fixed and 0 <= t.index < len(beside):
                    beside[t.index]()
            run_tiles(dve, body)

        def pool_b(pool):
            def split(e):
                whole = W[:, e].rearrange("p m n -> p (m n)")
                if e > 1:
                    pool.wait_ge(T["experts_split"], e - 1)
                pool.tensor_tensor(wtmp_p[:, :, :].rearrange("p m n -> p (m n)"), whole,
                                   w_scale[:, 1, e:e + 1].broadcast_to([P, 3 * MW]), ALU.mult).then_inc(T["pool_split"], 1)
                pool.wait_ge(T["pool_split"], 2 * e - 1)
                settle(pool)
                pool.tensor_copy(W16[:, e, :, 0, :], wtmp_p[:, :, :]).then_inc(T["pool_split"], 1)
                pool.wait_ge(T["pool_split"], 2 * e)
                pool.tensor_tensor(W16[:, e, :, 1, :], wtmp_p[:, :, :], W16[:, e, :, 0, :], ALU.subtract)\
                    .then_inc(T["experts_split"], 1)

            pool.wait_ge(s_scale, 1)
            split(1)
            pool.wait_ge(s_wmax, 1 + NE - HEAD)
            pool.partition_all_reduce(wmax[:, 1, HEAD:NE], wmax[:, 0, HEAD:NE], P, RMAX).then_inc(s_wall, 1)
            for e in range(2, HEAD):
                split(e)
            pool.wait_ge(s_scale, 2)
            for e in range(HEAD, NE):
                split(e)

        def pool_c(pool):
            for n in range(2):
                pool.wait_ge(yo_stored[n], 16 * RT // 2)
            pool.wait_ge(s_place, 1)

            def gather(c):
                due_dma(pool, ya_loaded, c + -2, B * TOPK)
                due(pool, U["mix2"], B, c + -2, B)
                settle(pool)
                pool.tensor_copy(gi[c.side][:, :].unsqueeze(1), pos_all[:, bass.ds(c.index, 1), :])\
                    .then_inc(U["gi_ready"], 1)
                due(pool, U["gi_ready"], 1, c, 1)
                for b in range(B):
                    for k in range(TOPK):
                        settle(pool)
                        pool.indirect_dma_start(ya[c.side][b][k][:, :], None, ys_d[:, :], bass.IndirectOffsetOnAxis(
                            ap=gi[c.side][:, b * TOPK + k:b * TOPK + k + 1], axis=0)).then_inc(ya_loaded[c.side], 16)

            def rstd(c):
                due(pool, U["vare"], 1, c, 1)
                due(pool, U["lnc_ready"], B, c + -2, B)
                pool.tensor_tensor(rsc[c.side][:, :], vec[c.side][:, :], half_neg[:, 0:B], ALU.pow)\
                    .then_inc(U["rstd_ready"], 1)

            def body(c):
                rstd(c)
                if not c.fixed or c.index + 2 < C:
                    gather(c + 2)

            for c in range(2):
                gather(Step.of(c))
            for c in range(2):
                body(Step.of(c))
            with pool.Fori(1, C // 2 - 1) as j:
                body(Step(j, 0))
                body(Step(j, 1))
            for c in range(C - 2, C):
                body(Step.of(c))

        phase_b.close()

        with nc.Block() as block:
            @block.sync
            def _(sp):
                sync_a(sp)
                sync_b(sp)

            @block.scalar
            def _(act):
                scalar_a(act)
                scalar_b(act)

            @block.gpsimd
            def _(pool):
                pool_a(pool)
                pool_b(pool)
                pool_c(pool)

            @block.vector
            def _(dve):
                vector_a(dve)
                vector_b(dve)

            @block.tensor
            def _(pe):
                tensor_a(pe)
                tensor_b(pe)


_INS = ['L0_attn_x', 'L0_attn_Wq', 'L0_attn_Wk', 'L0_attn_Wv', 'L0_attn_Wo', 'L0_attn_Wg', 'L0_attn_bg',
        'L0_ffn_gate_w', 'L0_ffn_ew1', 'L0_ffn_ew2', 'L0_ffn_ew3', 'L0_ffn_sw1', 'L0_ffn_sw2', 'L0_ffn_sw3']
_OUTS = [((2, 2048, 256), 'float32')]


def kernel(**inputs):
    import numpy as _np
    import concourse.bacc as _bacc
    from concourse import mybir as _mybir
    from concourse.bass_utils import run_bass_kernel_spmd as _run

    nc = _bacc.Bacc("TRN2", target_bir_lowering=False, num_devices=1)
    arrays, args = {}, []
    for name in _INS:
        a = _np.ascontiguousarray(inputs[name])
        arrays[f"in_{name}_dram"] = a
        args.append(nc.dram_tensor(f"in_{name}_dram", a.shape, _mybir.dt.from_np(a.dtype), kind="ExternalInput").ap())
    for i, (shape, dtype) in enumerate(_OUTS):
        dt = _mybir.dt.from_np(_np.dtype(dtype))
        args.append(nc.dram_tensor(f"out_{i}_dram", shape, dt, kind="ExternalOutput").ap())
    sandwich_kernel(nc, *args)
    r = _run(nc, [arrays], core_ids=[0])
    return r.results[0]["out_0_dram"]
```
